# Optimizing a Trainium2 kernel written in Bass

```python
import numpy as np
import jax
import jax.numpy as jnp

def _softmax(x, axis=-1):
    return jax.nn.softmax(x, axis=axis)

def _gelu(x):
    return jax.nn.gelu(x, approximate=True)

def _silu(x):
    return jax.nn.silu(x)

def _sigmoid(x):
    return jax.nn.sigmoid(x)

def _layernorm(x, axis=-1, eps=1e-05):
    m = jnp.mean(x, axis=axis, keepdims=True)
    v = jnp.var(x, axis=axis, keepdims=True)
    return (x - m) / jnp.sqrt(v + eps)

def _scatter_add(tgt, idx, src, axis=0):
    return tgt.at[idx].add(src)

def _segment_sum(src, seg, n):
    return jax.ops.segment_sum(src, seg, n)
kernel_name = 'mk_recurrent_d2_jaxref_r8_8e7c6c'

def setup_inputs(seed: int=0):
    np.random.seed(seed)
    _w = jnp.asarray

    def _L0_attn_setup():
        import jax, jax.numpy as jnp
        import numpy as np
        import math
        B, S, D_IN, D_KQ, D_OUT = (4, 256, 128, 128, 128)
        key = jax.random.key(seed)
        ks = jax.random.split(key, 7)
        sc = 0.02
        return {'x': jax.random.normal(ks[0], (B, S, D_IN), jnp.float32), 'Wq': jax.random.normal(ks[1], (D_KQ, D_IN), jnp.float32) * sc, 'bq': jax.random.normal(ks[2], (D_KQ,), jnp.float32) * sc, 'Wk': jax.random.normal(ks[3], (D_KQ, D_IN), jnp.float32) * sc, 'bk': jax.random.normal(ks[4], (D_KQ,), jnp.float32) * sc, 'Wv': jax.random.normal(ks[5], (D_OUT, D_IN), jnp.float32) * sc, 'bv': jax.random.normal(ks[6], (D_OUT,), jnp.float32) * sc}
    _L0_attn_in = _L0_attn_setup()

    def _L0_ffn_setup():
        import jax, jax.numpy as jnp
        import numpy as np
        D = 128
        H = 4
        DF = 512
        E = 8
        EPS = 1e-05

        def _layer_norm(x, g, b):
            mu = jnp.mean(x, axis=-1, keepdims=True)
            var = jnp.mean(jnp.square(x - mu), axis=-1, keepdims=True)
            return (x - mu) * jax.lax.rsqrt(var + EPS) * g + b

        def _mha(x, Wqkv, bqkv, Wo, bo):
            S, B, _ = x.shape
            hd = D // H
            qkv = x @ Wqkv.T + bqkv
            q, k, v = jnp.split(qkv, 3, axis=-1)
            to_heads = lambda t: t.reshape(S, B, H, hd).transpose(1, 2, 0, 3)
            q, k, v = (to_heads(q), to_heads(k), to_heads(v))
            scores = jnp.einsum('bhqd,bhkd->bhqk', q, k) * (1.0 / np.sqrt(hd))
            att = jax.nn.softmax(scores, axis=-1)
            o = jnp.einsum('bhqk,bhkd->bhqd', att, v)
            o = o.transpose(2, 0, 1, 3).reshape(S, B, D)
            return o @ Wo.T + bo

        def _moe(x, Wg, W1, b1, W2, b2):
            S, B, _ = x.shape
            xf = x.reshape(S * B, D)
            logits = xf @ Wg.T
            idx = jnp.argmax(logits, axis=-1)
            out = jnp.zeros_like(xf)
            for e in range(E):
                m = (idx == e)[:, None].astype(xf.dtype)
                h = jax.nn.relu(xf @ W1[e] + b1[e])
                out = out + m * (h @ W2[e] + b2[e])
            return out.reshape(S, B, D)
        key = jax.random.key(seed)
        ks = jax.random.split(key, 16)
        S, B = (64, 8)
        s = lambda k, shape, fan: jax.random.normal(k, shape, jnp.float32) * (1.0 / np.sqrt(fan))
        return {'x': jax.random.normal(ks[0], (S, B, D), jnp.float32), 'Wqkv': s(ks[1], (3 * D, D), D), 'bqkv': jnp.zeros((3 * D,), jnp.float32), 'Wo': s(ks[2], (D, D), D), 'bo': jnp.zeros((D,), jnp.float32), 'g1': jnp.ones((D,), jnp.float32), 'be1': jnp.zeros((D,), jnp.float32), 'g2': jnp.ones((D,), jnp.float32), 'be2': jnp.zeros((D,), jnp.float32), 'Wg': s(ks[3], (E, D), D), 'W1': s(ks[4], (E, D, DF), D), 'b1': jnp.zeros((E, DF), jnp.float32), 'W2': s(ks[5], (E, DF, D), DF), 'b2': jnp.zeros((E, D), jnp.float32)}
    _L0_ffn_in = _L0_ffn_setup()

    def _L1_attn_setup():
        import jax, jax.numpy as jnp
        import numpy as np
        DIM = 128
        H = 16
        D = DIM // H
        CS = 64
        SCALE = D ** (-0.5)
        key = jax.random.key(seed)
        k1, k2, k3 = jax.random.split(key, 3)
        B, N = (4, 512)
        x = jax.random.normal(k1, (B, N, DIM), dtype=jnp.float32)
        W_qkv = jax.random.normal(k2, (DIM, 3 * DIM), dtype=jnp.float32) * DIM ** (-0.5)
        W_out = jax.random.normal(k3, (DIM, DIM), dtype=jnp.float32) * DIM ** (-0.5)
        return {'x': x, 'W_qkv': W_qkv, 'W_out': W_out}
    _L1_attn_in = _L1_attn_setup()

    def _L1_ffn_setup():
        import jax, jax.numpy as jnp
        import numpy as np
        D_MODEL = 128
        NUM_HEADS = 4
        NUM_EXPERTS = 8
        TOP_K = 2
        D_FF = 128
        EPS = 1e-06

        def _rmsnorm(x, g):
            return x * jax.lax.rsqrt(jnp.mean(x * x, axis=-1, keepdims=True) + EPS) * g

        def _swiglu(x, w1, w2, w3):
            return jax.nn.silu(x @ w1.T) * (x @ w3.T) @ w2.T
        key = jax.random.key(seed)
        ks = jax.random.split(key, 16)
        d, e, f = (D_MODEL, NUM_EXPERTS, D_FF)
        dc = d // 4
        s = 0.02
        return {'X': jax.random.normal(ks[0], (2, 128, d), dtype=jnp.float32), 'g1': jnp.ones((d,), jnp.float32), 'g2': jnp.ones((d,), jnp.float32), 'Wq': jax.random.normal(ks[1], (d, d), jnp.float32) * s, 'Wkc': jax.random.normal(ks[2], (dc, d), jnp.float32) * s, 'Wvc': jax.random.normal(ks[3], (dc, d), jnp.float32) * s, 'Wo': jax.random.normal(ks[4], (d, d), jnp.float32) * s, 'Wr': jax.random.normal(ks[5], (e, d), jnp.float32) * s, 'expert_bias': jnp.zeros((e,), jnp.float32), 'sW1': jax.random.normal(ks[6], (f, d), jnp.float32) * s, 'sW2': jax.random.normal(ks[7], (d, f), jnp.float32) * s, 'sW3': jax.random.normal(ks[8], (f, d), jnp.float32) * s, 'eW1': jax.random.normal(ks[9], (e, f, d), jnp.float32) * s, 'eW2': jax.random.normal(ks[10], (e, d, f), jnp.float32) * s, 'eW3': jax.random.normal(ks[11], (e, f, d), jnp.float32) * s}
    _L1_ffn_in = _L1_ffn_setup()
    _d = {'L0_attn_x': _L0_attn_in['x'], 'L0_attn_Wq': _L0_attn_in['Wq'], 'L0_attn_bq': _L0_attn_in['bq'], 'L0_attn_Wk': _L0_attn_in['Wk'], 'L0_attn_bk': _L0_attn_in['bk'], 'L0_attn_Wv': _L0_attn_in['Wv'], 'L0_attn_bv': _L0_attn_in['bv'], 'L0_ffn_Wqkv': _L0_ffn_in['Wqkv'], 'L0_ffn_bqkv': _L0_ffn_in['bqkv'], 'L0_ffn_Wo': _L0_ffn_in['Wo'], 'L0_ffn_bo': _L0_ffn_in['bo'], 'L0_ffn_g1': _L0_ffn_in['g1'], 'L0_ffn_be1': _L0_ffn_in['be1'], 'L0_ffn_g2': _L0_ffn_in['g2'], 'L0_ffn_be2': _L0_ffn_in['be2'], 'L0_ffn_Wg': _L0_ffn_in['Wg'], 'L0_ffn_W1': _L0_ffn_in['W1'], 'L0_ffn_b1': _L0_ffn_in['b1'], 'L0_ffn_W2': _L0_ffn_in['W2'], 'L0_ffn_b2': _L0_ffn_in['b2'], 'L1_attn_W_qkv': _L1_attn_in['W_qkv'], 'L1_attn_W_out': _L1_attn_in['W_out'], 'L1_ffn_g1': _L1_ffn_in['g1'], 'L1_ffn_g2': _L1_ffn_in['g2'], 'L1_ffn_Wq': _L1_ffn_in['Wq'], 'L1_ffn_Wkc': _L1_ffn_in['Wkc'], 'L1_ffn_Wvc': _L1_ffn_in['Wvc'], 'L1_ffn_Wo': _L1_ffn_in['Wo'], 'L1_ffn_Wr': _L1_ffn_in['Wr'], 'L1_ffn_expert_bias': _L1_ffn_in['expert_bias'], 'L1_ffn_sW1': _L1_ffn_in['sW1'], 'L1_ffn_sW2': _L1_ffn_in['sW2'], 'L1_ffn_sW3': _L1_ffn_in['sW3'], 'L1_ffn_eW1': _L1_ffn_in['eW1'], 'L1_ffn_eW2': _L1_ffn_in['eW2'], 'L1_ffn_eW3': _L1_ffn_in['eW3']}
    _x0 = _d['L0_attn_x']
    _d['L0_attn_x'] = jax.random.normal(jax.random.fold_in(jax.random.key(seed), 1), (1, 2048, 128), dtype=_x0.dtype)
    del _x0
    return _d

def reference(L0_attn_x, L0_attn_Wq, L0_attn_bq, L0_attn_Wk, L0_attn_bk, L0_attn_Wv, L0_attn_bv, L0_ffn_Wqkv, L0_ffn_bqkv, L0_ffn_Wo, L0_ffn_bo, L0_ffn_g1, L0_ffn_be1, L0_ffn_g2, L0_ffn_be2, L0_ffn_Wg, L0_ffn_W1, L0_ffn_b1, L0_ffn_W2, L0_ffn_b2, L1_attn_W_qkv, L1_attn_W_out, L1_ffn_g1, L1_ffn_g2, L1_ffn_Wq, L1_ffn_Wkc, L1_ffn_Wvc, L1_ffn_Wo, L1_ffn_Wr, L1_ffn_expert_bias, L1_ffn_sW1, L1_ffn_sW2, L1_ffn_sW3, L1_ffn_eW1, L1_ffn_eW2, L1_ffn_eW3):

    def _L0_attn_ref(x, Wq, bq, Wk, bk, Wv, bv):
        import jax, jax.numpy as jnp
        import numpy as np
        import math
        B, S, D_IN, D_KQ, D_OUT = (4, 256, 128, 128, 128)
        Q = jnp.einsum('bsd,kd->bsk', x, Wq) + bq
        K = jnp.einsum('bsd,kd->bsk', x, Wk) + bk
        V = jnp.einsum('bsd,od->bso', x, Wv) + bv
        scale = 1.0 / math.sqrt(D_KQ)
        attn = jnp.einsum('bqk,bsk->bqs', Q, K) * scale
        s = attn.shape[-1]
        causal = jnp.tril(jnp.ones((s, s), dtype=bool))
        attn = jnp.where(causal[None, :, :], attn, -jnp.inf)
        attn = jax.nn.softmax(attn, axis=-1)
        Z = jnp.einsum('bqs,bso->bqo', attn, V)
        return Z

    def _L0_ffn_ref(x, Wqkv, bqkv, Wo, bo, g1, be1, g2, be2, Wg, W1, b1, W2, b2):
        import jax, jax.numpy as jnp
        import numpy as np
        D = 128
        H = 4
        DF = 512
        E = 8
        EPS = 1e-05

        def _layer_norm(x, g, b):
            mu = jnp.mean(x, axis=-1, keepdims=True)
            var = jnp.mean(jnp.square(x - mu), axis=-1, keepdims=True)
            return (x - mu) * jax.lax.rsqrt(var + EPS) * g + b

        def _mha(x, Wqkv, bqkv, Wo, bo):
            S, B, _ = x.shape
            hd = D // H
            qkv = x @ Wqkv.T + bqkv
            q, k, v = jnp.split(qkv, 3, axis=-1)
            to_heads = lambda t: t.reshape(S, B, H, hd).transpose(1, 2, 0, 3)
            q, k, v = (to_heads(q), to_heads(k), to_heads(v))
            scores = jnp.einsum('bhqd,bhkd->bhqk', q, k) * (1.0 / np.sqrt(hd))
            att = jax.nn.softmax(scores, axis=-1)
            o = jnp.einsum('bhqk,bhkd->bhqd', att, v)
            o = o.transpose(2, 0, 1, 3).reshape(S, B, D)
            return o @ Wo.T + bo

        def _moe(x, Wg, W1, b1, W2, b2):
            S, B, _ = x.shape
            xf = x.reshape(S * B, D)
            logits = xf @ Wg.T
            idx = jnp.argmax(logits, axis=-1)
            out = jnp.zeros_like(xf)
            for e in range(E):
                m = (idx == e)[:, None].astype(xf.dtype)
                h = jax.nn.relu(xf @ W1[e] + b1[e])
                out = out + m * (h @ W2[e] + b2[e])
            return out.reshape(S, B, D)
        y = _layer_norm(x + _mha(x, Wqkv, bqkv, Wo, bo), g1, be1)
        z = _layer_norm(y + _moe(y, Wg, W1, b1, W2, b2), g2, be2)
        return z

    def _L1_attn_ref(x, W_qkv, W_out):
        import jax, jax.numpy as jnp
        import numpy as np
        DIM = 128
        H = 16
        D = DIM // H
        CS = 64
        SCALE = D ** (-0.5)
        B, N, C = x.shape
        qkv = (x @ W_qkv).reshape(B, N, 3, H, D)
        qkv = jnp.transpose(qkv, (2, 0, 3, 1, 4))
        q, k, v = (qkv[0], qkv[1], qkv[2])
        nc = N // CS
        q = q.reshape(B, H, nc, CS, D)
        k = k.reshape(B, H, nc, CS, D)
        v = v.reshape(B, H, nc, CS, D)
        attn = jnp.einsum('bhcqd,bhckd->bhcqk', q, k) * SCALE
        mask = jnp.triu(jnp.ones((CS, CS), dtype=bool), k=1)
        attn = jnp.where(mask, jnp.float32(-65000.0), attn)
        attn = jax.nn.softmax(attn, axis=-1)
        out_local = jnp.einsum('bhcqk,bhckd->bhcqd', attn, v)
        chunk_k = k.mean(axis=3)
        chunk_v = v.mean(axis=3)
        cum_k = jnp.cumsum(chunk_k, axis=2)
        cum_v = jnp.cumsum(chunk_v, axis=2)
        zeros = jnp.zeros((B, H, 1, D), dtype=x.dtype)
        cum_k = jnp.concatenate([zeros, cum_k[:, :, :-1]], axis=2)
        cum_v = jnp.concatenate([zeros, cum_v[:, :, :-1]], axis=2)
        cross = jax.nn.sigmoid(jnp.einsum('bhcsd,bhcd->bhcs', q, cum_k) * SCALE)
        out = out_local + cross[..., None] * cum_v[:, :, :, None, :] * 0.5
        out = out.reshape(B, H, N, D)
        out = jnp.transpose(out, (0, 2, 1, 3)).reshape(B, N, C)
        return out @ W_out

    def _L1_ffn_ref(X, g1, g2, Wq, Wkc, Wvc, Wo, Wr, expert_bias, sW1, sW2, sW3, eW1, eW2, eW3):
        import jax, jax.numpy as jnp
        import numpy as np
        D_MODEL = 128
        NUM_HEADS = 4
        NUM_EXPERTS = 8
        TOP_K = 2
        D_FF = 128
        EPS = 1e-06

        def _rmsnorm(x, g):
            return x * jax.lax.rsqrt(jnp.mean(x * x, axis=-1, keepdims=True) + EPS) * g

        def _swiglu(x, w1, w2, w3):
            return jax.nn.silu(x @ w1.T) * (x @ w3.T) @ w2.T
        B, S, d = X.shape
        H = NUM_HEADS
        dk = d // H
        scale = 1.0 / jnp.sqrt(jnp.float32(dk))
        nx = _rmsnorm(X, g1)
        Q = (nx @ Wq.T).reshape(B, S, H, dk).transpose(0, 2, 1, 3)
        Kc = nx @ Wkc.T
        Vc = nx @ Wvc.T
        scores = jnp.einsum('bhsd,btd->bhst', Q, Kc) * scale
        attn = jax.nn.softmax(scores, axis=-1)
        out = jnp.einsum('bhst,btd->bhsd', attn, Vc)
        out = out.transpose(0, 2, 1, 3).reshape(B, S, d) @ Wo.T
        X = X + out
        nx = _rmsnorm(X, g2)
        xf = nx.reshape(-1, d)
        logits = xf @ Wr.T + expert_bias
        rw = jax.nn.softmax(logits, axis=-1)
        topw, topi = jax.lax.top_k(rw, TOP_K)
        topw = jax.nn.softmax(topw, axis=-1)
        combine = jnp.sum(jax.nn.one_hot(topi, NUM_EXPERTS, dtype=xf.dtype) * topw[..., None], axis=1)
        shared = _swiglu(xf, sW1, sW2, sW3)
        h = jax.nn.silu(jnp.einsum('td,efd->etf', xf, eW1)) * jnp.einsum('td,efd->etf', xf, eW3)
        eo = jnp.einsum('etf,edf->etd', h, eW2)
        specialist = jnp.einsum('te,etd->td', combine, eo)
        moe_out = (shared + specialist).reshape(B, S, d)
        return X + moe_out
    x = L0_attn_x
    xn = _layernorm(x, axis=-1)
    s = _L0_attn_ref(xn, L0_attn_Wq, L0_attn_bq, L0_attn_Wk, L0_attn_bk, L0_attn_Wv, L0_attn_bv)
    g = _silu(_L0_ffn_ref(xn, L0_ffn_Wqkv, L0_ffn_bqkv, L0_ffn_Wo, L0_ffn_bo, L0_ffn_g1, L0_ffn_be1, L0_ffn_g2, L0_ffn_be2, L0_ffn_Wg, L0_ffn_W1, L0_ffn_b1, L0_ffn_W2, L0_ffn_b2))
    x = x + s * g
    xn = _layernorm(x, axis=-1)
    s = _L1_attn_ref(xn, L1_attn_W_qkv, L1_attn_W_out)
    g = _silu(_L1_ffn_ref(xn, L1_ffn_g1, L1_ffn_g2, L1_ffn_Wq, L1_ffn_Wkc, L1_ffn_Wvc, L1_ffn_Wo, L1_ffn_Wr, L1_ffn_expert_bias, L1_ffn_sW1, L1_ffn_sW2, L1_ffn_sW3, L1_ffn_eW1, L1_ffn_eW2, L1_ffn_eW3))
    x = x + s * g
    return x

_drawn_inputs = setup_inputs


def setup_inputs(seed=0):
    import zlib

    import numpy as np

    out = dict(_drawn_inputs(seed))
    spreads = {'L0_ffn_bqkv': (0.0, 0.8),
     'L0_ffn_bo': (0.0, 0.8),
     'L0_ffn_g1': (1.0, 0.6),
     'L0_ffn_be1': (0.0, 0.8),
     'L0_ffn_g2': (1.0, 0.6),
     'L0_ffn_be2': (0.0, 0.8),
     'L0_ffn_b1': (0.0, 0.8),
     'L0_ffn_b2': (0.0, 0.8),
     'L1_ffn_g1': (1.0, 0.6),
     'L1_ffn_g2': (1.0, 0.6),
     'L1_ffn_expert_bias': (0.0, 0.8)}
    factors = {'L0_attn_Wq': 8.0,
     'L0_attn_bq': 8.0,
     'L0_attn_Wk': 8.0,
     'L0_attn_bk': 8.0,
     'L0_attn_Wv': 4.208,
     'L0_ffn_Wqkv': 4.15,
     'L0_ffn_Wo': 4.12,
     'L0_ffn_Wg': 5.835,
     'L0_ffn_W1': 6.476,
     'L0_ffn_W2': 5.119,
     'L1_ffn_Wq': 8.0,
     'L1_ffn_Wkc': 8.0,
     'L1_ffn_Wvc': 8.0,
     'L1_ffn_Wo': 8.0,
     'L1_ffn_Wr': 8.0,
     'L1_ffn_sW1': 8.0,
     'L1_ffn_sW2': 8.0,
     'L1_ffn_sW3': 8.0,
     'L1_ffn_eW1': 8.0,
     'L1_ffn_eW2': 8.0,
     'L1_ffn_eW3': 8.0}
    for name, (base, spread) in spreads.items():
        noise = np.random.default_rng([zlib.crc32(name.encode()), seed]).standard_normal(out[name].shape)
        drawn = base * np.exp(spread * noise) if base else spread * noise
        out[name] = jnp.asarray(drawn.astype(out[name].dtype))
    for name, factor in factors.items():
        out[name] = (out[name] * factor).astype(out[name].dtype)
    return out
```

```python
from contextlib import ExitStack

import concourse.bass as bass
from concourse import mybir

P = 128
T = 2048
NT = T // P
D = 128
F32 = mybir.dt.float32
BF16 = mybir.dt.bfloat16
I32 = mybir.dt.int32
U32 = mybir.dt.uint32
ALU = mybir.AluOpType
ACT = mybir.ActivationFunctionType
AX = mybir.AxisListType

E0 = 8
F0 = 512
FC0 = F0 // P
GROUP = 4
WINDOWS = -(-(NT + E0 - 1) // GROUP) * GROUP
GROUPS = WINDOWS // GROUP
NEG = -1.0e30

CS = 64
NC = T // CS
H1 = 16
D1 = D // H1
HG = 4
SC1 = float(D1) ** -0.5
MASKED = -65000.0
REGION = 29 * 1024
HM = 4
DM = D // HM
SCM = float(DM) ** -0.5
PARTS = 3
KA_ROWS = PARTS * DM
KB_ROWS = PARTS * DM + PARTS
UNITS = NT // 2
E1 = 8
ES = E1 + 1
CH = 512
NCH = T // CH


class Region:

    def __init__(self, tensor, size):
        self.tensor, self.size, self.at = tensor, size, 0

    def reset(self, at=0):
        self.at = at

    def take(self, *shape, dt=F32):
        n = 1
        for d in shape:
            n *= d
        words = n if dt != BF16 else n // 2
        assert self.at + words <= self.size, (self.at, words, self.size)
        a = self.tensor[:, self.at:self.at + words]
        self.at += words
        if dt == BF16:
            a = a.bitcast(BF16)
        names = "abcd"[:len(shape)]
        if len(shape) == 1:
            return a
        return a.rearrange(f"p ({' '.join(names)}) -> p {' '.join(names)}", **dict(zip(names, shape)))


class Link:

    def __init__(self, engine, sem):
        self.engine, self.sem, self.n = engine, sem, 0

    def mark(self, ins):
        self.n += 1
        ins.then_inc(self.sem, 1)

    def wait(self):
        self.engine.wait_ge(self.sem, self.n)

    def __call__(self, ins):
        self.mark(ins)
        self.wait()


def cuts(sizes):
    at, found = 0, []
    for n in sizes:
        found.append((at, at + n))
        at += n
    return found


def bass_recurrent_two_layers(nc, A, out):
    with ExitStack() as ctx:
        def sb(name, shape, dt=F32):
            return ctx.enter_context(nc.sbuf_tensor(name, shape, dt))

        def sem(name):
            return ctx.enter_context(nc.semaphore(name))

        ps = ctx.enter_context(nc.psum_tensor("ps", [P, 8, 512], F32))

        slots_in = nc.dram_tensor("slots_in", [WINDOWS * P, D], F32, kind="Internal").ap()
        slots_out = nc.dram_tensor("slots_out", [WINDOWS * P, D], F32, kind="Internal").ap()

        region = Region(sb("region", [P, REGION]), REGION)
        x = sb("x", [P, NT, D])
        xn = sb("xn", [P, NT, D])
        xnT = sb("xnT", [P, T])
        qT = region.take(T)
        kT = region.take(T)
        v = region.take(NT, D)
        vfT = region.take(T)
        y = sb("y", [P, NT, D])
        tmp = region.take(NT, D)
        s0 = sb("s0", [P, NT, D])
        w0 = sb("w0", [P, 5 * D])
        cols0 = sb("cols0", [P, 3])
        rows0 = sb("rows0", [P, 6 * D])
        bv_row, bo_row, g1_row, be1_row, g2_row, be2_row = (rows0[:, n * D:(n + 1) * D] for n in range(6))
        wgT = sb("wgT", [P, E0])
        w1 = region.take(E0, F0)
        w2 = region.take(E0, FC0, D)
        b1_row = region.take(E0, F0)
        b2_row = region.take(E0, D)
        ident = sb("ident", [P, P])
        ones = sb("ones", [P, P])
        before = sb("before", [P, P])
        causal = sb("causal", [P, P])
        zeros = sb("zeros", [P, D])
        stats = sb("stats", [P, NT, 6])
        mv = sb("mv", [P, NT, 2])
        vare = sb("vare", [P, NT])
        mhalf = sb("mhalf", [P, NT])
        rstd = sb("rstd", [P, NT])
        lg = sb("lg", [P, NT, E0])
        top = sb("top", [P, NT, 8])
        topi = sb("topi", [P, NT, 8], U32)
        expert = sb("expert", [P, NT])
        iota_e = sb("iota_e", [P, E0, NT])
        onehot = sb("onehot", [P, E0, NT])
        rank = sb("rank", [P, E0, NT])
        upto = sb("upto", [P, E0, NT])
        scanmask = sb("scanmask", [P, E0, NT])
        cnt_i = sb("cnt_i", [P, E0], I32)
        cnt_f = sb("cnt_f", [P, E0])
        pad = sb("pad", [P, E0])
        end = sb("end", [P, E0])
        base = sb("base", [P, E0])
        slot_f = sb("slot_f", [P, NT])
        slot = sb("slot", [P, NT], U32)
        wstart = sb("wstart", [P, WINDOWS, E0])
        wcmp = sb("wcmp", [P, WINDOWS, E0])
        wexp_f = sb("wexp_f", [P, WINDOWS])
        wexp = sb("wexp", [P, WINDOWS], I32)
        xg = region.take(GROUP, D)
        overlay = region.at
        prob = region.take(2, T)
        probT = region.take(2, 512)
        rmax = sb("rmax", [P, NT])
        nmax = sb("nmax", [P, NT])
        rsum = sb("rsum", [P, NT])
        rinv = sb("rinv", [P, NT])
        region.reset(overlay)
        xgT = region.take(GROUP, P)
        hb = region.take(GROUP, F0)
        hT = region.take(GROUP, F0)
        og = sb("og", [P, GROUP, D])
        moe = vfT[:, :].rearrange("p (t d) -> p t d", t=NT)
        yT = qT

        wl1 = sb("wl1", [P, 3 * D + D + (D + 2 * DM) + D + E1])
        wq1, wk1, wv1, wout1, wmq, wmo, wr = (wl1[:, a:b] for a, b in cuts([D, D, D, D, D + 2 * DM, D, E1]))
        e13 = sb("e13", [P, ES, 2 * D])
        e2 = sb("e2", [P, ES, D])
        rows1 = sb("rows1", [P, 2 * D + E1])
        rg1_row, rg2_row, eb_row = (rows1[:, a:b] for a, b in cuts([D, D, E1]))
        identb = sb("identb", [P, P], BF16)
        msq = sb("msq", [P, NT])
        region.reset()
        k4 = region.take(NC, HG, CS + 1)
        vbd = region.take(NT, 2, H1 // 2, 2 * D1 + 2)
        vsum = region.take(NT, D)
        q1T = region.take(T)
        k1T = region.take(T)
        sm = region.take(H1, CS)
        pe1 = region.take(H1, CS)
        p1T = region.take(H1 // 2, P)
        amask = region.take(CS)
        mask4 = region.take(HG)
        vmask = region.take(D)
        xsum = region.take(NC)
        xcum = region.take(NC)
        xrep = region.take(2, 2, P)
        qtile = region.take(P)
        ktile = region.take(2, HG, CS + 1)
        vtile = region.take(2, H1 // 2, 2 * D1 + 2)
        crs = region.take(H1)
        sig = region.take(H1)
        mx1 = region.take(H1)
        rs1 = region.take(H1)
        cvx = region.take(D)
        o1 = region.take(NT, D)
        region.reset()
        om = region.take(NT, D)
        qkv = region.take(NT, D + 2 * DM)
        rest = region.take(NT, D)
        qa = region.take(NT, HM, KA_ROWS, dt=BF16)
        ka = region.take(NT, KA_ROWS, dt=BF16)
        qb = region.take(NT, HM, P, dt=BF16)
        kb = region.take(NT, P, dt=BF16)
        restk = region.take(NT, DM)
        qaT = region.take(NT, HM * P, dt=BF16)
        kaT = region.take(T, dt=BF16)
        qbT = region.take(2, HM * P, dt=BF16)
        kbT = region.take(T, dt=BF16)
        v1 = region.take(NT, DM + 1)
        pm = region.take(2, 2, HM * P)
        mxp = region.take(HM, 2)
        negm = region.take(HM)
        mr = region.take(HM)
        rsm = region.take(HM)
        region.reset(NT * D)
        lg1 = region.take(NT, E1)
        rw = region.take(NT, E1)
        top1 = region.take(NT, 8)
        topi1 = region.take(NT, 8).bitcast(U32)
        mrow = region.take(NT)
        w12 = region.take(2, NT)
        ix12 = region.take(2, NT)
        iota1 = region.take(NT, E1)
        comb = region.take(NT, ES)
        ctmp = region.take(NT, E1)
        sg = region.take(2, CH)
        h1T = region.take(2, CH)
        acc = y

        s_x = sem("s_x"); s_w0 = sem("s_w0"); s_rows0 = sem("s_rows0"); s_wexp = sem("s_wexp")
        s_const = sem("s_const"); s_zero = sem("s_zero"); s_zeroed = sem("s_zeroed")
        dve_step = sem("dve_step"); pool_step = sem("pool_step"); act_step = sem("act_step")
        var_ready = sem("var_ready"); rstd_ready = sem("rstd_ready")
        xn_ready = sem("xn_ready")
        d_filled = sem("d_filled"); d_drained = sem("d_drained")
        a_filled = sem("a_filled"); a_drained = sem("a_drained")
        y_ready = sem("y_ready"); onehot_ready = sem("onehot_ready")
        slot_ready = sem("slot_ready"); scattered = sem("scattered"); wexp_ready = sem("wexp_ready")
        score_done = sem("score_done"); nmax_ready = sem("nmax_ready"); prob_ready = sem("prob_ready")
        xg_loaded = sem("xg_loaded"); xg_turned = sem("xg_turned"); xgT_ready = sem("xgT_ready")
        h_done = sem("h_done"); hb_ready = sem("hb_ready"); h_turned = sem("h_turned"); hT_ready = sem("hT_ready")
        o_done = sem("o_done"); og_ready = sem("og_ready"); og_stored = sem("og_stored")
        gathered = sem("gathered"); s_out = sem("s_out"); fin_ready = sem("fin_ready")

        s_w1 = sem("s_w1")
        z_ready = sem("z_ready"); g_ready = sem("g_ready"); x1_ready = sem("x1_ready")
        xsum_ready = sem("xsum_ready"); prep_ready = sem("prep_ready"); mask_ready = sem("mask_ready")
        xrep_ready = sem("xrep_ready"); xrep_used = sem("xrep_used")
        qtile_ready = sem("qtile_ready"); s_done = sem("s_done"); s_read = sem("s_read")
        vtile_ready = sem("vtile_ready"); sm_ready = sem("sm_ready"); p_ready = sem("p_ready"); p_turned = sem("p_turned"); pT_ready = sem("pT_ready")
        sigexp_ready = sem("sigexp_ready"); crs_ready = sem("crs_ready"); pv_done = sem("pv_done"); pv_read = sem("pv_read")
        loop_step = sem("loop_step"); o1_ready = sem("o1_ready")
        nx_ready = sem("nx_ready"); parts_ready = sem("parts_ready"); copies_ready = sem("copies_ready")
        cut_ready = sem("cut_ready")
        mx_filled = sem("mx_filled"); mx_read = sem("mx_read"); m_ready = sem("m_ready"); qb_turned = sem("qb_turned")
        qbT_ready = sem("qbT_ready"); st_filled = sem("st_filled"); pm_ready = sem("pm_ready"); pm_used = sem("pm_used")
        om_filled = sem("om_filled"); om_read = sem("om_read"); m_step = sem("m_step")
        rx_ready = sem("rx_ready"); rexp_ready = sem("rexp_ready"); comb_ready = sem("comb_ready")
        h13_filled = sem("h13_filled"); sg_ready = sem("sg_ready"); h1T_ready = sem("h1T_ready"); e_filled = sem("e_filled")
        e_read = sem("e_read"); acc_ready = sem("acc_ready"); g1_ready = sem("g1_ready")

        def bank(n):
            return ps[:, n, :]

        def bankb(n):
            return ps[:, n, :].bitcast(BF16)

        D_FILLS = dict(zip(
            ("xnT", "v", "mha", "yT", "logits", "ranks", "pv", "xn1T", "kcum", "q1", "k1", "vdup", "vsum",
             "o1T", "s1", "nxT", "qkv", "kaT", "kbT", "qaT", "omT", "mo", "nx2T", "lg1"),
            (a for a, _ in cuts([4, 4, 4, 4, 1, 1, NT, 4, 1, 4, 4, 8, 4, 4, 4, 4, 8, 2, 2, 8, 4, 4, 4, 1]))))
        A_FILLS = dict(proj=0, turn=12)

        rows = lambda r, n: r.unsqueeze(1).broadcast_to([P, n, D])

        block = ctx.enter_context(nc.Block())

        @block.sync
        def _(sp):
            sp.dma_start(x[:, :, :], A["x"].rearrange("(t p) d -> p t d", p=P)).then_inc(s_x, 16)
            sp.dma_start(w0[:, :], A["w0"]).then_inc(s_w0, 16)
            sp.dma_start(cols0[:, :], A["cols0"]).then_inc(s_w0, 16)
            sp.dma_start(wgT[:, :], A["wgT"]).then_inc(s_w0, 16)
            sp.dma_start(rows0[:, :], A["rows0"].partition_broadcast(P)).then_inc(s_rows0, 16)
            sp.wait_ge(s_zero, 1)
            sp.dma_start(slots_in.rearrange("(w p) d -> p w d", p=P),
                         zeros[:, :].unsqueeze(1).broadcast_to([P, WINDOWS, D])).then_inc(s_zeroed, 16)
            sp.dma_start(w1[:, :, :], A["w1"]).then_inc(s_wexp, 16)
            sp.dma_start(b1_row[:, :, :], A["b1"].partition_broadcast(P)).then_inc(s_wexp, 16)
            sp.dma_start(w2[:, :, :, :], A["w2"]).then_inc(s_wexp, 16)
            sp.dma_start(b2_row[:, :, :], A["b2"].partition_broadcast(P)).then_inc(s_wexp, 16)
            sp.dma_start(wl1[:, :], A["wl1"]).then_inc(s_w1, 16)
            sp.dma_start(rows1[:, :], A["rows1"].partition_broadcast(P)).then_inc(s_w1, 16)
            sp.dma_start(e13[:, :, :], A["e13"]).then_inc(s_w1, 16)
            sp.dma_start(e2[:, :, :], A["e2"]).then_inc(s_w1, 16)
            sp.wait_ge(scattered, 16 * NT)
            rin = slots_in.rearrange("(w p) d -> p w d", p=P)
            rout = slots_out.rearrange("(w p) d -> p w d", p=P)
            sp.dma_start(xg[:, :, :], rin[:, 0:GROUP, :]).then_inc(xg_loaded, 16)
            with sp.Fori(1, GROUPS) as i:
                sp.wait_ge(xg_turned, i)
                sp.dma_start(xg[:, :, :], rin[:, bass.ds(i * GROUP, GROUP), :]).then_inc(xg_loaded, 16)
                sp.wait_ge(og_ready, i * GROUP)
                sp.dma_start(rout[:, bass.ds((i - 1) * GROUP, GROUP), :], og[:, :, :]).then_inc(og_stored, 16)
            sp.wait_ge(og_ready, GROUPS * GROUP)
            sp.dma_start(rout[:, (GROUPS - 1) * GROUP:GROUPS * GROUP, :], og[:, :, :]).then_inc(og_stored, 16)
            sp.wait_ge(og_stored, 16 * GROUPS)
            sp.wait_ge(fin_ready, 1)
            sp.dma_start(out.rearrange("(t p) d -> p t d", p=P), y[:, :, :]).then_inc(s_out, 16)
            sp.wait_ge(s_out, 16)

        @block.gpsimd
        def _(pool):
            link = Link(pool, pool_step)
            pool.memset(zeros[:, :], 0.0).then_inc(s_zero, 1)
            link.mark(pool.memset(ident[:, :], 0.0))
            link.mark(pool.memset(before[:, :], 1.0))
            link.mark(pool.memset(causal[:, :], 0.0))
            link.mark(pool.memset(scanmask[:, :, :], 1.0))
            link(pool.memset(mhalf[:, :], -0.5))
            link.mark(pool.affine_select(out=ident[:, :], in_=ident[:, :], compare_op=ALU.not_equal, fill=1.0,
                                         base=0, pattern=[[-1, P]], channel_multiplier=1))
            link.mark(pool.affine_select(out=before[:, :], in_=before[:, :], compare_op=ALU.is_gt, fill=0.0,
                                         base=0, pattern=[[1, P]], channel_multiplier=-1))
            link.mark(pool.affine_select(out=causal[:, :], in_=causal[:, :], compare_op=ALU.is_ge, fill=NEG,
                                         base=0, pattern=[[-1, P]], channel_multiplier=1))
            link.mark(pool.memset(scanmask[:, :, 0:1], 0.0))
            link.mark(pool.iota(iota_e[:, :, :], pattern=[[1, E0], [0, NT]], base=0, channel_multiplier=0,
                                allow_small_or_imprecise_dtypes=True))
            link.mark(pool.iota(wstart[:, :, :], pattern=[[P, WINDOWS], [0, E0]], base=0, channel_multiplier=0,
                                allow_small_or_imprecise_dtypes=True))
            link(pool.memset(ones[:, :], 1.0))
            link(pool.tensor_copy(identb[:, :], ident[:, :]))
            pool.sem_inc(s_const, 1)

            def inverse_deviation(n, eps):
                pool.wait_ge(var_ready, NT * (n + 1))
                link(pool.tensor_scalar(vare[:, :], mv[:, :, 1], eps, None, ALU.add))
                pool.tensor_tensor(rstd[:, :], vare[:, :], mhalf[:, :], ALU.pow).then_inc(rstd_ready, 1)

            def inverse_root(n, eps):
                pool.wait_ge(var_ready, NT * (n + 1))
                link(pool.tensor_tensor(msq[:, :], mv[:, :, 0], mv[:, :, 0], ALU.mult))
                link(pool.tensor_tensor(msq[:, :], msq[:, :], mv[:, :, 1], ALU.add))
                link(pool.tensor_scalar(vare[:, :], msq[:, :], eps, None, ALU.add))
                pool.tensor_tensor(rstd[:, :], vare[:, :], mhalf[:, :], ALU.pow).then_inc(rstd_ready, 1)

            inverse_deviation(0, 1e-5)
            inverse_deviation(1, 1e-5)
            pool.wait_ge(slot_ready, 1)
            pool.wait_ge(y_ready, NT)
            pool.wait_ge(s_zeroed, 16)
            for t in range(NT):
                pool.indirect_dma_start(out=slots_in[:, :], out_offset=bass.IndirectOffsetOnAxis(ap=slot[:, t:t + 1], axis=0),
                                        in_=y[:, t, :], in_offset=None).then_inc(scattered, 16)
            pool.wait_ge(og_stored, 16 * GROUPS)
            for t in range(NT):
                pool.indirect_dma_start(out=moe[:, t, :], out_offset=None, in_=slots_out[:, :],
                                        in_offset=bass.IndirectOffsetOnAxis(ap=slot[:, t:t + 1], axis=0)).then_inc(gathered, 16)
            inverse_deviation(2, 1e-5)

            pool.wait_ge(x1_ready, 1)
            link(pool.memset(amask[:, :], 0.0))
            link(pool.memset(mask4[:, :], 1.0))
            link(pool.memset(vmask[:, :], 1.0))
            link(pool.memset(vbd[:, :, :, :, :], 0.0))
            for c in range(2):
                v_ = amask[CS * c:CS * (c + 1), :]
                link(pool.affine_select(out=v_, in_=v_, compare_op=ALU.is_ge, fill=MASKED / SC1,
                                             base=0, pattern=[[-1, CS]], channel_multiplier=1))
            for g in range(D // 32):
                m_ = mask4[32 * g:32 * (g + 1), :]
                link(pool.affine_select(out=m_, in_=m_, compare_op=ALU.is_ge, fill=0.0,
                                        base=0, pattern=[[-D1, HG]], channel_multiplier=1))
                link(pool.affine_select(out=m_, in_=m_, compare_op=ALU.is_ge, fill=0.0,
                                             base=D1 - 1, pattern=[[D1, HG]], channel_multiplier=-1))
            for h in range(2):
                hv = vmask[CS * h:CS * (h + 1), :].rearrange("p (n two d) -> p n two d", two=2, d=D1)
                link(pool.memset(hv[:, :, 1 - h, :], 0.0))
                hb_ = vbd[CS * h:CS * (h + 1), :, :, :, 2 * D1 + h]
                link(pool.memset(hb_, 1.0))
            pool.sem_inc(mask_ready, 1)

            inverse_deviation(3, 1e-5)
            pool.wait_ge(prep_ready, 1)

            def tiles(i):
                if not isinstance(i, int):
                    pool.wait_ge(s_done, i)
                pool.tensor_copy(qtile[:, :], q1T[:, bass.ds(i * P, P)]).then_inc(qtile_ready, 1)
                pool.tensor_copy(ktile[:, :, :, :], k4[:, bass.ds(i * 2, 2), :, :]).then_inc(qtile_ready, 1)
                if not isinstance(i, int):
                    pool.wait_ge(pv_done, i)
                pool.tensor_copy(vtile[:, :, :, :].rearrange("p a b c -> p (a b c)"),
                                 vbd[:, bass.ds(i, 1), :, :, :].rearrange("p o a b c -> p (o a b c)")).then_inc(vtile_ready, 1)

            tiles(0)
            with pool.Fori(1, NT) as i:
                tiles(i)

            inverse_root(4, 1e-6)
            pool.wait_ge(cut_ready, 1)
            link.mark(pool.memset(kb[:, :, PARTS * DM:KB_ROWS], 1.0))
            link(pool.memset(v1[:, :, DM:DM + 1], 1.0))
            pool.sem_inc(copies_ready, 1)
            inverse_root(5, 1e-6)

        @block.vector
        def _(dve):
            link = Link(dve, dve_step)

            def normalise(n, src, dst, ready=None):
                for t in range(NT):
                    link.mark(dve.bn_stats(stats[:, t, :], src[:, t, :]))
                link.wait()
                for t in range(NT):
                    dve.bn_aggr(mv[:, t, :], stats[:, t, :]).then_inc(var_ready, 1)
                dve.wait_ge(var_ready, NT * (n + 1))
                dve.wait_ge(rstd_ready, n + 1)
                for t in range(NT):
                    ins = dve.tensor_scalar(dst[:, t, :], src[:, t, :], mv[:, t, 0:1], rstd[:, t:t + 1],
                                            ALU.subtract, ALU.mult)
                    if ready is None:
                        link.mark(ins)
                    else:
                        ins.then_inc(ready, 1)
                link.wait()

            def drain(k, dst, **kw):
                dve.wait_ge(d_filled, k + 1)
                dve.tensor_copy(dst, bank(k % 2)[:, 0:dst.free_size()] if len(dst.shape) == 2 else bank(k % 2)).then_inc(d_drained, 1)

            dve.wait_ge(s_x, 16)
            normalise(0, x, xn, xn_ready)
            for g in range(4):
                drain(D_FILLS["xnT"] + g, xnT[:, 512 * g:512 * (g + 1)])
            dve.wait_ge(s_rows0, 16)
            for g in range(4):
                k = D_FILLS["v"] + g
                dve.wait_ge(d_filled, k + 1)
                dve.tensor_tensor(v[:, 4 * g:4 * g + 4, :], bank(k % 2).rearrange("p (t d) -> p t d", t=4),
                                  rows(bv_row, 4), ALU.add).then_inc(d_drained, 1)
            link(dve.tensor_tensor(tmp[:, :, :], xn[:, :, :], rows(bo_row, NT), ALU.add))
            for g in range(4):
                k = D_FILLS["mha"] + g
                dve.wait_ge(d_filled, k + 1)
                dve.tensor_tensor(tmp[:, 4 * g:4 * g + 4, :], bank(k % 2).rearrange("p (t d) -> p t d", t=4),
                                  tmp[:, 4 * g:4 * g + 4, :], ALU.add).then_inc(d_drained, 1)
            dve.wait_ge(d_drained, D_FILLS["mha"] + 4)
            normalise(1, tmp, y)
            link(dve.tensor_tensor(y[:, :, :], y[:, :, :], rows(g1_row, NT), ALU.mult))
            dve.tensor_tensor(y[:, :, :], y[:, :, :], rows(be1_row, NT), ALU.add).then_inc(y_ready, NT)
            for g in range(4):
                drain(D_FILLS["yT"] + g, yT[:, 512 * g:512 * (g + 1)])
            k = D_FILLS["logits"]
            dve.wait_ge(d_filled, k + 1)
            dve.tensor_copy(lg[:, :, :], bank(k % 2)[:, 0:NT * E0].rearrange("p (t e) -> p t e", t=NT)).then_inc(d_drained, 1)
            dve.wait_ge(d_drained, k + 1)
            for t in range(NT):
                link.mark(dve.max(top[:, t, :], lg[:, t, :]))
            link.wait()
            for t in range(NT):
                link.mark(dve.max_index(topi[:, t, :], top[:, t, :], lg[:, t, :]))
            link.wait()
            link(dve.tensor_copy(expert[:, :], topi[:, :, 0]))
            dve.wait_ge(s_const, 1)
            dve.tensor_tensor(onehot[:, :, :], iota_e[:, :, :], expert[:, :].unsqueeze(1).broadcast_to([P, E0, NT]),
                              ALU.is_equal).then_inc(onehot_ready, 1)
            k = D_FILLS["ranks"]
            dve.wait_ge(d_filled, k + 1)
            in_tile = bank(k % 2)[:, 0:NT * E0].rearrange("p (e t) -> p e t", e=E0)
            of_tile = bank(k % 2)[:, NT * E0:2 * NT * E0].rearrange("p (e t) -> p e t", e=E0)
            fl = lambda a: a[:, :, :].rearrange("p e t -> p (e t)")
            link(dve.tensor_tensor_scan(fl(upto), fl(scanmask), bank(k % 2)[:, NT * E0:2 * NT * E0], 0.0, ALU.mult, ALU.add))
            link(dve.tensor_tensor(rank[:, :, :], upto[:, :, :], of_tile, ALU.subtract))
            link(dve.tensor_tensor(rank[:, :, :], rank[:, :, :], in_tile, ALU.add))
            dve.sem_inc(d_drained, 1)
            link(dve.tensor_scalar(cnt_i[:, :], upto[:, :, NT - 1], float(P - 1), None, ALU.add))
            sh = P.bit_length() - 1
            link(dve.tensor_scalar(cnt_i[:, :], cnt_i[:, :], sh, sh, ALU.logical_shift_right, ALU.logical_shift_left))
            link(dve.tensor_copy(pad[:, :], cnt_i[:, :]))
            link(dve.tensor_tensor_scan(end[:, :], ones[:, 0:E0], pad[:, :], 0.0, ALU.mult, ALU.add))
            link(dve.tensor_tensor(base[:, :], end[:, :], pad[:, :], ALU.subtract))
            link(dve.tensor_tensor(rank[:, :, :], rank[:, :, :], base[:, :].unsqueeze(2).broadcast_to([P, E0, NT]), ALU.add))
            link(dve.tensor_tensor(rank[:, :, :], rank[:, :, :], onehot[:, :, :], ALU.mult))
            link(dve.tensor_reduce(slot_f[:, :], rank[:, :, :].rearrange("p e t -> p t e"), AX.X, ALU.add))
            dve.tensor_copy(slot[:, :], slot_f[:, :]).then_inc(slot_ready, 1)
            link(dve.tensor_tensor(wcmp[:, :, :], end[:, :].unsqueeze(1).broadcast_to([P, WINDOWS, E0]), wstart[:, :, :], ALU.is_le))
            link(dve.tensor_reduce(wexp_f[:, :], wcmp[:, :, :], AX.X, ALU.add))
            dve.tensor_scalar(wexp[:, :], wexp_f[:, :], float(E0 - 1), None, ALU.min).then_inc(wexp_ready, 1)

            def row_max(i):
                dve.wait_ge(score_done, i + 1)
                diag = ps[:, 4 + i // 4, P * (i % 4):P * (i % 4 + 1)]
                link(dve.tensor_tensor(diag, diag, causal[:, :], ALU.add))
                n = (i + 1) * P
                s = ps[:, 4:8, :].rearrange("p b c -> p (b c)")[:, 0:n]
                link(dve.tensor_reduce(rmax[:, i:i + 1], s, AX.X, ALU.max))
                dve.tensor_scalar(nmax[:, i:i + 1], rmax[:, i:i + 1], -float(D) ** -0.5, None, ALU.mult).then_inc(nmax_ready, 1)

            def attention_out(i):
                k = D_FILLS["pv"] + i
                dve.wait_ge(prob_ready, i + 1)
                link(dve.reciprocal(rinv[:, i:i + 1], rsum[:, i:i + 1]))
                dve.wait_ge(d_filled, k + 1)
                dve.tensor_scalar(s0[:, i, :], bank(k % 2)[:, 0:D], rinv[:, i:i + 1], None, ALU.mult).then_inc(d_drained, 1)

            for i in range(NT + 1):
                if i < NT:
                    row_max(i)
                if i >= 1:
                    attention_out(i - 1)

            dve.wait_ge(s_wexp, 64)

            def mix(i, first=False):
                e = [dve.value_load(wexp[0:1, bass.ds(i * GROUP + b, 1)], min_val=0, max_val=E0 - 1) for b in range(GROUP)]
                dve.wait_ge(xg_turned, i + 1)
                dve.tensor_copy(xgT[:, :, :], bank(0).rearrange("p (b d) -> p b d", b=GROUP)).then_inc(xgT_ready, 1)
                for b in range(GROUP):
                    dve.wait_ge(h_done, i * GROUP + b + 1)
                    dve.tensor_tensor(hb[:, b, :], bank(2 + b), b1_row[:, e[b], :], ALU.add).then_inc(hb_ready, 1)
                if not first:
                    dve.wait_ge(og_stored, i * 16)
                for b in range(GROUP):
                    dve.wait_ge(o_done, i * GROUP + b + 1)
                    dve.tensor_tensor(og[:, b, :], bank(2 + b)[:, 0:D], b2_row[:, e[b], :], ALU.add).then_inc(og_ready, 1)

            mix(0, first=True)
            with dve.Fori(1, GROUPS) as i:
                mix(i)

            dve.wait_ge(gathered, 16 * NT)
            link(dve.tensor_tensor(tmp[:, :, :], y[:, :, :], moe[:, :, :], ALU.add))
            normalise(2, tmp, tmp)
            link(dve.tensor_tensor(tmp[:, :, :], tmp[:, :, :], rows(g2_row, NT), ALU.mult))
            link(dve.tensor_tensor(tmp[:, :, :], tmp[:, :, :], rows(be2_row, NT), ALU.add))
            dve.sem_inc(z_ready, 1)
            dve.wait_ge(g_ready, 1)
            link(dve.tensor_tensor(tmp[:, :, :], tmp[:, :, :], s0[:, :, :], ALU.mult))
            dve.tensor_tensor(x[:, :, :], x[:, :, :], tmp[:, :, :], ALU.add).then_inc(x1_ready, 1)
            dve.wait_ge(x1_ready, 1)

            normalise(3, x, xn, xn_ready)
            dve.wait_ge(xn_ready, 2 * NT)
            for g in range(4):
                drain(D_FILLS["xn1T"] + g, xnT[:, 512 * g:512 * (g + 1)])
            dve.wait_ge(d_drained, D_FILLS["xn1T"] + 4)
            link(dve.tensor_reduce(xsum[:, :], xnT[:, :].rearrange("p (c s) -> p c s", s=CS), AX.X, ALU.add))
            link(dve.tensor_scalar(xsum[:, :], xsum[:, :], 1.0 / CS, None, ALU.mult))
            link(dve.tensor_tensor_scan(xcum[:, :], ones[:, 0:NC], xsum[:, :], 0.0, ALU.mult, ALU.add))
            dve.tensor_tensor(xcum[:, :], xcum[:, :], xsum[:, :], ALU.subtract).then_inc(xsum_ready, 1)
            dve.wait_ge(mask_ready, 1)
            k = D_FILLS["kcum"]
            dve.wait_ge(d_filled, k + 1)
            dve.tensor_tensor(k4[:, :, :, CS], bank(k % 2)[:, 0:NC].unsqueeze(2).broadcast_to([P, NC, HG]),
                              mask4[:, :].unsqueeze(1).broadcast_to([P, NC, HG]), ALU.mult).then_inc(d_drained, 1)
            for g in range(4):
                drain(D_FILLS["q1"] + g, q1T[:, 512 * g:512 * (g + 1)])
            n = 512 // CS
            for g in range(4):
                drain(D_FILLS["k1"] + g, k1T[:, 512 * g:512 * (g + 1)])
            dve.wait_ge(d_drained, D_FILLS["k1"] + 4)
            for h in range(HG):
                link.mark(dve.tensor_scalar(k4[:, :, h, 0:CS], k1T[:, :].rearrange("p (c s) -> p c s", s=CS),
                                            mask4[:, h:h + 1], None, ALU.mult))
            for g in range(8):
                k = D_FILLS["vdup"] + g
                dve.wait_ge(d_filled, k + 1)
                for c in range(4):
                    ins = dve.tensor_tensor(vbd[:, 2 * g + c // 2, c % 2, :, 0:2 * D1],
                                            bank(k % 2)[:, c * D:(c + 1) * D].rearrange("p (n d) -> p n d", d=2 * D1),
                                            vmask[:, :].rearrange("p (n d) -> p n d", d=2 * D1), ALU.mult)
                ins.then_inc(d_drained, 1)
            for g in range(4):
                k = D_FILLS["vsum"] + g
                drain(k, vsum[:, 4 * g:4 * g + 4, :].rearrange("p t d -> p (t d)"))
            dve.wait_ge(d_drained, D_FILLS["vsum"] + 4)
            link.wait()
            dve.sem_inc(prep_ready, 1)

            sv = ps[:, 4:8, :]

            STEPS = 7

            def chunk_scores(i):
                dve.wait_ge(s_done, i + 1)
                if not isinstance(i, int) or i > 0:
                    dve.wait_ge(sigexp_ready, i)
                dve.tensor_copy(crs[:, :].rearrange("p (g h) -> p g h", g=4),
                                sv[:, :, 0:HG * (CS + 1)].rearrange("p g (h s) -> p g h s", h=HG)[:, :, :, CS]).then_inc(crs_ready, 1)
                if not isinstance(i, int) or i > 0:
                    dve.wait_ge(p_ready, i)
                for g in range(4):
                    ins = dve.tensor_tensor(sm[:, HG * g:HG * (g + 1), :], sv[:, g, 0:HG * (CS + 1)].rearrange("p (h s) -> p h s", h=HG)[:, :, 0:CS],
                                            amask[:, :].unsqueeze(1).broadcast_to([P, HG, CS]), ALU.add)
                ins.then_inc(s_read, 1)
                dve.wait_ge(s_read, i + 1)
                dve.tensor_reduce(mx1[:, :], sm[:, :, :], AX.X, ALU.max).then_inc(loop_step, 1)
                dve.wait_ge(loop_step, i * STEPS + 1)
                dve.tensor_tensor(sm[:, :, :], sm[:, :, :], mx1[:, :].unsqueeze(2).broadcast_to([P, H1, CS]), ALU.subtract).then_inc(sm_ready, 1)
                dve.wait_ge(sigexp_ready, i + 1)
                dve.tensor_scalar(sig[:, :], sig[:, :], 2.0, 2.0, ALU.mult, ALU.add).then_inc(loop_step, 1)
                dve.wait_ge(loop_step, i * STEPS + 2)
                dve.reciprocal(sig[:, :], sig[:, :]).then_inc(loop_step, 1)
                dve.wait_ge(loop_step, i * STEPS + 3)
                dve.tensor_tensor(cvx[:, :].rearrange("p (h d) -> p h d", d=D1), vsum[:, i, :].rearrange("p (h d) -> p h d", d=D1) if isinstance(i, int) else vsum[:, bass.ds(i, 1), :].rearrange("p o (h d) -> p (o h) d", d=D1),
                                  sig[:, :].unsqueeze(2).broadcast_to([P, H1, D1]), ALU.mult).then_inc(loop_step, 1)

            def chunk_out(i):
                dve.wait_ge(pv_done, i + 1)
                pv = bank(1)[:, 0:(H1 // 2) * (2 * D1 + 2)].rearrange("p (n c) -> p n c", n=H1 // 2)
                dve.reciprocal(rs1[:, :].rearrange("p (n c) -> p n c", c=2), pv[:, :, 2 * D1:2 * D1 + 2]).then_inc(loop_step, 1)
                dve.wait_ge(loop_step, i * STEPS + 5)
                ot = o1[:, i, :] if isinstance(i, int) else o1[:, bass.ds(i, 1), :].rearrange("p o d -> p (o d)")
                o_ = ot.rearrange("p (n c d) -> p n c d", c=2, d=D1)
                dve.tensor_tensor(o_, pv[:, :, 0:2 * D1].rearrange("p n (c d) -> p n c d", c=2),
                                  rs1[:, :].rearrange("p (n c) -> p n c", c=2).unsqueeze(3).broadcast_to([P, H1 // 2, 2, D1]), ALU.mult).then_inc(loop_step, 1)
                dve.wait_ge(loop_step, i * STEPS + 6)
                dve.sem_inc(pv_read, 1)
                dve.tensor_tensor(ot, ot, cvx[:, :], ALU.add).then_inc(loop_step, 1)
                dve.wait_ge(loop_step, i * STEPS + 7)

            chunk_scores(0)
            chunk_out(0)
            with dve.Fori(1, NT) as i:
                chunk_scores(i)
                chunk_out(i)
            dve.sem_inc(o1_ready, 1)
            for g in range(4):
                drain(D_FILLS["o1T"] + g, q1T[:, 512 * g:512 * (g + 1)])
            for g in range(4):
                drain(D_FILLS["s1"] + g, s0[:, 4 * g:4 * g + 4, :].rearrange("p t d -> p (t d)"))
            dve.wait_ge(d_drained, D_FILLS["s1"] + 4)

            def root_mean_square(n, src, dst, g_row, ready):
                for t in range(NT):
                    link.mark(dve.bn_stats(stats[:, t, :], src[:, t, :]))
                link.wait()
                for t in range(NT):
                    dve.bn_aggr(mv[:, t, :], stats[:, t, :]).then_inc(var_ready, 1)
                dve.wait_ge(rstd_ready, n + 1)
                for t in range(NT):
                    dve.scalar_tensor_tensor(out=dst[:, t, :], in0=src[:, t, :], scalar=rstd[:, t:t + 1], in1=g_row,
                                             op0=ALU.mult, op1=ALU.mult).then_inc(ready, 1)

            root_mean_square(4, xn, y, rg1_row, nx_ready)
            nxT = xnT
            for g in range(4):
                drain(D_FILLS["nxT"] + g, nxT[:, 512 * g:512 * (g + 1)])
            W3 = D + 2 * DM
            for g in range(8):
                k = D_FILLS["qkv"] + g
                dve.wait_ge(d_filled, k + 1)
                dve.tensor_copy(qkv[:, 2 * g:2 * g + 2, :], bank(k % 2)[:, 0:2 * W3].rearrange("p (t c) -> p t c", t=2)).then_inc(d_drained, 1)
            dve.wait_ge(d_drained, D_FILLS["qkv"] + 8)
            dve.sem_inc(cut_ready, 1)
            qv = qkv[:, :, 0:D].rearrange("p t (h d) -> p t h d", h=HM)
            kv = qkv[:, :, D:D + DM]
            r4 = rest[:, :, :].rearrange("p t (h d) -> p t h d", h=HM)
            link.mark(dve.tensor_copy(ka[:, :, 0:DM], kv))
            link.mark(dve.tensor_copy(v1[:, :, 0:DM], qkv[:, :, D + DM:W3]))
            link(dve.tensor_copy(qa[:, :, :, 0:DM], qv))
            link.mark(dve.tensor_tensor(restk[:, :, :], kv, ka[:, :, 0:DM], ALU.subtract))
            link(dve.tensor_tensor(r4, qv, qa[:, :, :, 0:DM], ALU.subtract))
            link.mark(dve.tensor_copy(ka[:, :, DM:2 * DM], restk[:, :, :]))
            link(dve.tensor_copy(qa[:, :, :, 2 * DM:3 * DM], r4))
            dve.sem_inc(parts_ready, 1)
            link.mark(dve.tensor_tensor(kb[:, :, 0:DM], restk[:, :, :], ka[:, :, DM:2 * DM], ALU.subtract))
            link(dve.tensor_tensor(qb[:, :, :, DM:2 * DM], r4, qa[:, :, :, 2 * DM:3 * DM], ALU.subtract))
            dve.sem_inc(parts_ready, 1)
            for n_, k0, dst in ((KA_ROWS, "kaT", kaT), (KB_ROWS, "kbT", kbT)):
                for g in range(2):
                    k = D_FILLS[k0] + g
                    dve.wait_ge(d_filled, k + 1)
                    dve.tensor_copy(dst[0:n_, 1024 * g:1024 * (g + 1)], bankb(k % 2)[0:n_, :]).then_inc(d_drained, 1)
            for g in range(8):
                k = D_FILLS["qaT"] + g
                dve.wait_ge(d_filled, k + 1)
                dve.tensor_copy(qaT[0:KA_ROWS, 2 * g:2 * g + 2, :].rearrange("p t c -> p (t c)"), bankb(k % 2)[0:KA_ROWS, :]).then_inc(d_drained, 1)

            MSTEPS = 5
            MU = 2 * HM

            def maximum(i, u):
                dve.wait_ge(mx_filled, i * MU + u + 1)
                dve.tensor_reduce(mxp[:, u // 2, u % 2:u % 2 + 1], ps[:, 0:2, :].rearrange("p b c -> p (b c)"), AX.X, ALU.max).then_inc(mx_read, 1)

            def cut_maximum(i):
                one = lambda a, c: a[:, i, :, c] if isinstance(i, int) else a[:, bass.ds(i, 1), :, c].rearrange("p o h -> p (o h)")
                dve.wait_ge(mx_read, i * MU + MU)
                dve.tensor_reduce(negm[:, :], mxp[:, :, :], AX.X, ALU.max, negate=True).then_inc(m_step, 1)
                dve.wait_ge(m_step, i * MSTEPS + 1)
                dve.tensor_copy(one(qb, 3 * DM), negm[:, :]).then_inc(m_step, 1)
                dve.wait_ge(m_step, i * MSTEPS + 2)
                dve.tensor_tensor(mr[:, :], negm[:, :], one(qb, 3 * DM), ALU.subtract).then_inc(m_step, 1)
                dve.wait_ge(m_step, i * MSTEPS + 3)
                dve.tensor_copy(one(qb, 3 * DM + 1), mr[:, :]).then_inc(m_step, 1)
                dve.wait_ge(m_step, i * MSTEPS + 4)
                dve.tensor_tensor(one(qb, 3 * DM + 2), mr[:, :], one(qb, 3 * DM + 1), ALU.subtract).then_inc(m_step, 1)
                dve.wait_ge(m_step, i * MSTEPS + 5)
                dve.sem_inc(m_ready, 1)

            def queries_b(i, slot_):
                dve.wait_ge(qb_turned, i + 1)
                dve.tensor_copy(qbT[0:KB_ROWS, slot_, :], bankb(7)[0:KB_ROWS, 0:HM * P]).then_inc(qbT_ready, 1)

            def shared_out(i):
                dve.wait_ge(om_filled, i + 1)
                o4 = bank(6)[:, 0:HM * (DM + 1)].rearrange("p (h c) -> p h c", h=HM)
                dve.reciprocal(rsm[:, :], o4[:, :, DM]).then_inc(om_read, 1)
                dve.wait_ge(om_read, 2 * i + 1)
                dst = (om[:, i, :] if isinstance(i, int) else om[:, bass.ds(i, 1), :].rearrange("p o d -> p (o d)")).rearrange("p (h d) -> p h d", h=HM)
                dve.tensor_tensor(dst, o4[:, :, 0:DM], rsm[:, :].unsqueeze(2).broadcast_to([P, HM, DM]), ALU.mult).then_inc(om_read, 1)

            dve.wait_ge(copies_ready, 2)
            for u in range(MU):
                maximum(0, u)
            cut_maximum(0)
            queries_b(0, 0)

            def shared_tile(i, parity, last=False):
                if not last:
                    for u in range(MU):
                        maximum(i + 1, u)
                    cut_maximum(i + 1)
                    queries_b(i + 1, 1 - parity)
                shared_out(i)

            with dve.Fori(0, NT // 2 - 1) as j:
                for parity in range(2):
                    shared_tile(j * 2 + parity, parity)
            shared_tile(NT - 2, 0)
            shared_tile(NT - 1, 1, last=True)
            dve.wait_ge(om_read, 2 * NT)

            for g in range(4):
                drain(D_FILLS["omT"] + g, xnT[:, 512 * g:512 * (g + 1)])
            for g in range(4):
                k = D_FILLS["mo"] + g
                dve.wait_ge(d_filled, k + 1)
                dve.tensor_tensor(xn[:, 4 * g:4 * g + 4, :], bank(k % 2).rearrange("p (t d) -> p t d", t=4),
                                  xn[:, 4 * g:4 * g + 4, :], ALU.add).then_inc(d_drained, 1)
            dve.wait_ge(d_drained, D_FILLS["mo"] + 4)
            nx2 = om
            root_mean_square(5, xn, nx2, rg2_row, nx_ready)
            for g in range(4):
                drain(D_FILLS["nx2T"] + g, xnT[:, 512 * g:512 * (g + 1)])
            k = D_FILLS["lg1"]
            dve.wait_ge(d_filled, k + 1)
            dve.tensor_tensor(lg1[:, :, :], bank(k % 2)[:, 0:NT * E1].rearrange("p (t e) -> p t e", t=NT),
                              eb_row.unsqueeze(1).broadcast_to([P, NT, E1]), ALU.add).then_inc(d_drained, 1)
            dve.wait_ge(d_drained, k + 1)
            wide = lambda a: a.unsqueeze(2).broadcast_to([P, NT, E1])
            link(dve.tensor_reduce(mrow[:, :], lg1[:, :, :], AX.X, ALU.max))
            dve.tensor_tensor(lg1[:, :, :], lg1[:, :, :], wide(mrow[:, :]), ALU.subtract).then_inc(rx_ready, 1)
            dve.wait_ge(rexp_ready, 1)
            link(dve.tensor_reduce(mrow[:, :], rw[:, :, :], AX.X, ALU.add))
            link(dve.reciprocal(mrow[:, :], mrow[:, :]))
            link(dve.tensor_tensor(rw[:, :, :], rw[:, :, :], wide(mrow[:, :]), ALU.mult))
            for t in range(NT):
                link.mark(dve.max(top1[:, t, :], rw[:, t, :]))
            link.wait()
            for t in range(NT):
                link.mark(dve.max_index(topi1[:, t, :], top1[:, t, :], rw[:, t, :]))
            link.wait()
            dve.tensor_tensor(w12[:, 1, :], top1[:, :, 1], top1[:, :, 0], ALU.subtract).then_inc(rx_ready, 1)
            link.mark(dve.tensor_copy(ix12[:, 0, :], topi1[:, :, 0]))
            link(dve.tensor_copy(ix12[:, 1, :], topi1[:, :, 1]))
            for e in range(E1):
                link.mark(dve.memset(iota1[:, :, e], float(e)))
            link.mark(dve.memset(comb[:, :, E1:ES], 1.0))
            dve.wait_ge(rexp_ready, 2)
            link(dve.tensor_scalar(w12[:, 0, :], w12[:, 1, :], 1.0, None, ALU.add))
            link(dve.reciprocal(w12[:, 0, :], w12[:, 0, :]))
            link(dve.tensor_tensor(w12[:, 1, :], w12[:, 1, :], w12[:, 0, :], ALU.mult))
            link.mark(dve.tensor_tensor(comb[:, :, 0:E1], iota1[:, :, :], wide(ix12[:, 0, :]), ALU.is_equal))
            link(dve.tensor_tensor(ctmp[:, :, :], iota1[:, :, :], wide(ix12[:, 1, :]), ALU.is_equal))
            link.mark(dve.tensor_tensor(comb[:, :, 0:E1], comb[:, :, 0:E1], wide(w12[:, 0, :]), ALU.mult))
            link(dve.tensor_tensor(ctmp[:, :, :], ctmp[:, :, :], wide(w12[:, 1, :]), ALU.mult))
            link(dve.tensor_tensor(comb[:, :, 0:E1], comb[:, :, 0:E1], ctmp[:, :, :], ALU.add))

            def expert_rows(j, e):
                n_ = j * ES + e
                dve.wait_ge(sg_ready, n_ + 1)
                if e >= 2 or not isinstance(j, int):
                    dve.wait_ge(e_filled, n_ - 1 + (e == 0))
                dve.tensor_tensor(h1T[:, e % 2, :], sg[:, e % 2, :], bank(2 * (e % 2) + 1), ALU.mult).then_inc(h1T_ready, 1)

            def add_expert(j, e):
                n_ = j * ES + e
                dve.wait_ge(e_filled, n_ + 1)
                q_ = CH // P
                for t in range(q_):
                    a_ = (xn[:, j * q_ + t, :] if isinstance(j, int) else xn[:, bass.ds(j * q_ + t, 1), :].rearrange("p o d -> p (o d)"))
                    c_ = (comb[:, j * q_ + t, e:e + 1] if isinstance(j, int) else comb[:, bass.ds(j * q_ + t, 1), e])
                    if e > 0:
                        dve.wait_ge(e_read, (n_ - 1) * q_ + t + 1)
                    dve.scalar_tensor_tensor(out=a_, in0=bank(4 + e % 2)[:, t * P:(t + 1) * P], scalar=c_, in1=a_,
                                             op0=ALU.mult, op1=ALU.add).then_inc(e_read, 1)

            def mixture(j):
                for e in range(ES + 1):
                    if e < ES:
                        expert_rows(j, e)
                    if e >= 1:
                        add_expert(j, e - 1)

            mixture(0)
            with dve.Fori(1, NCH) as j:
                mixture(j)
            dve.wait_ge(e_read, NT * ES)
            dve.sem_inc(acc_ready, 1)
            dve.wait_ge(g1_ready, 1)
            link(dve.tensor_tensor(y[:, :, :], y[:, :, :], s0[:, :, :], ALU.mult))
            dve.tensor_tensor(y[:, :, :], y[:, :, :], x[:, :, :], ALU.add).then_inc(fin_ready, 1)

        @block.scalar
        def _(act):
            act.wait_ge(s_w0, 48)
            dst = [vfT, kT, qT]
            for n in range(3):
                for g in range(4):
                    k = A_FILLS["proj"] + 4 * n + g
                    act.wait_ge(a_filled, k + 1)
                    act.activation(dst[n][:, 512 * g:512 * (g + 1)], bank(2 + k % 2), ACT.Identity,
                                   bias=cols0[:, n:n + 1], scale=1.0).then_inc(a_drained, 1)

            def exponents(i):
                act.wait_ge(nmax_ready, i + 1)
                n = (i + 1) * P
                s = ps[:, 4:8, :].rearrange("p b c -> p (b c)")[:, 0:n]
                if i >= 2:
                    act.wait_ge(d_filled, D_FILLS["pv"] + i - 1)
                act.activation(prob[:, i % 2, 0:n], s, ACT.Exp, bias=nmax[:, i:i + 1], scale=float(D) ** -0.5,
                               accum_out=rsum[:, i:i + 1]).then_inc(prob_ready, 1)

            turn = [A_FILLS["turn"]]

            def turned(i):
                for b in range(0, i + 1, 4):
                    k = turn[0]
                    n = min(4, i + 1 - b) * P
                    act.wait_ge(a_filled, k + 1)
                    act.activation(probT[:, k % 2, 0:n], bank(2 + k % 2)[:, 0:n], ACT.Copy).then_inc(a_drained, 1)
                    turn[0] += 1

            for i in range(NT + 1):
                if i < NT:
                    exponents(i)
                if i >= 1:
                    turned(i - 1)

            with act.Fori(0, GROUPS) as i:
                for b in range(GROUP):
                    act.wait_ge(h_turned, i * GROUP + b + 1)
                    act.activation(hT[:, b, :], bank(6 + b % 2), ACT.Relu).then_inc(hT_ready, 1)

            act.wait_ge(z_ready, 1)
            act.activation(tmp[:, :, :], tmp[:, :, :], ACT.Silu).then_inc(g_ready, 1)

            act.wait_ge(xsum_ready, 1)
            step = [0]
            for t in range(NT):
                if t >= 2:
                    act.wait_ge(xrep_used, t - 1)
                for c in range(2):
                    src = xnT[:, t * P + c * CS:t * P + (c + 1) * CS].unsqueeze(1).broadcast_to([P, 2, CS])
                    act.activation(xrep[:, t % 2, c, :].rearrange("p (r s) -> p r s", r=2), src, ACT.Copy).then_inc(xrep_ready, 1)
            for t in range(NT):
                act.wait_ge(xrep_used, NT + t - 1)
                src = xcum[:, 2 * t:2 * t + 2].unsqueeze(2).broadcast_to([P, 2, CS])
                act.activation(xrep[:, t % 2, 0, :].rearrange("p (r s) -> p r s", r=2), src, ACT.Copy).then_inc(xrep_ready, 1)

            def chunk_exponents(i):
                act.wait_ge(crs_ready, i + 1)
                if not isinstance(i, int):
                    act.wait_ge(loop_step, i * 7)
                act.activation(sig[:, :], crs[:, :], ACT.Exp, scale=-SC1).then_inc(sigexp_ready, 1)
                act.wait_ge(sm_ready, i + 1)
                if not isinstance(i, int):
                    act.wait_ge(p_turned, i)
                act.activation(pe1[:, :, :], sm[:, :, :], ACT.Exp, scale=SC1).then_inc(p_ready, 1)
                act.wait_ge(p_turned, i + 1)
                if not isinstance(i, int):
                    act.wait_ge(pv_done, i)
                act.activation(p1T[:, :, :], ps[:, 2:4, :].rearrange("p b (n c) -> p (b n) c", c=P), ACT.Copy).then_inc(pT_ready, 1)

            chunk_exponents(0)
            with act.Fori(1, NT) as i:
                chunk_exponents(i)

            act.wait_ge(parts_ready, 1)
            act.activation(ka[:, :, 2 * DM:3 * DM], ka[:, :, 0:DM], ACT.Copy).then_inc(act_step, 1)
            act.activation(kb[:, :, DM:2 * DM], ka[:, :, 0:DM], ACT.Copy).then_inc(act_step, 1)
            act.activation(kb[:, :, 2 * DM:3 * DM], ka[:, :, DM:2 * DM], ACT.Copy).then_inc(act_step, 1)
            act.activation(qa[:, :, :, DM:2 * DM], qa[:, :, :, 0:DM], ACT.Copy).then_inc(act_step, 1)
            act.activation(qb[:, :, :, 0:DM], qa[:, :, :, 0:DM], ACT.Copy).then_inc(act_step, 1)
            act.activation(qb[:, :, :, 2 * DM:3 * DM], qa[:, :, :, 2 * DM:3 * DM], ACT.Copy).then_inc(act_step, 1)
            act.wait_ge(act_step, 6)
            act.sem_inc(copies_ready, 1)

            def exponentials(i, first=False):
                for u in range(UNITS):
                    act.wait_ge(st_filled, i * UNITS + u + 1)
                    if not (first and u < 2):
                        act.wait_ge(pm_used, i * UNITS + u - 1)
                    b = 2 + 2 * (u % 2)
                    act.activation(pm[:, u % 2, :, :], ps[:, b:b + 2, :], ACT.Exp, scale=SCM).then_inc(pm_ready, 1)

            exponentials(0, first=True)
            with act.Fori(1, NT) as i:
                exponentials(i)

            act.wait_ge(rx_ready, 1)
            act.activation(rw[:, :, :], lg1[:, :, :], ACT.Exp).then_inc(rexp_ready, 1)
            act.wait_ge(rx_ready, 2)
            act.activation(w12[:, 1, :], w12[:, 1, :], ACT.Exp).then_inc(rexp_ready, 1)

            def gates(j):
                for e in range(ES):
                    n_ = j * ES + e
                    act.wait_ge(h13_filled, n_ + 1)
                    if e >= 2 or not isinstance(j, int):
                        act.wait_ge(h1T_ready, n_ - 1 + (e == 0))
                    act.activation(sg[:, e % 2, :], bank(2 * (e % 2)), ACT.Silu).then_inc(sg_ready, 1)

            gates(0)
            with act.Fori(1, NCH) as j:
                gates(j)
            act.wait_ge(acc_ready, 1)
            act.activation(y[:, :, :], xn[:, :, :], ACT.Silu).then_inc(g1_ready, 1)

        @block.tensor
        def _(pe):
            def d_fill(k):
                if k >= 2:
                    pe.wait_ge(d_drained, k - 1)
                return bank(k % 2)

            def a_fill(k):
                if k >= 2:
                    pe.wait_ge(a_drained, k - 1)
                return bank(2 + k % 2)

            pe.wait_ge(s_const, 1)

            def turn(k0, src, ready):
                for g in range(4):
                    o = d_fill(k0 + g)
                    for t in range(4 * g, 4 * g + 4):
                        if ready is not None:
                            pe.wait_ge(ready, t + 1)
                        ins = pe.transpose(o[:, P * (t % 4):P * (t % 4 + 1)], src[:, t, :], ident[:, :])
                    ins.then_inc(d_filled, 1)

            turn(D_FILLS["xnT"], xn, xn_ready)
            pe.wait_ge(s_w0, 48)
            W = dict(q=w0[:, 0:D], k=w0[:, D:2 * D], v=w0[:, 2 * D:3 * D], vf=w0[:, 3 * D:4 * D], o=w0[:, 4 * D:5 * D])
            for g in range(4):
                pe.wait_ge(d_drained, D_FILLS["xnT"] + g + 1)
                pe.matmul(a_fill(g), W["vf"], xnT[:, 512 * g:512 * (g + 1)], start=True, stop=True).then_inc(a_filled, 1)
            for g in range(4):
                o = d_fill(D_FILLS["v"] + g)
                for t in range(4 * g, 4 * g + 4):
                    ins = pe.matmul(o[:, P * (t % 4):P * (t % 4 + 1)], xnT[:, P * t:P * (t + 1)], W["v"], start=True, stop=True)
                ins.then_inc(d_filled, 1)
            for g in range(4):
                o = d_fill(D_FILLS["mha"] + g)
                pe.wait_ge(a_drained, g + 1)
                for t in range(4 * g, 4 * g + 4):
                    ins = pe.matmul(o[:, P * (t % 4):P * (t % 4 + 1)], vfT[:, P * t:P * (t + 1)], W["o"], start=True, stop=True)
                ins.then_inc(d_filled, 1)
            for g in range(4):
                pe.matmul(a_fill(4 + g), W["k"], xnT[:, 512 * g:512 * (g + 1)], start=True, stop=True).then_inc(a_filled, 1)
            pe.wait_ge(y_ready, NT)
            turn(D_FILLS["yT"], y, None)
            o = d_fill(D_FILLS["logits"])
            pe.wait_ge(d_drained, D_FILLS["yT"] + 4)
            for t in range(NT):
                ins = pe.matmul(o[:, E0 * t:E0 * (t + 1)], yT[:, P * t:P * (t + 1)], wgT[:, :], start=True, stop=True)
            ins.then_inc(d_filled, 1)
            pe.wait_ge(d_filled, D_FILLS["logits"] + 1)
            for g in range(4):
                pe.matmul(a_fill(8 + g), W["q"], xnT[:, 512 * g:512 * (g + 1)], start=True, stop=True).then_inc(a_filled, 1)
            pe.wait_ge(onehot_ready, 1)
            o = d_fill(D_FILLS["ranks"])
            oh = onehot[:, :, :].rearrange("p e t -> p (e t)")
            pe.matmul(o[:, 0:NT * E0], before[:, :], oh, start=True, stop=True)
            pe.matmul(o[:, NT * E0:2 * NT * E0], ones[:, :], oh, start=True, stop=True).then_inc(d_filled, 1)

            pe.wait_ge(a_drained, A_FILLS["turn"])
            turns = [A_FILLS["turn"]]

            def scores(i):
                n = (i + 1) * P
                if i >= 1:
                    pe.wait_ge(prob_ready, i)
                for c in range(0, n, 512):
                    m = min(512, n - c)
                    ins = pe.matmul(ps[:, 4 + c // 512, 0:m], qT[:, P * i:P * (i + 1)], kT[:, c:c + m], start=True, stop=True)
                ins.then_inc(score_done, 1)

            def turn_probs(i, b):
                k = turns[0]
                o = a_fill(k)
                if b == 0:
                    pe.wait_ge(prob_ready, i + 1)
                for j in range(b, min(b + 4, i + 1)):
                    ins = pe.transpose(o[:, P * (j - b):P * (j - b + 1)], prob[:, i % 2, P * j:P * (j + 1)], ident[:, :])
                ins.then_inc(a_filled, 1)
                turns[0] += 1
                return k

            def weigh(i, b, k, o):
                pe.wait_ge(a_drained, k + 1)
                for j in range(b, min(b + 4, i + 1)):
                    ins = pe.matmul(o[:, 0:D], probT[:, k % 2, P * (j - b):P * (j - b + 1)], v[:, j, :],
                                    start=(j == 0), stop=(j == i))
                if b + 4 > i:
                    ins.then_inc(d_filled, 1)

            def values(i):
                o = d_fill(D_FILLS["pv"] + i)
                last = None
                for b in range(0, i + 1, 4):
                    k = turn_probs(i, b)
                    if last is not None:
                        weigh(i, *last, o)
                    last = (b, k)
                weigh(i, *last, o)

            for i in range(NT + 1):
                if i < NT:
                    scores(i)
                if i >= 1:
                    values(i - 1)

            pe.wait_ge(wexp_ready, 1)
            pe.wait_ge(s_wexp, 64)
            pe.wait_ge(d_drained, D_FILLS["pv"] + NT)
            pe.wait_ge(prob_ready, NT)

            def mix(i, first=False):
                e = [pe.value_load(wexp[0:1, bass.ds(i * GROUP + b, 1)], min_val=0, max_val=E0 - 1) for b in range(GROUP)]
                pe.wait_ge(xg_loaded, i * 16 + 16)
                for b in range(GROUP):
                    ins = pe.transpose(bank(0)[:, b * D:(b + 1) * D], xg[:, b, :], ident[:, :])
                ins.then_inc(xg_turned, 1)
                pe.wait_ge(xgT_ready, i + 1)
                for b in range(GROUP):
                    if not first:
                        pe.wait_ge(og_ready, i * GROUP + b - GROUP + 1)
                    pe.matmul(bank(2 + b), xgT[:, b, :], w1[:, e[b], :], start=True, stop=True).then_inc(h_done, 1)
                for b in range(GROUP):
                    pe.wait_ge(hb_ready, i * GROUP + b + 1)
                    if b >= 2:
                        pe.wait_ge(hT_ready, i * GROUP + b - 1)
                    for c in range(FC0):
                        ins = pe.transpose(bank(6 + b % 2)[:, c * P:(c + 1) * P], hb[:, b, c * P:(c + 1) * P], ident[:, :])
                    ins.then_inc(h_turned, 1)
                for b in range(GROUP):
                    pe.wait_ge(hT_ready, i * GROUP + b + 1)
                    for c in range(FC0):
                        ins = pe.matmul(bank(2 + b)[:, 0:D], hT[:, b, c * P:(c + 1) * P], w2[:, e[b], c, :],
                                        start=(c == 0), stop=(c == FC0 - 1))
                    ins.then_inc(o_done, 1)

            mix(0, first=True)
            with pe.Fori(1, GROUPS) as i:
                mix(i)



            pe.wait_ge(s_w1, 64)

            def turn1(k0, src, ready, first):
                for g in range(4):
                    o = d_fill(k0 + g)
                    for t in range(4 * g, 4 * g + 4):
                        if ready is not None:
                            pe.wait_ge(ready, first + t + 1)
                        ins = pe.transpose(o[:, P * (t % 4):P * (t % 4 + 1)], src[:, t, :], ident[:, :])
                    ins.then_inc(d_filled, 1)

            turn1(D_FILLS["xn1T"], xn, xn_ready, NT)
            pe.wait_ge(xsum_ready, 1)
            o = d_fill(D_FILLS["kcum"])
            pe.matmul(o[:, 0:NC], wk1, xcum[:, :], start=True, stop=True).then_inc(d_filled, 1)
            for name, w in (("q1", wq1), ("k1", wk1)):
                for g in range(4):
                    pe.matmul(d_fill(D_FILLS[name] + g), w, xnT[:, 512 * g:512 * (g + 1)], start=True, stop=True).then_inc(d_filled, 1)
            for g in range(8):
                o = d_fill(D_FILLS["vdup"] + g)
                for t in (2 * g, 2 * g + 1):
                    for c in range(2):
                        pe.wait_ge(xrep_ready, 2 * t + c + 1)
                        n = 2 * (t % 2) + c
                        ins = pe.matmul(o[:, n * D:(n + 1) * D], xrep[:, t % 2, c, :], wv1, start=True, stop=True)
                        if n < 3 and c == 1:
                            ins.then_inc(xrep_used, 1)
                ins.then_inc(d_filled, 1)
                pe.wait_ge(d_filled, D_FILLS["vdup"] + g + 1)
                pe.sem_inc(xrep_used, 1)
            for g in range(4):
                o = d_fill(D_FILLS["vsum"] + g)
                for t in range(4 * g, 4 * g + 4):
                    pe.wait_ge(xrep_ready, 2 * NT + t + 1)
                    ins = pe.matmul(o[:, P * (t % 4):P * (t % 4 + 1)], xrep[:, t % 2, 0, :], wv1, start=True, stop=True)
                    if t % 4 < 3:
                        ins.then_inc(xrep_used, 1)
                ins.then_inc(d_filled, 1)
                pe.wait_ge(d_filled, D_FILLS["vsum"] + g + 1)
                pe.sem_inc(xrep_used, 1)
            pe.wait_ge(prep_ready, 1)

            def chunk_products(i):
                pe.wait_ge(qtile_ready, i * 2 + 2)
                if not isinstance(i, int):
                    pe.wait_ge(s_read, i)
                for c in range(2):
                    for g in range(D // 32):
                        r = slice(32 * g, 32 * (g + 1))
                        kk = ktile[r, c, :, :].rearrange("p h s -> p (h s)")
                        ins = pe.matmul(ps[CS * c:CS * (c + 1), 4 + g, 0:HG * (CS + 1)], qtile[r, CS * c:CS * (c + 1)], kk,
                                        start=True, stop=True)
                ins.then_inc(s_done, 1)
                pe.wait_ge(p_ready, i + 1)
                if not isinstance(i, int):
                    pe.wait_ge(pT_ready, i)
                flat = pe1[:, :, :].rearrange("p h s -> p (h s)")
                for n in range(H1 // 2):
                    ins = pe.transpose(ps[:, 2 + n // 4, P * (n % 4):P * (n % 4 + 1)], flat[:, P * n:P * (n + 1)], ident[:, :])
                ins.then_inc(p_turned, 1)
                pe.wait_ge(pT_ready, i + 1)
                if not isinstance(i, int):
                    pe.wait_ge(pv_read, i)
                w = 2 * D1 + 2
                pe.wait_ge(vtile_ready, i + 1)
                for c in range(2):
                    for n in range(H1 // 2):
                        ins = pe.matmul(ps[CS * c:CS * (c + 1), 1, w * n:w * (n + 1)], p1T[:, n, CS * c:CS * (c + 1)], vtile[:, c, n, :],
                                        start=True, stop=True)
                ins.then_inc(pv_done, 1)

            chunk_products(0)
            with pe.Fori(1, NT) as i:
                chunk_products(i)
            pe.wait_ge(o1_ready, 1)
            turn1(D_FILLS["o1T"], o1, None, 0)
            for g in range(4):
                o = d_fill(D_FILLS["s1"] + g)
                pe.wait_ge(d_drained, D_FILLS["o1T"] + g + 1)
                for t in range(4 * g, 4 * g + 4):
                    ins = pe.matmul(o[:, P * (t % 4):P * (t % 4 + 1)], q1T[:, P * t:P * (t + 1)], wout1, start=True, stop=True)
                ins.then_inc(d_filled, 1)

            turn1(D_FILLS["nxT"], y, nx_ready, 0)
            W3 = D + 2 * DM
            for g in range(8):
                o = d_fill(D_FILLS["qkv"] + g)
                pe.wait_ge(d_drained, D_FILLS["nxT"] + g // 2 + 1)
                for t in range(2 * g, 2 * g + 2):
                    ins = pe.matmul(o[:, W3 * (t % 2):W3 * (t % 2 + 1)], xnT[:, P * t:P * (t + 1)], wmq, start=True, stop=True)
                ins.then_inc(d_filled, 1)
            pe.wait_ge(parts_ready, 2)
            pe.wait_ge(copies_ready, 2)
            for n_, k0, src in ((KA_ROWS, "kaT", ka), (KB_ROWS, "kbT", kb)):
                for g in range(2):
                    d_fill(D_FILLS[k0] + g)
                    o = bankb((D_FILLS[k0] + g) % 2)
                    for t in range(8):
                        ins = pe.transpose(o[0:n_, P * t:P * (t + 1)], src[:, 8 * g + t, 0:n_], identb[:, :])
                    ins.then_inc(d_filled, 1)
            for g in range(8):
                d_fill(D_FILLS["qaT"] + g)
                o = bankb((D_FILLS["qaT"] + g) % 2)
                for n in range(8):
                    ins = pe.transpose(o[0:KA_ROWS, P * n:P * (n + 1)], qa[:, 2 * g + n // HM, n % HM, :], identb[:, :])
                ins.then_inc(d_filled, 1)
            pe.wait_ge(d_drained, D_FILLS["qaT"] + 8)

            MU = 2 * HM

            def at(a, i):
                return a[:, i] if isinstance(i, int) else a[:, bass.ds(i, 1)]

            def maximum(i, u, first=False):
                h, half = u // 2, u % 2
                if not (first and u == 0):
                    pe.wait_ge(mx_read, i * MU + u)
                q = qaT[0:KA_ROWS, i, h * P:(h + 1) * P] if isinstance(i, int) else \
                    qaT[0:KA_ROWS, bass.ds(i, 1), h * P:(h + 1) * P].rearrange("p o c -> p (o c)")
                for n in range(2):
                    c = half * 1024 + n * 512
                    ins = pe.matmul(bank(n), q, kaT[0:KA_ROWS, c:c + 512], start=True, stop=True)
                ins.then_inc(mx_filled, 1)

            def turn_b(i):
                pe.wait_ge(m_ready, i + 1)
                for h in range(HM):
                    q = qb[:, i, h, 0:KB_ROWS] if isinstance(i, int) else qb[:, bass.ds(i, 1), h, 0:KB_ROWS].rearrange("p o c -> p (o c)")
                    ins = pe.transpose(bankb(7)[0:KB_ROWS, P * h:P * (h + 1)], q, identb[:, :])
                ins.then_inc(qb_turned, 1)

            def scores_t(i, u, parity, first):
                if u == 0:
                    pe.wait_ge(qbT_ready, i + 1)
                if not (first and u < 2):
                    pe.wait_ge(pm_ready, i * UNITS + u - 1)
                q = qaT[0:KA_ROWS, i, :] if isinstance(i, int) else qaT[0:KA_ROWS, bass.ds(i, 1), :].rearrange("p o c -> p (o c)")
                for n in range(2):
                    kt = slice((2 * u + n) * P, (2 * u + n + 1) * P)
                    o = bank(2 + 2 * (u % 2) + n)
                    pe.matmul(o, kaT[0:KA_ROWS, kt], q, start=True, stop=False)
                    ins = pe.matmul(o, kbT[0:KB_ROWS, kt], qbT[0:KB_ROWS, parity, :], start=False, stop=True)
                ins.then_inc(st_filled, 1)

            def weigh_t(i, u, first):
                pe.wait_ge(pm_ready, i * UNITS + u + 1)
                if u == 0 and not first:
                    pe.wait_ge(om_read, i * 2)
                for n in range(2):
                    for h in range(HM):
                        ins = pe.matmul(bank(6)[:, h * (DM + 1):(h + 1) * (DM + 1)], pm[:, u % 2, n, h * P:(h + 1) * P],
                                        v1[:, 2 * u + n, :], start=(u == 0 and n == 0 and h == 0),
                                        stop=(u == UNITS - 1 and n == 1 and h == HM - 1), skip_group_check=True)
                ins.then_inc(pm_used, 1)

            for u in range(MU):
                maximum(0, u, first=True)
            turn_b(0)

            def shared_tile(i, parity, first=False, last=False):
                m = 0
                for u in range(UNITS + 1):
                    if u < UNITS:
                        if not last and u < 2:
                            maximum(i + 1, m)
                            m += 1
                        scores_t(i, u, parity, first)
                        if not last and u < 6:
                            maximum(i + 1, m)
                            m += 1
                    if u == UNITS - 1 and not last:
                        turn_b(i + 1)
                    if u >= 1:
                        weigh_t(i, u - 1, first)
                        if u == UNITS:
                            pe.wait_ge(pm_used, i * UNITS + UNITS)
                            pe.sem_inc(om_filled, 1)

            shared_tile(0, 0, first=True)
            shared_tile(1, 1)
            with pe.Fori(1, NT // 2 - 1) as j:
                for parity in range(2):
                    shared_tile(j * 2 + parity, parity)
            shared_tile(NT - 2, 0)
            shared_tile(NT - 1, 1, last=True)

            pe.wait_ge(om_read, 2 * NT)
            turn1(D_FILLS["omT"], om, None, 0)
            for g in range(4):
                o = d_fill(D_FILLS["mo"] + g)
                pe.wait_ge(d_drained, D_FILLS["omT"] + g + 1)
                for t in range(4 * g, 4 * g + 4):
                    ins = pe.matmul(o[:, P * (t % 4):P * (t % 4 + 1)], xnT[:, P * t:P * (t + 1)], wmo, start=True, stop=True)
                ins.then_inc(d_filled, 1)
            turn1(D_FILLS["nx2T"], om, nx_ready, NT)
            pe.wait_ge(d_drained, D_FILLS["nx2T"] + 4)
            o = d_fill(D_FILLS["lg1"])
            for t in range(NT):
                ins = pe.matmul(o[:, E1 * t:E1 * (t + 1)], xnT[:, P * t:P * (t + 1)], wr, start=True, stop=True)
            ins.then_inc(d_filled, 1)
            pe.wait_ge(d_drained, D_FILLS["lg1"] + 1)

            def hidden(j, e):
                n_ = j * ES + e
                if e >= 2 or not isinstance(j, int):
                    pe.wait_ge(h1T_ready, n_ - 1 + (e == 0))
                rhs = xnT[:, j * CH:(j + 1) * CH] if isinstance(j, int) else xnT[:, bass.ds(j * CH, CH)]
                pe.matmul(bank(2 * (e % 2)), e13[:, e, 0:D], rhs, start=True, stop=True)
                pe.matmul(bank(2 * (e % 2) + 1), e13[:, e, D:2 * D], rhs, start=True, stop=True).then_inc(h13_filled, 1)

            def project(j, e):
                n_ = j * ES + e
                pe.wait_ge(h1T_ready, n_ + 1)
                if e >= 2 or not isinstance(j, int):
                    pe.wait_ge(e_read, (n_ - 1 + (e == 0)) * (CH // P))
                for t in range(CH // P):
                    ins = pe.matmul(bank(4 + e % 2)[:, t * P:(t + 1) * P], h1T[:, e % 2, t * P:(t + 1) * P], e2[:, e, :],
                                    start=True, stop=True)
                ins.then_inc(e_filled, 1)

            def mixture(j):
                for e in range(ES + 1):
                    if e < ES:
                        hidden(j, e)
                    if e >= 1:
                        project(j, e - 1)

            mixture(0)
            with pe.Fori(1, NCH) as j:
                mixture(j)


def layouts(np, i):
    c = np.ascontiguousarray
    a = {k: np.asarray(v) for k, v in i.items()}
    D_ = a["L0_attn_Wq"].shape[0]
    return dict(
        x=c(a["L0_attn_x"].reshape(-1, D_)),
        w0=c(np.concatenate([a["L0_attn_Wq"].T, a["L0_attn_Wk"].T, a["L0_attn_Wv"].T, a["L0_ffn_Wqkv"][2 * D_:].T, a["L0_ffn_Wo"].T], axis=1)),
        cols0=c(np.stack([a["L0_ffn_bqkv"][2 * D_:], a["L0_attn_bk"], a["L0_attn_bq"]], axis=1)),
        rows0=c(np.concatenate([a["L0_attn_bv"], a["L0_ffn_bo"], a["L0_ffn_g1"], a["L0_ffn_be1"], a["L0_ffn_g2"], a["L0_ffn_be2"]])),
        wgT=c(a["L0_ffn_Wg"].T),
        w1=c(a["L0_ffn_W1"].transpose(1, 0, 2)),
        b1=c(a["L0_ffn_b1"].reshape(-1)),
        w2=c(a["L0_ffn_W2"].reshape(8, 4, 128, D_).transpose(2, 0, 1, 3)),
        b2=c(a["L0_ffn_b2"].reshape(-1)),
        wl1=c(np.concatenate([a["L1_attn_W_qkv"], a["L1_attn_W_out"], a["L1_ffn_Wq"].T, a["L1_ffn_Wkc"].T, a["L1_ffn_Wvc"].T,
                              a["L1_ffn_Wo"].T, a["L1_ffn_Wr"].T], axis=1)),
        rows1=c(np.concatenate([a["L1_ffn_g1"], a["L1_ffn_g2"], a["L1_ffn_expert_bias"]])),
        e13=c(np.concatenate([np.concatenate([a["L1_ffn_eW1"], a["L1_ffn_sW1"][None]]),
                              np.concatenate([a["L1_ffn_eW3"], a["L1_ffn_sW3"][None]])], axis=1).transpose(2, 0, 1)),
        e2=c(np.concatenate([a["L1_ffn_eW2"], a["L1_ffn_sW2"][None]]).transpose(2, 0, 1)),
    )


def kernel(**inputs):
    import numpy as np
    import concourse.bacc as bacc
    from concourse.bass_utils import run_bass_kernel_spmd

    arrays = layouts(np, inputs)
    shape = tuple(inputs["L0_attn_x"].shape)
    nc = bacc.Bacc("TRN2", target_bir_lowering=False, num_devices=1)
    aps = {n: nc.dram_tensor(f"in_{n}", a.shape, mybir.dt.from_np(a.dtype), kind="ExternalInput").ap() for n, a in arrays.items()}
    out = nc.dram_tensor("out_0", [shape[0] * shape[1], shape[2]], F32, kind="ExternalOutput").ap()
    bass_recurrent_two_layers(nc, aps, out)
    r = run_bass_kernel_spmd(nc, [{f"in_{n}": a for n, a in arrays.items()}], core_ids=[0])
    return r.results[0]["out_0"].reshape(shape)
```

```python
from contextlib import ExitStack

import concourse.bass as bass
from concourse import mybir

P = 128
T = 2048
NT = T // P
D = 128
F32 = mybir.dt.float32
F32R = mybir.dt.float32r
I32 = mybir.dt.int32
U32 = mybir.dt.uint32
ALU = mybir.AluOpType
ACT = mybir.ActivationFunctionType
AX = mybir.AxisListType

E0 = 8
F0 = 512
FC0 = F0 // P
GROUP = 4
WINDOWS = -(-(NT + E0 - 1) // GROUP) * GROUP
GROUPS = WINDOWS // GROUP
NEG = -1.0e30

CS = 64
NC = T // CS
H1 = 16
D1 = D // H1
HG = 4
SC1 = float(D1) ** -0.5
MASKED = -65000.0
REGION = 24 * 1024
HM = 4
DM = D // HM
SCM = float(DM) ** -0.5
R_ROWS = 3 * DM
M_ROWS = R_ROWS + 2
VW = 3 * DM
KIND = "dpdwdpdwdpdpdpdw"
CUT = [t for t in range(NT) if KIND[t] != "w"]
CUT_D = [t for t in range(NT) if KIND[t] == "d"]
CUT_P = [t for t in range(NT) if KIND[t] == "p"]
RING = 4
LAG = 3
MU = HM * T // 512
MAX_SLOTS = (2, 3, 3, 4, 5, 6, 6, 7, 8, 9, 9, 10, 11, 12, 12, 13)
TURN_SLOT = 14
E1 = 8
ES = E1 + 1
CH = 512
NCH = T // CH


class Region:

    def __init__(self, tensor, size):
        self.tensor, self.size, self.at = tensor, size, 0

    def reset(self, at=0):
        self.at = at

    def take(self, *shape):
        words = 1
        for d in shape:
            words *= d
        assert self.at + words <= self.size, (self.at, words, self.size)
        a = self.tensor[:, self.at:self.at + words]
        self.at += words
        names = "abcd"[:len(shape)]
        if len(shape) == 1:
            return a
        return a.rearrange(f"p ({' '.join(names)}) -> p {' '.join(names)}", **dict(zip(names, shape)))


class Link:

    def __init__(self, engine, sem):
        self.engine, self.sem, self.n = engine, sem, 0

    def mark(self, ins):
        self.n += 1
        ins.then_inc(self.sem, 1)

    def wait(self):
        self.engine.wait_ge(self.sem, self.n)

    def __call__(self, ins):
        self.mark(ins)
        self.wait()


def at(a, i):
    if isinstance(i, int):
        return a[:, i]
    one = a[:, bass.ds(i, 1)]
    names = " ".join("abcd"[:len(one.shape) - 2])
    return one.rearrange(f"p o {names} -> p (o {names.split()[0]}) {' '.join(names.split()[1:])}")


def over_tiles(engine, tile, ahead):
    tile(0, 0, first=True, more=ahead < NT)
    tile(1, 1)
    with engine.Fori(1, NT // 2 - 1) as j:
        for parity in range(2):
            tile(j * 2 + parity, parity)
    tile(NT - 2, 0, more=ahead < 2)
    tile(NT - 1, 1, more=False)


def cuts(sizes):
    at, found = 0, []
    for n in sizes:
        found.append((at, at + n))
        at += n
    return found


def bass_recurrent_two_layers(nc, A, out):
    with ExitStack() as ctx:
        def sb(name, shape, dt=F32):
            return ctx.enter_context(nc.sbuf_tensor(name, shape, dt))

        def sem(name):
            return ctx.enter_context(nc.semaphore(name))

        ps = ctx.enter_context(nc.psum_tensor("ps", [P, 8, 512], F32))

        slots_in = nc.dram_tensor("slots_in", [WINDOWS * P, D], F32, kind="Internal").ap()
        slots_out = nc.dram_tensor("slots_out", [WINDOWS * P, D], F32, kind="Internal").ap()

        region = Region(sb("region", [P, REGION]), REGION)
        x = sb("x", [P, NT, D])
        xn = sb("xn", [P, NT, D])
        xnT = sb("xnT", [P, T])
        qT = region.take(T)
        kT = region.take(T)
        v = region.take(NT, D)
        vfT = region.take(T)
        y = sb("y", [P, NT, D])
        s0 = sb("s0", [P, NT, D])
        w0 = sb("w0", [P, 5 * D])
        cols0 = sb("cols0", [P, 3])
        rows0 = sb("rows0", [P, 6 * D])
        bv_row, bo_row, g1_row, be1_row, g2_row, be2_row = (rows0[:, n * D:(n + 1) * D] for n in range(6))
        wgT = sb("wgT", [P, E0])
        b1_col = sb("b1_col", [P, E0, FC0])
        w1 = region.take(E0, F0)
        w2 = region.take(E0, FC0, D)
        b2_row = region.take(E0, D)
        ident = sb("ident", [P, P])
        ones = sb("ones", [P, P])
        before = sb("before", [P, P])
        causal = sb("causal", [P, P])
        zeros = sb("zeros", [P, D])
        stats = sb("stats", [P, NT, 6])
        mv = sb("mv", [P, NT, 2])
        vare = sb("vare", [P, NT])
        mhalf = sb("mhalf", [P, NT])
        rstd = sb("rstd", [P, NT])
        lg = sb("lg", [P, NT, E0])
        top = sb("top", [P, NT, 8])
        topi = sb("topi", [P, NT, 8], U32)
        expert = sb("expert", [P, NT])
        iota_e = sb("iota_e", [P, E0, NT])
        onehot = sb("onehot", [P, E0, NT])
        rank = sb("rank", [P, E0, NT])
        upto = sb("upto", [P, E0, NT])
        scanmask = sb("scanmask", [P, E0, NT])
        cnt_i = sb("cnt_i", [P, E0], I32)
        cnt_f = sb("cnt_f", [P, E0])
        pad = sb("pad", [P, E0])
        end = sb("end", [P, E0])
        base = sb("base", [P, E0])
        slot_f = sb("slot_f", [P, NT])
        slot = sb("slot", [P, NT], U32)
        wstart = sb("wstart", [P, WINDOWS, E0])
        wcmp = sb("wcmp", [P, WINDOWS, E0])
        wexp_f = sb("wexp_f", [P, WINDOWS])
        wexp = sb("wexp", [P, WINDOWS], I32)
        xg = region.take(GROUP, D)
        overlay = region.at
        prob = region.take(2, T)
        probT = region.take(2, 512)
        rmax = sb("rmax", [P, NT])
        nmax = sb("nmax", [P, NT])
        rsum = sb("rsum", [P, NT])
        rinv = sb("rinv", [P, NT])
        region.reset(overlay)
        tmp = region.take(NT, D)
        region.reset(overlay)
        xgT = region.take(GROUP, P)
        hb = region.take(GROUP, F0)
        hT = region.take(GROUP, F0)
        og = sb("og", [P, GROUP, D])
        moe = vfT[:, :].rearrange("p (t d) -> p t d", t=NT)
        yT = qT

        wl1 = sb("wl1", [P, 3 * D + D + (D + 2 * DM) + D + E1])
        wq1, wk1, wv1, wout1, wmq, wmo, wr = (wl1[:, a:b] for a, b in cuts([D, D, D, D, D + 2 * DM, D, E1]))
        e13 = sb("e13", [P, ES, 2 * D])
        e2 = sb("e2", [P, ES, D])
        rows1 = sb("rows1", [P, 2 * D + E1])
        rg1_row, rg2_row, eb_row = (rows1[:, a:b] for a, b in cuts([D, D, E1]))
        msq = sb("msq", [P, NT])
        region.reset()
        k4 = region.take(NC, HG, CS + 1)
        vbd = region.take(NT, 2, H1 // 2, 2 * D1 + 2)
        vsum = region.take(NT, D)
        q1T = region.take(T)
        sm = region.take(H1, CS)
        pe1 = region.take(H1, CS)
        p1T = region.take(H1 // 2, P)
        amask = region.take(CS)
        mask4 = region.take(HG)
        vmask = region.take(D)
        xsum = region.take(NC)
        xcum = region.take(NC)
        xrep = region.take(2, 2, P)
        qtile = region.take(P)
        ktile = region.take(2, HG, CS + 1)
        vtile = region.take(2, H1 // 2, 2 * D1 + 2)
        crs = region.take(H1)
        sig = region.take(H1)
        mx1 = region.take(H1)
        rs1 = region.take(H1)
        cvx = region.take(D)
        o1 = region.take(NT, D)
        region.reset()
        om = region.take(NT, D)
        qkv = region.take(NT, D + 2 * DM)
        rest = region.take(NT, D)
        qa = region.take(NT, HM, R_ROWS)
        ka = region.take(NT, M_ROWS)
        qtile2 = region.take(2, HM, M_ROWS)
        v1 = region.take(NT, DM + 1)
        pm = region.take(RING, HM * P)
        mxp = region.take(HM, MU // HM)
        negm = region.take(HM)
        oT = region.take(HM * P)
        ol = region.take(HM, DM)
        rsm = region.take(HM)
        qr = sb("qr", [P, 2, HM * P], F32R)
        kr = sb("kr", [P, T], F32R)
        vr = sb("vr", [P, NT, VW], F32R)
        ph = sb("ph", [P, RING, HM * P], F32R)
        pl = sb("pl", [P, RING, HM * P], F32R)
        region.reset(NT * D)
        lg1 = region.take(NT, E1)
        rw = region.take(NT, E1)
        top1 = region.take(NT, 8)
        topi1 = region.take(NT, 8).bitcast(U32)
        mrow = region.take(NT)
        w12 = region.take(2, NT)
        ix12 = region.take(2, NT)
        iota1 = region.take(NT, E1)
        comb = region.take(NT, ES)
        ctmp = region.take(NT, E1)
        sg = region.take(2, CH)
        h1T = region.take(2, CH)
        acc = y

        s_x = sem("s_x"); s_w0 = sem("s_w0"); s_rows0 = sem("s_rows0"); s_wexp = sem("s_wexp")
        s_const = sem("s_const"); s_zero = sem("s_zero"); s_zeroed = sem("s_zeroed")
        dve_step = sem("dve_step"); pool_step = sem("pool_step"); act_step = sem("act_step")
        var_ready = sem("var_ready"); rstd_ready = sem("rstd_ready")
        xn_ready = sem("xn_ready")
        d_filled = sem("d_filled"); d_drained = sem("d_drained")
        a_filled = sem("a_filled"); a_drained = sem("a_drained")
        y_ready = sem("y_ready"); onehot_ready = sem("onehot_ready")
        slot_ready = sem("slot_ready"); scattered = sem("scattered"); wexp_ready = sem("wexp_ready")
        score_done = sem("score_done"); nmax_ready = sem("nmax_ready"); prob_ready = sem("prob_ready")
        xg_loaded = sem("xg_loaded"); xg_turned = sem("xg_turned"); xgT_ready = sem("xgT_ready")
        h_done = sem("h_done"); hb_ready = sem("hb_ready"); h_turned = sem("h_turned"); hT_ready = sem("hT_ready")
        o_done = sem("o_done"); og_ready = sem("og_ready"); og_stored = sem("og_stored")
        gathered = sem("gathered"); s_out = sem("s_out"); fin_ready = sem("fin_ready")

        s_w1 = sem("s_w1")
        z_ready = sem("z_ready"); g_ready = sem("g_ready"); x1_ready = sem("x1_ready")
        xsum_ready = sem("xsum_ready"); prep_ready = sem("prep_ready"); mask_ready = sem("mask_ready")
        xrep_ready = sem("xrep_ready"); xrep_used = sem("xrep_used")
        qtile_ready = sem("qtile_ready"); s_done = sem("s_done"); s_read = sem("s_read")
        vtile_ready = sem("vtile_ready"); sm_ready = sem("sm_ready"); p_ready = sem("p_ready"); p_turned = sem("p_turned"); pT_ready = sem("pT_ready")
        sigexp_ready = sem("sigexp_ready"); crs_ready = sem("crs_ready"); pv_done = sem("pv_done"); pv_read = sem("pv_read")
        loop_step = sem("loop_step"); o1_ready = sem("o1_ready")
        nx_ready = sem("nx_ready"); parts_ready = sem("parts_ready"); copies_ready = sem("copies_ready")
        cut_ready = sem("cut_ready")
        mx_filled = sem("mx_filled"); mx_read = sem("mx_read"); m_ready = sem("m_ready"); m_turned = sem("m_turned")
        tile_ready = sem("tile_ready"); q_turned = sem("q_turned"); qr_ready = sem("qr_ready")
        ph_ready = sem("ph_ready"); pl_ready = sem("pl_ready"); pl2_ready = sem("pl2_ready"); oT_ready = sem("oT_ready"); o_turned = sem("o_turned")
        mr_ready = sem("mr_ready"); st_filled = sem("st_filled"); p_whole = sem("p_whole"); pm_ready = sem("pm_ready"); pm_used = sem("pm_used")
        om_filled = sem("om_filled"); om_read = sem("om_read"); m_step = sem("m_step")
        rx_ready = sem("rx_ready"); rexp_ready = sem("rexp_ready"); comb_ready = sem("comb_ready")
        h13_filled = sem("h13_filled"); sg_ready = sem("sg_ready"); h1T_ready = sem("h1T_ready"); e_filled = sem("e_filled")
        e_read = sem("e_read"); acc_ready = sem("acc_ready"); g1_ready = sem("g1_ready")

        def bank(n):
            return ps[:, n, :]

        D_FILLS = dict(zip(
            ("xnT", "v", "mha", "yT", "logits", "ranks", "pv", "xn1T", "kcum", "q1", "k1", "vdup", "vsum",
             "o1T", "s1", "nxT", "qkv", "kaT", "omT", "mo", "nx2T", "lg1"),
            (a for a, _ in cuts([4, 4, 4, 4, 1, 1, NT, 4, 1, 4, 4, 8, 4, 4, 4, 4, 8, 4, 4, 4, 4, 1]))))
        A_FILLS = dict(proj=0, turn=12)

        rows = lambda r, n: r.unsqueeze(1).broadcast_to([P, n, D])

        block = ctx.enter_context(nc.Block())

        @block.sync
        def _(sp):
            sp.dma_start(x[:, :, :], A["x"].rearrange("(t p) d -> p t d", p=P)).then_inc(s_x, 16)
            sp.dma_start(w0[:, :], A["w0"]).then_inc(s_w0, 16)
            sp.dma_start(cols0[:, :], A["cols0"]).then_inc(s_w0, 16)
            sp.dma_start(wgT[:, :], A["wgT"]).then_inc(s_w0, 16)
            sp.dma_start(rows0[:, :], A["rows0"].partition_broadcast(P)).then_inc(s_rows0, 16)
            sp.wait_ge(s_zero, 1)
            sp.dma_start(slots_in.rearrange("(w p) d -> p w d", p=P),
                         zeros[:, :].unsqueeze(1).broadcast_to([P, WINDOWS, D])).then_inc(s_zeroed, 16)
            sp.dma_start(w1[:, :, :], A["w1"]).then_inc(s_wexp, 16)
            sp.dma_start(b1_col[:, :, :], A["b1"]).then_inc(s_wexp, 16)
            sp.dma_start(w2[:, :, :, :], A["w2"]).then_inc(s_wexp, 16)
            sp.dma_start(b2_row[:, :, :], A["b2"].partition_broadcast(P)).then_inc(s_wexp, 16)
            sp.dma_start(wl1[:, :], A["wl1"]).then_inc(s_w1, 16)
            sp.dma_start(rows1[:, :], A["rows1"].partition_broadcast(P)).then_inc(s_w1, 16)
            sp.dma_start(e13[:, :, :], A["e13"]).then_inc(s_w1, 16)
            sp.dma_start(e2[:, :, :], A["e2"]).then_inc(s_w1, 16)
            sp.wait_ge(scattered, 16 * NT)
            rin = slots_in.rearrange("(w p) d -> p w d", p=P)
            rout = slots_out.rearrange("(w p) d -> p w d", p=P)
            sp.dma_start(xg[:, :, :], rin[:, 0:GROUP, :]).then_inc(xg_loaded, 16)
            with sp.Fori(1, GROUPS) as i:
                sp.wait_ge(xg_turned, i)
                sp.dma_start(xg[:, :, :], rin[:, bass.ds(i * GROUP, GROUP), :]).then_inc(xg_loaded, 16)
                sp.wait_ge(og_ready, i * GROUP)
                sp.dma_start(rout[:, bass.ds((i - 1) * GROUP, GROUP), :], og[:, :, :]).then_inc(og_stored, 16)
            sp.wait_ge(og_ready, GROUPS * GROUP)
            sp.dma_start(rout[:, (GROUPS - 1) * GROUP:GROUPS * GROUP, :], og[:, :, :]).then_inc(og_stored, 16)
            sp.wait_ge(og_stored, 16 * GROUPS)
            sp.wait_ge(fin_ready, 1)
            sp.dma_start(out.rearrange("(t p) d -> p t d", p=P), y[:, :, :]).then_inc(s_out, 16)
            sp.wait_ge(s_out, 16)

        @block.gpsimd
        def _(pool):
            link = Link(pool, pool_step)
            pool.memset(zeros[:, :], 0.0).then_inc(s_zero, 1)
            link.mark(pool.memset(ident[:, :], 0.0))
            link.mark(pool.memset(before[:, :], 1.0))
            link.mark(pool.memset(causal[:, :], 0.0))
            link.mark(pool.memset(scanmask[:, :, :], 1.0))
            link(pool.memset(mhalf[:, :], -0.5))
            link.mark(pool.affine_select(out=ident[:, :], in_=ident[:, :], compare_op=ALU.not_equal, fill=1.0,
                                         base=0, pattern=[[-1, P]], channel_multiplier=1))
            link.mark(pool.affine_select(out=before[:, :], in_=before[:, :], compare_op=ALU.is_gt, fill=0.0,
                                         base=0, pattern=[[1, P]], channel_multiplier=-1))
            link.mark(pool.affine_select(out=causal[:, :], in_=causal[:, :], compare_op=ALU.is_ge, fill=NEG,
                                         base=0, pattern=[[-1, P]], channel_multiplier=1))
            link.mark(pool.memset(scanmask[:, :, 0:1], 0.0))
            link.mark(pool.iota(iota_e[:, :, :], pattern=[[1, E0], [0, NT]], base=0, channel_multiplier=0,
                                allow_small_or_imprecise_dtypes=True))
            link.mark(pool.iota(wstart[:, :, :], pattern=[[P, WINDOWS], [0, E0]], base=0, channel_multiplier=0,
                                allow_small_or_imprecise_dtypes=True))
            link(pool.memset(ones[:, :], 1.0))
            pool.sem_inc(s_const, 1)

            def inverse_deviation(n, eps):
                pool.wait_ge(var_ready, NT * (n + 1))
                link(pool.tensor_scalar(vare[:, :], mv[:, :, 1], eps, None, ALU.add))
                pool.tensor_tensor(rstd[:, :], vare[:, :], mhalf[:, :], ALU.pow).then_inc(rstd_ready, 1)

            def inverse_root(n, eps):
                pool.wait_ge(var_ready, NT * (n + 1))
                link(pool.tensor_tensor(msq[:, :], mv[:, :, 0], mv[:, :, 0], ALU.mult))
                link(pool.tensor_tensor(msq[:, :], msq[:, :], mv[:, :, 1], ALU.add))
                link(pool.tensor_scalar(vare[:, :], msq[:, :], eps, None, ALU.add))
                pool.tensor_tensor(rstd[:, :], vare[:, :], mhalf[:, :], ALU.pow).then_inc(rstd_ready, 1)

            inverse_deviation(0, 1e-5)
            inverse_deviation(1, 1e-5)
            pool.wait_ge(slot_ready, 1)
            pool.wait_ge(y_ready, NT)
            pool.wait_ge(s_zeroed, 16)
            for t in range(NT):
                pool.indirect_dma_start(out=slots_in[:, :], out_offset=bass.IndirectOffsetOnAxis(ap=slot[:, t:t + 1], axis=0),
                                        in_=y[:, t, :], in_offset=None).then_inc(scattered, 16)
            pool.wait_ge(og_stored, 16 * GROUPS)
            for t in range(NT):
                pool.indirect_dma_start(out=moe[:, t, :], out_offset=None, in_=slots_out[:, :],
                                        in_offset=bass.IndirectOffsetOnAxis(ap=slot[:, t:t + 1], axis=0)).then_inc(gathered, 16)
            inverse_deviation(2, 1e-5)

            pool.wait_ge(x1_ready, 1)
            link(pool.memset(amask[:, :], 0.0))
            link(pool.memset(mask4[:, :], 1.0))
            link(pool.memset(vmask[:, :], 1.0))
            link(pool.memset(vbd[:, :, :, :, :], 0.0))
            for c in range(2):
                v_ = amask[CS * c:CS * (c + 1), :]
                link(pool.affine_select(out=v_, in_=v_, compare_op=ALU.is_ge, fill=MASKED / SC1,
                                             base=0, pattern=[[-1, CS]], channel_multiplier=1))
            for g in range(D // 32):
                m_ = mask4[32 * g:32 * (g + 1), :]
                link(pool.affine_select(out=m_, in_=m_, compare_op=ALU.is_ge, fill=0.0,
                                        base=0, pattern=[[-D1, HG]], channel_multiplier=1))
                link(pool.affine_select(out=m_, in_=m_, compare_op=ALU.is_ge, fill=0.0,
                                             base=D1 - 1, pattern=[[D1, HG]], channel_multiplier=-1))
            for h in range(2):
                hv = vmask[CS * h:CS * (h + 1), :].rearrange("p (n two d) -> p n two d", two=2, d=D1)
                link(pool.memset(hv[:, :, 1 - h, :], 0.0))
                hb_ = vbd[CS * h:CS * (h + 1), :, :, :, 2 * D1 + h]
                link(pool.memset(hb_, 1.0))
            pool.sem_inc(mask_ready, 1)

            inverse_deviation(3, 1e-5)
            pool.wait_ge(prep_ready, 1)

            def tiles(i):
                if not isinstance(i, int):
                    pool.wait_ge(s_done, i)
                pool.tensor_copy(qtile[:, :], q1T[:, bass.ds(i * P, P)]).then_inc(qtile_ready, 1)
                pool.tensor_copy(ktile[:, :, :, :], k4[:, bass.ds(i * 2, 2), :, :]).then_inc(qtile_ready, 1)
                if not isinstance(i, int):
                    pool.wait_ge(pv_done, i)
                pool.tensor_copy(vtile[:, :, :, :].rearrange("p a b c -> p (a b c)"),
                                 vbd[:, bass.ds(i, 1), :, :, :].rearrange("p o a b c -> p (o a b c)")).then_inc(vtile_ready, 1)

            tiles(0)
            with pool.Fori(1, NT) as i:
                tiles(i)

            inverse_root(4, 1e-6)
            pool.wait_ge(cut_ready, 1)
            link(pool.memset(ka[:, :, R_ROWS:M_ROWS], 1.0))
            link(pool.memset(vr[:, :, DM:DM + 1].bitcast(F32), 1.0))
            link(pool.memset(vr[:, :, 2 * DM + 1:VW].bitcast(F32), 0.0))
            link(pool.memset(v1[:, :, DM:DM + 1], 1.0))
            pool.sem_inc(copies_ready, 1)

            def query_tile(i, parity, first=False):
                if not first:
                    pool.wait_ge(m_turned, i - 1)
                pool.tensor_copy(qtile2[:, parity, :, 0:R_ROWS], at(qa, i)).then_inc(tile_ready, 1)

            pool.wait_ge(copies_ready, 2)
            query_tile(0, 0, first=True)
            query_tile(1, 1, first=True)

            def shared_tile(i, parity, first=False, more=True):
                for t in CUT_P:
                    pool.wait_ge(ph_ready, i * len(CUT) + CUT.index(t) + 1)
                    pool.tensor_tensor(pl[:, t % RING, :], pm[:, t % RING, :], ph[:, t % RING, :].bitcast(F32),
                                       ALU.subtract).then_inc(pl2_ready, 1)
                if more:
                    query_tile(i + 2, parity)

            over_tiles(pool, shared_tile, 2)
            inverse_root(5, 1e-6)

        @block.vector
        def _(dve):
            link = Link(dve, dve_step)

            def normalise(n, src, dst, ready=None):
                for t in range(NT):
                    link.mark(dve.bn_stats(stats[:, t, :], src[:, t, :]))
                link.wait()
                for t in range(NT):
                    dve.bn_aggr(mv[:, t, :], stats[:, t, :]).then_inc(var_ready, 1)
                dve.wait_ge(var_ready, NT * (n + 1))
                dve.wait_ge(rstd_ready, n + 1)
                for t in range(NT):
                    ins = dve.tensor_scalar(dst[:, t, :], src[:, t, :], mv[:, t, 0:1], rstd[:, t:t + 1],
                                            ALU.subtract, ALU.mult)
                    if ready is None:
                        link.mark(ins)
                    else:
                        ins.then_inc(ready, 1)
                link.wait()

            def drain(k, dst, **kw):
                dve.wait_ge(d_filled, k + 1)
                dve.tensor_copy(dst, bank(k % 2)[:, 0:dst.free_size()] if len(dst.shape) == 2 else bank(k % 2)).then_inc(d_drained, 1)

            dve.wait_ge(s_x, 16)
            normalise(0, x, xn, xn_ready)
            for g in range(4):
                drain(D_FILLS["xnT"] + g, xnT[:, 512 * g:512 * (g + 1)])
            dve.wait_ge(s_rows0, 16)
            for g in range(4):
                k = D_FILLS["v"] + g
                dve.wait_ge(d_filled, k + 1)
                dve.tensor_tensor(v[:, 4 * g:4 * g + 4, :], bank(k % 2).rearrange("p (t d) -> p t d", t=4),
                                  rows(bv_row, 4), ALU.add).then_inc(d_drained, 1)
            link(dve.tensor_tensor(tmp[:, :, :], xn[:, :, :], rows(bo_row, NT), ALU.add))
            for g in range(4):
                k = D_FILLS["mha"] + g
                dve.wait_ge(d_filled, k + 1)
                dve.tensor_tensor(tmp[:, 4 * g:4 * g + 4, :], bank(k % 2).rearrange("p (t d) -> p t d", t=4),
                                  tmp[:, 4 * g:4 * g + 4, :], ALU.add).then_inc(d_drained, 1)
            dve.wait_ge(d_drained, D_FILLS["mha"] + 4)
            normalise(1, tmp, y)
            link(dve.tensor_tensor(y[:, :, :], y[:, :, :], rows(g1_row, NT), ALU.mult))
            dve.tensor_tensor(y[:, :, :], y[:, :, :], rows(be1_row, NT), ALU.add).then_inc(y_ready, NT)
            for g in range(4):
                drain(D_FILLS["yT"] + g, yT[:, 512 * g:512 * (g + 1)])
            k = D_FILLS["logits"]
            dve.wait_ge(d_filled, k + 1)
            dve.tensor_copy(lg[:, :, :], bank(k % 2)[:, 0:NT * E0].rearrange("p (t e) -> p t e", t=NT)).then_inc(d_drained, 1)
            dve.wait_ge(d_drained, k + 1)
            for t in range(NT):
                link.mark(dve.max(top[:, t, :], lg[:, t, :]))
            link.wait()
            for t in range(NT):
                link.mark(dve.max_index(topi[:, t, :], top[:, t, :], lg[:, t, :]))
            link.wait()
            link(dve.tensor_copy(expert[:, :], topi[:, :, 0]))
            dve.wait_ge(s_const, 1)
            dve.tensor_tensor(onehot[:, :, :], iota_e[:, :, :], expert[:, :].unsqueeze(1).broadcast_to([P, E0, NT]),
                              ALU.is_equal).then_inc(onehot_ready, 1)
            k = D_FILLS["ranks"]
            dve.wait_ge(d_filled, k + 1)
            in_tile = bank(k % 2)[:, 0:NT * E0].rearrange("p (e t) -> p e t", e=E0)
            of_tile = bank(k % 2)[:, NT * E0:2 * NT * E0].rearrange("p (e t) -> p e t", e=E0)
            fl = lambda a: a[:, :, :].rearrange("p e t -> p (e t)")
            link(dve.tensor_tensor_scan(fl(upto), fl(scanmask), bank(k % 2)[:, NT * E0:2 * NT * E0], 0.0, ALU.mult, ALU.add))
            link(dve.tensor_tensor(rank[:, :, :], upto[:, :, :], of_tile, ALU.subtract))
            link(dve.tensor_tensor(rank[:, :, :], rank[:, :, :], in_tile, ALU.add))
            dve.sem_inc(d_drained, 1)
            link(dve.tensor_scalar(cnt_i[:, :], upto[:, :, NT - 1], float(P - 1), None, ALU.add))
            sh = P.bit_length() - 1
            link(dve.tensor_scalar(cnt_i[:, :], cnt_i[:, :], sh, sh, ALU.logical_shift_right, ALU.logical_shift_left))
            link(dve.tensor_copy(pad[:, :], cnt_i[:, :]))
            link(dve.tensor_tensor_scan(end[:, :], ones[:, 0:E0], pad[:, :], 0.0, ALU.mult, ALU.add))
            link(dve.tensor_tensor(base[:, :], end[:, :], pad[:, :], ALU.subtract))
            link(dve.tensor_tensor(rank[:, :, :], rank[:, :, :], base[:, :].unsqueeze(2).broadcast_to([P, E0, NT]), ALU.add))
            link(dve.tensor_tensor(rank[:, :, :], rank[:, :, :], onehot[:, :, :], ALU.mult))
            link(dve.tensor_reduce(slot_f[:, :], rank[:, :, :].rearrange("p e t -> p t e"), AX.X, ALU.add))
            dve.tensor_copy(slot[:, :], slot_f[:, :]).then_inc(slot_ready, 1)
            link(dve.tensor_tensor(wcmp[:, :, :], end[:, :].unsqueeze(1).broadcast_to([P, WINDOWS, E0]), wstart[:, :, :], ALU.is_le))
            link(dve.tensor_reduce(wexp_f[:, :], wcmp[:, :, :], AX.X, ALU.add))
            dve.tensor_scalar(wexp[:, :], wexp_f[:, :], float(E0 - 1), None, ALU.min).then_inc(wexp_ready, 1)

            def row_max(i):
                dve.wait_ge(score_done, i + 1)
                diag = ps[:, 4 + i // 4, P * (i % 4):P * (i % 4 + 1)]
                link(dve.tensor_tensor(diag, diag, causal[:, :], ALU.add))
                n = (i + 1) * P
                s = ps[:, 4:8, :].rearrange("p b c -> p (b c)")[:, 0:n]
                link(dve.tensor_reduce(rmax[:, i:i + 1], s, AX.X, ALU.max))
                dve.tensor_scalar(nmax[:, i:i + 1], rmax[:, i:i + 1], -float(D) ** -0.5, None, ALU.mult).then_inc(nmax_ready, 1)

            def attention_out(i):
                k = D_FILLS["pv"] + i
                dve.wait_ge(prob_ready, i + 1)
                link(dve.reciprocal(rinv[:, i:i + 1], rsum[:, i:i + 1]))
                dve.wait_ge(d_filled, k + 1)
                dve.tensor_scalar(s0[:, i, :], bank(k % 2)[:, 0:D], rinv[:, i:i + 1], None, ALU.mult).then_inc(d_drained, 1)

            for i in range(NT + 1):
                if i < NT:
                    row_max(i)
                if i >= 1:
                    attention_out(i - 1)

            dve.wait_ge(s_wexp, 64)

            def mix(i, first=False):
                e = [dve.value_load(wexp[0:1, bass.ds(i * GROUP + b, 1)], min_val=0, max_val=E0 - 1) for b in range(GROUP)]
                dve.wait_ge(xg_turned, i + 1)
                dve.tensor_copy(xgT[:, :, :], bank(0).rearrange("p (b d) -> p b d", b=GROUP)).then_inc(xgT_ready, 1)
                for b in range(GROUP):
                    dve.wait_ge(h_turned, i * GROUP + b + 1)
                    for c in range(FC0):
                        ins = dve.tensor_scalar(hT[:, b, c * P:(c + 1) * P], bank(6 + b % 2)[:, c * P:(c + 1) * P],
                                                b1_col[:, e[b], c:c + 1], 0.0, ALU.add, ALU.max)
                    ins.then_inc(hT_ready, 1)
                if not first:
                    dve.wait_ge(og_stored, i * 16)
                for b in range(GROUP):
                    dve.wait_ge(o_done, i * GROUP + b + 1)
                    dve.tensor_tensor(og[:, b, :], bank(2 + b)[:, 0:D], b2_row[:, e[b], :], ALU.add).then_inc(og_ready, 1)

            mix(0, first=True)
            with dve.Fori(1, GROUPS) as i:
                mix(i)

            dve.wait_ge(gathered, 16 * NT)
            link(dve.tensor_tensor(moe[:, :, :], y[:, :, :], moe[:, :, :], ALU.add))
            normalise(2, moe, moe)
            link(dve.tensor_tensor(moe[:, :, :], moe[:, :, :], rows(g2_row, NT), ALU.mult))
            link(dve.tensor_tensor(moe[:, :, :], moe[:, :, :], rows(be2_row, NT), ALU.add))
            dve.sem_inc(z_ready, 1)
            dve.wait_ge(g_ready, 1)
            link(dve.tensor_tensor(moe[:, :, :], moe[:, :, :], s0[:, :, :], ALU.mult))
            dve.tensor_tensor(x[:, :, :], x[:, :, :], moe[:, :, :], ALU.add).then_inc(x1_ready, 1)
            dve.wait_ge(x1_ready, 1)

            normalise(3, x, xn, xn_ready)
            dve.wait_ge(xn_ready, 2 * NT)
            for g in range(4):
                drain(D_FILLS["xn1T"] + g, xnT[:, 512 * g:512 * (g + 1)])
            dve.wait_ge(d_drained, D_FILLS["xn1T"] + 4)
            link(dve.tensor_reduce(xsum[:, :], xnT[:, :].rearrange("p (c s) -> p c s", s=CS), AX.X, ALU.add))
            link(dve.tensor_scalar(xsum[:, :], xsum[:, :], 1.0 / CS, None, ALU.mult))
            link(dve.tensor_tensor_scan(xcum[:, :], ones[:, 0:NC], xsum[:, :], 0.0, ALU.mult, ALU.add))
            dve.tensor_tensor(xcum[:, :], xcum[:, :], xsum[:, :], ALU.subtract).then_inc(xsum_ready, 1)
            dve.wait_ge(mask_ready, 1)
            k = D_FILLS["kcum"]
            dve.wait_ge(d_filled, k + 1)
            dve.tensor_tensor(k4[:, :, :, CS], bank(k % 2)[:, 0:NC].unsqueeze(2).broadcast_to([P, NC, HG]),
                              mask4[:, :].unsqueeze(1).broadcast_to([P, NC, HG]), ALU.mult).then_inc(d_drained, 1)
            for g in range(4):
                drain(D_FILLS["q1"] + g, q1T[:, 512 * g:512 * (g + 1)])
            n = 512 // CS
            for g in range(4):
                k = D_FILLS["k1"] + g
                dve.wait_ge(d_filled, k + 1)
                dve.tensor_tensor(k4[:, n * g:n * (g + 1), :, 0:CS],
                                  bank(k % 2).rearrange("p (c s) -> p c s", s=CS).unsqueeze(2).broadcast_to([P, n, HG, CS]),
                                  mask4[:, :].unsqueeze(1).unsqueeze(3).broadcast_to([P, n, HG, CS]), ALU.mult).then_inc(d_drained, 1)
            dve.wait_ge(d_drained, D_FILLS["k1"] + 4)
            for g in range(8):
                k = D_FILLS["vdup"] + g
                dve.wait_ge(d_filled, k + 1)
                for c in range(4):
                    ins = dve.tensor_tensor(vbd[:, 2 * g + c // 2, c % 2, :, 0:2 * D1],
                                            bank(k % 2)[:, c * D:(c + 1) * D].rearrange("p (n d) -> p n d", d=2 * D1),
                                            vmask[:, :].rearrange("p (n d) -> p n d", d=2 * D1), ALU.mult)
                ins.then_inc(d_drained, 1)
            for g in range(4):
                k = D_FILLS["vsum"] + g
                drain(k, vsum[:, 4 * g:4 * g + 4, :].rearrange("p t d -> p (t d)"))
            dve.wait_ge(d_drained, D_FILLS["vsum"] + 4)
            link.wait()
            dve.sem_inc(prep_ready, 1)

            sv = ps[:, 4:8, :]

            STEPS = 7

            def chunk_scores(i):
                dve.wait_ge(s_done, i + 1)
                if not isinstance(i, int) or i > 0:
                    dve.wait_ge(sigexp_ready, i)
                dve.tensor_copy(crs[:, :].rearrange("p (g h) -> p g h", g=4),
                                sv[:, :, 0:HG * (CS + 1)].rearrange("p g (h s) -> p g h s", h=HG)[:, :, :, CS]).then_inc(crs_ready, 1)
                if not isinstance(i, int) or i > 0:
                    dve.wait_ge(p_ready, i)
                for g in range(4):
                    ins = dve.tensor_tensor(sm[:, HG * g:HG * (g + 1), :], sv[:, g, 0:HG * (CS + 1)].rearrange("p (h s) -> p h s", h=HG)[:, :, 0:CS],
                                            amask[:, :].unsqueeze(1).broadcast_to([P, HG, CS]), ALU.add)
                ins.then_inc(s_read, 1)
                dve.wait_ge(s_read, i + 1)
                dve.tensor_reduce(mx1[:, :], sm[:, :, :], AX.X, ALU.max).then_inc(loop_step, 1)
                dve.wait_ge(loop_step, i * STEPS + 1)
                dve.tensor_tensor(sm[:, :, :], sm[:, :, :], mx1[:, :].unsqueeze(2).broadcast_to([P, H1, CS]), ALU.subtract).then_inc(sm_ready, 1)
                dve.wait_ge(sigexp_ready, i + 1)
                dve.tensor_scalar(sig[:, :], sig[:, :], 2.0, 2.0, ALU.mult, ALU.add).then_inc(loop_step, 1)
                dve.wait_ge(loop_step, i * STEPS + 2)
                dve.reciprocal(sig[:, :], sig[:, :]).then_inc(loop_step, 1)
                dve.wait_ge(loop_step, i * STEPS + 3)
                dve.tensor_tensor(cvx[:, :].rearrange("p (h d) -> p h d", d=D1), vsum[:, i, :].rearrange("p (h d) -> p h d", d=D1) if isinstance(i, int) else vsum[:, bass.ds(i, 1), :].rearrange("p o (h d) -> p (o h) d", d=D1),
                                  sig[:, :].unsqueeze(2).broadcast_to([P, H1, D1]), ALU.mult).then_inc(loop_step, 1)

            def chunk_out(i):
                dve.wait_ge(pv_done, i + 1)
                pv = bank(1)[:, 0:(H1 // 2) * (2 * D1 + 2)].rearrange("p (n c) -> p n c", n=H1 // 2)
                dve.reciprocal(rs1[:, :].rearrange("p (n c) -> p n c", c=2), pv[:, :, 2 * D1:2 * D1 + 2]).then_inc(loop_step, 1)
                dve.wait_ge(loop_step, i * STEPS + 5)
                ot = o1[:, i, :] if isinstance(i, int) else o1[:, bass.ds(i, 1), :].rearrange("p o d -> p (o d)")
                o_ = ot.rearrange("p (n c d) -> p n c d", c=2, d=D1)
                dve.tensor_tensor(o_, pv[:, :, 0:2 * D1].rearrange("p n (c d) -> p n c d", c=2),
                                  rs1[:, :].rearrange("p (n c) -> p n c", c=2).unsqueeze(3).broadcast_to([P, H1 // 2, 2, D1]), ALU.mult).then_inc(loop_step, 1)
                dve.wait_ge(loop_step, i * STEPS + 6)
                dve.sem_inc(pv_read, 1)
                dve.tensor_tensor(ot, ot, cvx[:, :], ALU.add).then_inc(loop_step, 1)
                dve.wait_ge(loop_step, i * STEPS + 7)

            chunk_scores(0)
            chunk_out(0)
            with dve.Fori(1, NT) as i:
                chunk_scores(i)
                chunk_out(i)
            dve.sem_inc(o1_ready, 1)
            for g in range(4):
                drain(D_FILLS["o1T"] + g, q1T[:, 512 * g:512 * (g + 1)])
            for g in range(4):
                drain(D_FILLS["s1"] + g, s0[:, 4 * g:4 * g + 4, :].rearrange("p t d -> p (t d)"))
            dve.wait_ge(d_drained, D_FILLS["s1"] + 4)

            def root_mean_square(n, src, dst, g_row, ready):
                for t in range(NT):
                    link.mark(dve.bn_stats(stats[:, t, :], src[:, t, :]))
                link.wait()
                for t in range(NT):
                    dve.bn_aggr(mv[:, t, :], stats[:, t, :]).then_inc(var_ready, 1)
                dve.wait_ge(rstd_ready, n + 1)
                for t in range(NT):
                    dve.scalar_tensor_tensor(out=dst[:, t, :], in0=src[:, t, :], scalar=rstd[:, t:t + 1], in1=g_row,
                                             op0=ALU.mult, op1=ALU.mult).then_inc(ready, 1)

            root_mean_square(4, xn, y, rg1_row, nx_ready)
            nxT = xnT
            for g in range(4):
                drain(D_FILLS["nxT"] + g, nxT[:, 512 * g:512 * (g + 1)])
            W3 = D + 2 * DM
            for g in range(8):
                k = D_FILLS["qkv"] + g
                dve.wait_ge(d_filled, k + 1)
                dve.tensor_copy(qkv[:, 2 * g:2 * g + 2, :], bank(k % 2)[:, 0:2 * W3].rearrange("p (t c) -> p t c", t=2)).then_inc(d_drained, 1)
            dve.wait_ge(d_drained, D_FILLS["qkv"] + 8)
            dve.sem_inc(cut_ready, 1)
            qv = qkv[:, :, 0:D].rearrange("p t (h d) -> p t h d", h=HM)
            kv = qkv[:, :, D:D + DM]
            vv = qkv[:, :, D + DM:W3]
            link.mark(dve.tensor_copy(ka[:, :, 0:DM].bitcast(F32R), kv))
            link.mark(dve.tensor_copy(vr[:, :, 0:DM], vv))
            link.mark(dve.tensor_copy(v1[:, :, 0:DM], vv))
            link(dve.tensor_copy(qa[:, :, :, 0:DM].bitcast(F32R), qv))
            link.mark(dve.tensor_tensor(ka[:, :, DM:2 * DM].bitcast(F32R), kv, ka[:, :, 0:DM], ALU.subtract))
            link.mark(dve.tensor_tensor(vr[:, :, DM + 1:2 * DM + 1], vv, vr[:, :, 0:DM].bitcast(F32), ALU.subtract))
            link(dve.tensor_tensor(qa[:, :, :, 2 * DM:3 * DM].bitcast(F32R), qv, qa[:, :, :, 0:DM], ALU.subtract))
            dve.sem_inc(parts_ready, 1)
            for g in range(4):
                k = D_FILLS["kaT"] + g
                dve.wait_ge(d_filled, k + 1)
                dve.tensor_copy(kr[0:M_ROWS, 512 * g:512 * (g + 1)], bank(k % 2)[0:M_ROWS, :]).then_inc(d_drained, 1)

            MSTEPS = 3

            def maximum(i, u):
                dve.wait_ge(mx_filled, i * MU + u + 1)
                dve.tensor_reduce(mxp[:, u // HM, u % HM:u % HM + 1], bank(u % 2), AX.X, ALU.max).then_inc(mx_read, 1)

            def cut_maximum(i, parity):
                high, low = (qtile2[:, parity, :, R_ROWS + n] for n in range(2))
                dve.wait_ge(mx_read, i * MU + MU)
                dve.wait_ge(tile_ready, i + 1)
                dve.tensor_reduce(negm[:, :], mxp[:, :, :], AX.X, ALU.max, negate=True).then_inc(m_step, 1)
                dve.wait_ge(m_step, i * MSTEPS + 1)
                dve.tensor_copy(high.bitcast(F32R), negm[:, :]).then_inc(m_step, 1)
                dve.wait_ge(m_step, i * MSTEPS + 2)
                dve.tensor_tensor(low.bitcast(F32R), negm[:, :], high, ALU.subtract).then_inc(m_step, 1)

            def low_parts(i, t):
                dve.wait_ge(ph_ready, i * len(CUT) + CUT.index(t) + 1)
                dve.tensor_tensor(pl[:, t % RING, :], pm[:, t % RING, :], ph[:, t % RING, :].bitcast(F32),
                                  ALU.subtract).then_inc(pl_ready, 1)

            OSTEPS = 4

            def shared_out(i):
                dve.wait_ge(o_turned, i + 1)
                o4 = bank(7)[:, 0:HM * VW].rearrange("p (h c) -> p h c", h=HM)
                dve.reciprocal(rsm[:, :], o4[:, :, DM]).then_inc(om_read, 1)
                dve.tensor_copy(ol[:, :, :], o4[:, :, DM + 1:2 * DM + 1]).then_inc(om_read, 1)
                dve.wait_ge(om_read, OSTEPS * i + 2)
                dve.tensor_tensor(ol[:, :, :], ol[:, :, :], o4[:, :, 0:DM], ALU.add).then_inc(om_read, 1)
                dve.wait_ge(om_read, OSTEPS * i + 3)
                dst = at(om, i).rearrange("p (h d) -> p h d", h=HM)
                dve.tensor_tensor(dst, ol[:, :, :], rsm[:, :].unsqueeze(2).broadcast_to([P, HM, DM]), ALU.mult).then_inc(om_read, 1)

            dve.wait_ge(copies_ready, 2)
            for u in range(MU):
                maximum(0, u)
            cut_maximum(0, 0)

            def shared_tile(i, parity, first=False, more=True):
                for t in range(NT):
                    if more:
                        for u in range(MU):
                            if MAX_SLOTS[u] == t:
                                maximum(i + 1, u)
                        if t == MAX_SLOTS[-1]:
                            cut_maximum(i + 1, 1 - parity)
                    if t == LAG + 1 and not first:
                        shared_out(i - 1)
                    if t in CUT_D:
                        low_parts(i, t)

            over_tiles(dve, shared_tile, 1)
            shared_out(NT - 1)
            dve.wait_ge(om_read, OSTEPS * NT)

            for g in range(4):
                drain(D_FILLS["omT"] + g, xnT[:, 512 * g:512 * (g + 1)])
            for g in range(4):
                k = D_FILLS["mo"] + g
                dve.wait_ge(d_filled, k + 1)
                dve.tensor_tensor(xn[:, 4 * g:4 * g + 4, :], bank(k % 2).rearrange("p (t d) -> p t d", t=4),
                                  xn[:, 4 * g:4 * g + 4, :], ALU.add).then_inc(d_drained, 1)
            dve.wait_ge(d_drained, D_FILLS["mo"] + 4)
            nx2 = om
            root_mean_square(5, xn, nx2, rg2_row, nx_ready)
            for g in range(4):
                drain(D_FILLS["nx2T"] + g, xnT[:, 512 * g:512 * (g + 1)])
            k = D_FILLS["lg1"]
            dve.wait_ge(d_filled, k + 1)
            dve.tensor_tensor(lg1[:, :, :], bank(k % 2)[:, 0:NT * E1].rearrange("p (t e) -> p t e", t=NT),
                              eb_row.unsqueeze(1).broadcast_to([P, NT, E1]), ALU.add).then_inc(d_drained, 1)
            dve.wait_ge(d_drained, k + 1)
            wide = lambda a: a.unsqueeze(2).broadcast_to([P, NT, E1])
            link(dve.tensor_reduce(mrow[:, :], lg1[:, :, :], AX.X, ALU.max))
            dve.tensor_tensor(lg1[:, :, :], lg1[:, :, :], wide(mrow[:, :]), ALU.subtract).then_inc(rx_ready, 1)
            dve.wait_ge(rexp_ready, 1)
            link(dve.tensor_reduce(mrow[:, :], rw[:, :, :], AX.X, ALU.add))
            link(dve.reciprocal(mrow[:, :], mrow[:, :]))
            link(dve.tensor_tensor(rw[:, :, :], rw[:, :, :], wide(mrow[:, :]), ALU.mult))
            for t in range(NT):
                link.mark(dve.max(top1[:, t, :], rw[:, t, :]))
            link.wait()
            for t in range(NT):
                link.mark(dve.max_index(topi1[:, t, :], top1[:, t, :], rw[:, t, :]))
            link.wait()
            dve.tensor_tensor(w12[:, 1, :], top1[:, :, 1], top1[:, :, 0], ALU.subtract).then_inc(rx_ready, 1)
            link.mark(dve.tensor_copy(ix12[:, 0, :], topi1[:, :, 0]))
            link(dve.tensor_copy(ix12[:, 1, :], topi1[:, :, 1]))
            for e in range(E1):
                link.mark(dve.memset(iota1[:, :, e], float(e)))
            link.mark(dve.memset(comb[:, :, E1:ES], 1.0))
            dve.wait_ge(rexp_ready, 2)
            link(dve.tensor_scalar(w12[:, 0, :], w12[:, 1, :], 1.0, None, ALU.add))
            link(dve.reciprocal(w12[:, 0, :], w12[:, 0, :]))
            link(dve.tensor_tensor(w12[:, 1, :], w12[:, 1, :], w12[:, 0, :], ALU.mult))
            link.mark(dve.tensor_tensor(comb[:, :, 0:E1], iota1[:, :, :], wide(ix12[:, 0, :]), ALU.is_equal))
            link(dve.tensor_tensor(ctmp[:, :, :], iota1[:, :, :], wide(ix12[:, 1, :]), ALU.is_equal))
            link.mark(dve.tensor_tensor(comb[:, :, 0:E1], comb[:, :, 0:E1], wide(w12[:, 0, :]), ALU.mult))
            link(dve.tensor_tensor(ctmp[:, :, :], ctmp[:, :, :], wide(w12[:, 1, :]), ALU.mult))
            link(dve.tensor_tensor(comb[:, :, 0:E1], comb[:, :, 0:E1], ctmp[:, :, :], ALU.add))

            def expert_rows(j, e):
                n_ = j * ES + e
                dve.wait_ge(sg_ready, n_ + 1)
                if e >= 2 or not isinstance(j, int):
                    dve.wait_ge(e_filled, n_ - 1 + (e == 0))
                dve.tensor_tensor(h1T[:, e % 2, :], sg[:, e % 2, :], bank(2 * (e % 2) + 1), ALU.mult).then_inc(h1T_ready, 1)

            def add_expert(j, e):
                n_ = j * ES + e
                dve.wait_ge(e_filled, n_ + 1)
                q_ = CH // P
                for t in range(q_):
                    a_ = (xn[:, j * q_ + t, :] if isinstance(j, int) else xn[:, bass.ds(j * q_ + t, 1), :].rearrange("p o d -> p (o d)"))
                    c_ = (comb[:, j * q_ + t, e:e + 1] if isinstance(j, int) else comb[:, bass.ds(j * q_ + t, 1), e])
                    if e > 0:
                        dve.wait_ge(e_read, (n_ - 1) * q_ + t + 1)
                    dve.scalar_tensor_tensor(out=a_, in0=bank(4 + e % 2)[:, t * P:(t + 1) * P], scalar=c_, in1=a_,
                                             op0=ALU.mult, op1=ALU.add).then_inc(e_read, 1)

            def mixture(j):
                for e in range(ES + 1):
                    if e < ES:
                        expert_rows(j, e)
                    if e >= 1:
                        add_expert(j, e - 1)

            mixture(0)
            with dve.Fori(1, NCH) as j:
                mixture(j)
            dve.wait_ge(e_read, NT * ES)
            dve.sem_inc(acc_ready, 1)
            dve.wait_ge(g1_ready, 1)
            link(dve.tensor_tensor(y[:, :, :], y[:, :, :], s0[:, :, :], ALU.mult))
            dve.tensor_tensor(y[:, :, :], y[:, :, :], x[:, :, :], ALU.add).then_inc(fin_ready, 1)

        @block.scalar
        def _(act):
            act.wait_ge(s_w0, 48)
            dst = [vfT, kT, qT]
            for n in range(3):
                for g in range(4):
                    k = A_FILLS["proj"] + 4 * n + g
                    act.wait_ge(a_filled, k + 1)
                    act.activation(dst[n][:, 512 * g:512 * (g + 1)], bank(2 + k % 2), ACT.Identity,
                                   bias=cols0[:, n:n + 1], scale=1.0).then_inc(a_drained, 1)

            def exponents(i):
                act.wait_ge(nmax_ready, i + 1)
                n = (i + 1) * P
                s = ps[:, 4:8, :].rearrange("p b c -> p (b c)")[:, 0:n]
                if i >= 2:
                    act.wait_ge(d_filled, D_FILLS["pv"] + i - 1)
                act.activation(prob[:, i % 2, 0:n], s, ACT.Exp, bias=nmax[:, i:i + 1], scale=float(D) ** -0.5,
                               accum_out=rsum[:, i:i + 1]).then_inc(prob_ready, 1)

            turn = [A_FILLS["turn"]]

            def turned(i):
                for b in range(0, i + 1, 4):
                    k = turn[0]
                    n = min(4, i + 1 - b) * P
                    act.wait_ge(a_filled, k + 1)
                    act.activation(probT[:, k % 2, 0:n], bank(2 + k % 2)[:, 0:n], ACT.Copy).then_inc(a_drained, 1)
                    turn[0] += 1

            for i in range(NT + 1):
                if i < NT:
                    exponents(i)
                if i >= 1:
                    turned(i - 1)

            with act.Fori(0, GROUPS) as i:
                for b in range(GROUP):
                    act.wait_ge(h_done, i * GROUP + b + 1)
                    act.activation(hb[:, b, :], bank(2 + b), ACT.Copy).then_inc(hb_ready, 1)

            act.wait_ge(z_ready, 1)
            act.activation(moe[:, :, :], moe[:, :, :], ACT.Silu).then_inc(g_ready, 1)

            act.wait_ge(xsum_ready, 1)
            step = [0]
            for t in range(NT):
                if t >= 2:
                    act.wait_ge(xrep_used, t - 1)
                for c in range(2):
                    src = xnT[:, t * P + c * CS:t * P + (c + 1) * CS].unsqueeze(1).broadcast_to([P, 2, CS])
                    act.activation(xrep[:, t % 2, c, :].rearrange("p (r s) -> p r s", r=2), src, ACT.Copy).then_inc(xrep_ready, 1)
            for t in range(NT):
                act.wait_ge(xrep_used, NT + t - 1)
                src = xcum[:, 2 * t:2 * t + 2].unsqueeze(2).broadcast_to([P, 2, CS])
                act.activation(xrep[:, t % 2, 0, :].rearrange("p (r s) -> p r s", r=2), src, ACT.Copy).then_inc(xrep_ready, 1)

            def chunk_exponents(i):
                act.wait_ge(crs_ready, i + 1)
                if not isinstance(i, int):
                    act.wait_ge(loop_step, i * 7)
                act.activation(sig[:, :], crs[:, :], ACT.Exp, scale=-SC1).then_inc(sigexp_ready, 1)
                act.wait_ge(sm_ready, i + 1)
                if not isinstance(i, int):
                    act.wait_ge(p_turned, i)
                act.activation(pe1[:, :, :], sm[:, :, :], ACT.Exp, scale=SC1).then_inc(p_ready, 1)
                act.wait_ge(p_turned, i + 1)
                if not isinstance(i, int):
                    act.wait_ge(pv_done, i)
                act.activation(p1T[:, :, :], ps[:, 2:4, :].rearrange("p b (n c) -> p (b n) c", c=P), ACT.Copy).then_inc(pT_ready, 1)

            chunk_exponents(0)
            with act.Fori(1, NT) as i:
                chunk_exponents(i)

            act.wait_ge(parts_ready, 1)
            act.activation(ka[:, :, 2 * DM:3 * DM], ka[:, :, 0:DM], ACT.Copy).then_inc(act_step, 1)
            act.activation(qa[:, :, :, DM:2 * DM], qa[:, :, :, 0:DM], ACT.Copy).then_inc(act_step, 1)
            act.wait_ge(act_step, 2)
            act.sem_inc(copies_ready, 1)

            def queries(i, parity):
                act.wait_ge(q_turned, i + 1)
                act.activation(qr[0:R_ROWS, parity, :], bank(7)[0:R_ROWS, :], ACT.Copy).then_inc(qr_ready, 1)

            def maxima(i, parity):
                act.wait_ge(m_turned, i + 1)
                act.activation(qr[R_ROWS:M_ROWS, parity, :], bank(7)[R_ROWS:M_ROWS, :], ACT.Copy).then_inc(mr_ready, 1)

            def probabilities(i, t, first):
                act.wait_ge(st_filled, i * NT + t + 1)
                if not (first and t < RING):
                    act.wait_ge(pm_used, i * NT + t - RING + 1)
                act.activation(pm[:, t % RING, :], bank(2 + t % RING), ACT.Exp, scale=SCM).then_inc(p_whole, 1)
                if t in CUT:
                    act.wait_ge(p_whole, i * NT + t + 1)
                    act.activation(ph[:, t % RING, :], bank(2 + t % RING), ACT.Exp, scale=SCM).then_inc(ph_ready, 1)

            def sums(i):
                act.wait_ge(pm_used, i * NT + NT)
                if not isinstance(i, int) or i > 0:
                    act.wait_ge(o_turned, i)
                act.activation(oT[0:VW, :], bank(6)[0:VW, :], ACT.Copy).then_inc(oT_ready, 1)

            queries(0, 0)
            maxima(0, 0)

            def shared_tile(i, parity, first=False, more=True):
                for t in range(NT):
                    probabilities(i, t, first)
                    if t == 0 and more:
                        queries(i + 1, 1 - parity)
                    if t == LAG - 1 and not first:
                        sums(i - 1)
                    if t == TURN_SLOT and more:
                        maxima(i + 1, 1 - parity)

            over_tiles(act, shared_tile, 1)
            sums(NT - 1)

            act.wait_ge(rx_ready, 1)
            act.activation(rw[:, :, :], lg1[:, :, :], ACT.Exp).then_inc(rexp_ready, 1)
            act.wait_ge(rx_ready, 2)
            act.activation(w12[:, 1, :], w12[:, 1, :], ACT.Exp).then_inc(rexp_ready, 1)

            def gates(j):
                for e in range(ES):
                    n_ = j * ES + e
                    act.wait_ge(h13_filled, n_ + 1)
                    if e >= 2 or not isinstance(j, int):
                        act.wait_ge(h1T_ready, n_ - 1 + (e == 0))
                    act.activation(sg[:, e % 2, :], bank(2 * (e % 2)), ACT.Silu).then_inc(sg_ready, 1)

            gates(0)
            with act.Fori(1, NCH) as j:
                gates(j)
            act.wait_ge(acc_ready, 1)
            act.activation(y[:, :, :], xn[:, :, :], ACT.Silu).then_inc(g1_ready, 1)

        @block.tensor
        def _(pe):
            def d_fill(k):
                if k >= 2:
                    pe.wait_ge(d_drained, k - 1)
                return bank(k % 2)

            def a_fill(k):
                if k >= 2:
                    pe.wait_ge(a_drained, k - 1)
                return bank(2 + k % 2)

            pe.wait_ge(s_const, 1)

            def turn(k0, src, ready):
                for g in range(4):
                    o = d_fill(k0 + g)
                    for t in range(4 * g, 4 * g + 4):
                        if ready is not None:
                            pe.wait_ge(ready, t + 1)
                        ins = pe.transpose(o[:, P * (t % 4):P * (t % 4 + 1)], src[:, t, :], ident[:, :])
                    ins.then_inc(d_filled, 1)

            turn(D_FILLS["xnT"], xn, xn_ready)
            pe.wait_ge(s_w0, 48)
            W = dict(q=w0[:, 0:D], k=w0[:, D:2 * D], v=w0[:, 2 * D:3 * D], vf=w0[:, 3 * D:4 * D], o=w0[:, 4 * D:5 * D])
            for g in range(4):
                pe.wait_ge(d_drained, D_FILLS["xnT"] + g + 1)
                pe.matmul(a_fill(g), W["vf"], xnT[:, 512 * g:512 * (g + 1)], start=True, stop=True).then_inc(a_filled, 1)
            for g in range(4):
                o = d_fill(D_FILLS["v"] + g)
                for t in range(4 * g, 4 * g + 4):
                    ins = pe.matmul(o[:, P * (t % 4):P * (t % 4 + 1)], xnT[:, P * t:P * (t + 1)], W["v"], start=True, stop=True)
                ins.then_inc(d_filled, 1)
            for g in range(4):
                o = d_fill(D_FILLS["mha"] + g)
                pe.wait_ge(a_drained, g + 1)
                for t in range(4 * g, 4 * g + 4):
                    ins = pe.matmul(o[:, P * (t % 4):P * (t % 4 + 1)], vfT[:, P * t:P * (t + 1)], W["o"], start=True, stop=True)
                ins.then_inc(d_filled, 1)
            for g in range(4):
                pe.matmul(a_fill(4 + g), W["k"], xnT[:, 512 * g:512 * (g + 1)], start=True, stop=True).then_inc(a_filled, 1)
            pe.wait_ge(y_ready, NT)
            turn(D_FILLS["yT"], y, None)
            o = d_fill(D_FILLS["logits"])
            pe.wait_ge(d_drained, D_FILLS["yT"] + 4)
            for t in range(NT):
                ins = pe.matmul(o[:, E0 * t:E0 * (t + 1)], yT[:, P * t:P * (t + 1)], wgT[:, :], start=True, stop=True)
            ins.then_inc(d_filled, 1)
            pe.wait_ge(d_filled, D_FILLS["logits"] + 1)
            for g in range(4):
                pe.matmul(a_fill(8 + g), W["q"], xnT[:, 512 * g:512 * (g + 1)], start=True, stop=True).then_inc(a_filled, 1)
            pe.wait_ge(onehot_ready, 1)
            o = d_fill(D_FILLS["ranks"])
            oh = onehot[:, :, :].rearrange("p e t -> p (e t)")
            pe.matmul(o[:, 0:NT * E0], before[:, :], oh, start=True, stop=True)
            pe.matmul(o[:, NT * E0:2 * NT * E0], ones[:, :], oh, start=True, stop=True).then_inc(d_filled, 1)

            pe.wait_ge(a_drained, A_FILLS["turn"])
            turns = [A_FILLS["turn"]]

            def scores(i):
                n = (i + 1) * P
                if i >= 1:
                    pe.wait_ge(prob_ready, i)
                for c in range(0, n, 512):
                    m = min(512, n - c)
                    ins = pe.matmul(ps[:, 4 + c // 512, 0:m], qT[:, P * i:P * (i + 1)], kT[:, c:c + m], start=True, stop=True)
                ins.then_inc(score_done, 1)

            def turn_probs(i, b):
                k = turns[0]
                o = a_fill(k)
                if b == 0:
                    pe.wait_ge(prob_ready, i + 1)
                for j in range(b, min(b + 4, i + 1)):
                    ins = pe.transpose(o[:, P * (j - b):P * (j - b + 1)], prob[:, i % 2, P * j:P * (j + 1)], ident[:, :])
                ins.then_inc(a_filled, 1)
                turns[0] += 1
                return k

            def weigh(i, b, k, o):
                pe.wait_ge(a_drained, k + 1)
                for j in range(b, min(b + 4, i + 1)):
                    ins = pe.matmul(o[:, 0:D], probT[:, k % 2, P * (j - b):P * (j - b + 1)], v[:, j, :],
                                    start=(j == 0), stop=(j == i))
                if b + 4 > i:
                    ins.then_inc(d_filled, 1)

            def values(i):
                o = d_fill(D_FILLS["pv"] + i)
                last = None
                for b in range(0, i + 1, 4):
                    k = turn_probs(i, b)
                    if last is not None:
                        weigh(i, *last, o)
                    last = (b, k)
                weigh(i, *last, o)

            for i in range(NT + 1):
                if i < NT:
                    scores(i)
                if i >= 1:
                    values(i - 1)

            pe.wait_ge(wexp_ready, 1)
            pe.wait_ge(s_wexp, 64)
            pe.wait_ge(d_drained, D_FILLS["pv"] + NT)
            pe.wait_ge(prob_ready, NT)

            def mix(i, first=False):
                e = [pe.value_load(wexp[0:1, bass.ds(i * GROUP + b, 1)], min_val=0, max_val=E0 - 1) for b in range(GROUP)]
                pe.wait_ge(xg_loaded, i * 16 + 16)
                for b in range(GROUP):
                    ins = pe.transpose(bank(0)[:, b * D:(b + 1) * D], xg[:, b, :], ident[:, :])
                ins.then_inc(xg_turned, 1)
                pe.wait_ge(xgT_ready, i + 1)
                for b in range(GROUP):
                    if not first:
                        pe.wait_ge(og_ready, i * GROUP + b - GROUP + 1)
                    pe.matmul(bank(2 + b), xgT[:, b, :], w1[:, e[b], :], start=True, stop=True).then_inc(h_done, 1)
                for b in range(GROUP):
                    pe.wait_ge(hb_ready, i * GROUP + b + 1)
                    if b >= 2:
                        pe.wait_ge(hT_ready, i * GROUP + b - 1)
                    for c in range(FC0):
                        ins = pe.transpose(bank(6 + b % 2)[:, c * P:(c + 1) * P], hb[:, b, c * P:(c + 1) * P], ident[:, :])
                    ins.then_inc(h_turned, 1)
                for b in range(GROUP):
                    pe.wait_ge(hT_ready, i * GROUP + b + 1)
                    for c in range(FC0):
                        ins = pe.matmul(bank(2 + b)[:, 0:D], hT[:, b, c * P:(c + 1) * P], w2[:, e[b], c, :],
                                        start=(c == 0), stop=(c == FC0 - 1))
                    ins.then_inc(o_done, 1)

            mix(0, first=True)
            with pe.Fori(1, GROUPS) as i:
                mix(i)



            pe.wait_ge(s_w1, 64)

            def turn1(k0, src, ready, first):
                for g in range(4):
                    o = d_fill(k0 + g)
                    for t in range(4 * g, 4 * g + 4):
                        if ready is not None:
                            pe.wait_ge(ready, first + t + 1)
                        ins = pe.transpose(o[:, P * (t % 4):P * (t % 4 + 1)], src[:, t, :], ident[:, :])
                    ins.then_inc(d_filled, 1)

            turn1(D_FILLS["xn1T"], xn, xn_ready, NT)
            pe.wait_ge(xsum_ready, 1)
            o = d_fill(D_FILLS["kcum"])
            pe.matmul(o[:, 0:NC], wk1, xcum[:, :], start=True, stop=True).then_inc(d_filled, 1)
            for name, w in (("q1", wq1), ("k1", wk1)):
                for g in range(4):
                    pe.matmul(d_fill(D_FILLS[name] + g), w, xnT[:, 512 * g:512 * (g + 1)], start=True, stop=True).then_inc(d_filled, 1)
            for g in range(8):
                o = d_fill(D_FILLS["vdup"] + g)
                for t in (2 * g, 2 * g + 1):
                    for c in range(2):
                        pe.wait_ge(xrep_ready, 2 * t + c + 1)
                        n = 2 * (t % 2) + c
                        ins = pe.matmul(o[:, n * D:(n + 1) * D], xrep[:, t % 2, c, :], wv1, start=True, stop=True)
                        if n < 3 and c == 1:
                            ins.then_inc(xrep_used, 1)
                ins.then_inc(d_filled, 1)
                pe.wait_ge(d_filled, D_FILLS["vdup"] + g + 1)
                pe.sem_inc(xrep_used, 1)
            for g in range(4):
                o = d_fill(D_FILLS["vsum"] + g)
                for t in range(4 * g, 4 * g + 4):
                    pe.wait_ge(xrep_ready, 2 * NT + t + 1)
                    ins = pe.matmul(o[:, P * (t % 4):P * (t % 4 + 1)], xrep[:, t % 2, 0, :], wv1, start=True, stop=True)
                    if t % 4 < 3:
                        ins.then_inc(xrep_used, 1)
                ins.then_inc(d_filled, 1)
                pe.wait_ge(d_filled, D_FILLS["vsum"] + g + 1)
                pe.sem_inc(xrep_used, 1)
            pe.wait_ge(prep_ready, 1)

            def chunk_products(i):
                pe.wait_ge(qtile_ready, i * 2 + 2)
                if not isinstance(i, int):
                    pe.wait_ge(s_read, i)
                for c in range(2):
                    for g in range(D // 32):
                        r = slice(32 * g, 32 * (g + 1))
                        kk = ktile[r, c, :, :].rearrange("p h s -> p (h s)")
                        ins = pe.matmul(ps[CS * c:CS * (c + 1), 4 + g, 0:HG * (CS + 1)], qtile[r, CS * c:CS * (c + 1)], kk,
                                        start=True, stop=True)
                ins.then_inc(s_done, 1)
                pe.wait_ge(p_ready, i + 1)
                if not isinstance(i, int):
                    pe.wait_ge(pT_ready, i)
                flat = pe1[:, :, :].rearrange("p h s -> p (h s)")
                for n in range(H1 // 2):
                    ins = pe.transpose(ps[:, 2 + n // 4, P * (n % 4):P * (n % 4 + 1)], flat[:, P * n:P * (n + 1)], ident[:, :])
                ins.then_inc(p_turned, 1)
                pe.wait_ge(pT_ready, i + 1)
                if not isinstance(i, int):
                    pe.wait_ge(pv_read, i)
                w = 2 * D1 + 2
                pe.wait_ge(vtile_ready, i + 1)
                for c in range(2):
                    for n in range(H1 // 2):
                        ins = pe.matmul(ps[CS * c:CS * (c + 1), 1, w * n:w * (n + 1)], p1T[:, n, CS * c:CS * (c + 1)], vtile[:, c, n, :],
                                        start=True, stop=True)
                ins.then_inc(pv_done, 1)

            chunk_products(0)
            with pe.Fori(1, NT) as i:
                chunk_products(i)
            pe.wait_ge(o1_ready, 1)
            turn1(D_FILLS["o1T"], o1, None, 0)
            for g in range(4):
                o = d_fill(D_FILLS["s1"] + g)
                pe.wait_ge(d_drained, D_FILLS["o1T"] + g + 1)
                for t in range(4 * g, 4 * g + 4):
                    ins = pe.matmul(o[:, P * (t % 4):P * (t % 4 + 1)], q1T[:, P * t:P * (t + 1)], wout1, start=True, stop=True)
                ins.then_inc(d_filled, 1)

            turn1(D_FILLS["nxT"], y, nx_ready, 0)
            W3 = D + 2 * DM
            for g in range(8):
                o = d_fill(D_FILLS["qkv"] + g)
                pe.wait_ge(d_drained, D_FILLS["nxT"] + g // 2 + 1)
                for t in range(2 * g, 2 * g + 2):
                    ins = pe.matmul(o[:, W3 * (t % 2):W3 * (t % 2 + 1)], xnT[:, P * t:P * (t + 1)], wmq, start=True, stop=True)
                ins.then_inc(d_filled, 1)
            pe.wait_ge(copies_ready, 2)
            for g in range(4):
                o = d_fill(D_FILLS["kaT"] + g)
                for t in range(4):
                    ins = pe.transpose(o[0:M_ROWS, P * t:P * (t + 1)], ka[:, 4 * g + t, :], ident[:, :])
                ins.then_inc(d_filled, 1)
            pe.wait_ge(d_drained, D_FILLS["kaT"] + 4)

            def turn_queries(i, parity, first=False):
                pe.wait_ge(tile_ready, i + 1)
                if not first:
                    pe.wait_ge(mr_ready, i)
                for h in range(HM):
                    ins = pe.transpose(bank(7)[0:R_ROWS, P * h:P * (h + 1)], qtile2[:, parity, h, 0:R_ROWS], ident[:, :])
                ins.then_inc(q_turned, 1)

            def turn_maxima(i, parity, first=False):
                pe.wait_ge(m_step, 3 * i + 3)
                pe.wait_ge(qr_ready, i + 1)
                if not first:
                    pe.wait_ge(om_read, 4 * i - 4)
                for h in range(HM):
                    ins = pe.transpose(bank(7)[0:M_ROWS, P * h:P * (h + 1)], qtile2[:, parity, h, :], ident[:, :])
                ins.then_inc(m_turned, 1)

            def maximum(i, u, parity, first=False):
                h, c = u // HM, u % HM * 512
                if u == 0:
                    pe.wait_ge(qr_ready, i + 1)
                if not (first and u < 2):
                    pe.wait_ge(mx_read, i * MU + u - 1)
                pe.matmul(bank(u % 2), qr[0:R_ROWS, parity, h * P:(h + 1) * P], kr[0:R_ROWS, c:c + 512],
                          start=True, stop=True).then_inc(mx_filled, 1)

            def scores_t(i, t, parity, first):
                if t == 0:
                    pe.wait_ge(mr_ready, i + 1)
                if not (first and t < RING):
                    pe.wait_ge(p_whole, i * NT + t - RING + 1)
                    pe.wait_ge(ph_ready, i * len(CUT) + len([c for c in CUT if c <= t - RING])
                               if t >= RING else i * len(CUT) - len([c for c in CUT if c > NT + t - RING]))
                pe.matmul(bank(2 + t % RING), kr[0:M_ROWS, t * P:(t + 1) * P], qr[0:M_ROWS, parity, :],
                          start=True, stop=True).then_inc(st_filled, 1)

            def weigh_t(i, t, first):
                if t == 0 and not first:
                    pe.wait_ge(oT_ready, i)
                if KIND[t] == "w":
                    pe.wait_ge(p_whole, i * NT + t + 1)
                    ins = pe.matmul(bank(6)[0:DM + 1, :], v1[:, t, :], pm[:, t % RING, :], start=False, stop=(t == NT - 1),
                                    skip_group_check=True)
                else:
                    pe.wait_ge(ph_ready, i * len(CUT) + CUT.index(t) + 1)
                    pe.matmul(bank(6)[0:VW, :], vr[:, t, :], ph[:, t % RING, :], start=(t == 0), stop=False, skip_group_check=True)
                    if KIND[t] == "p":
                        pe.wait_ge(pl2_ready, i * len(CUT_P) + CUT_P.index(t) + 1)
                    else:
                        pe.wait_ge(pl_ready, i * len(CUT_D) + CUT_D.index(t) + 1)
                    ins = pe.matmul(bank(6)[0:VW, :], vr[:, t, :], pl[:, t % RING, :], start=False, stop=(t == NT - 1),
                                    skip_group_check=True)
                ins.then_inc(pm_used, 1)

            def turn_rows(i):
                pe.wait_ge(oT_ready, i + 1)
                pe.wait_ge(qr_ready, min(i + 3, NT) if isinstance(i, int) else i + 3)
                for h in range(HM):
                    ins = pe.transpose(bank(7)[:, h * VW:(h + 1) * VW], oT[0:VW, h * P:(h + 1) * P], ident[0:VW, 0:VW])
                ins.then_inc(o_turned, 1)

            turn_queries(0, 0, first=True)
            for u in range(MU):
                maximum(0, u, 0, first=True)
            turn_maxima(0, 0, first=True)

            def shared_tile(i, parity, first=False, more=True):
                for t in range(NT):
                    scores_t(i, t, parity, first)
                    if more and t == 0:
                        turn_queries(i + 1, 1 - parity)
                    if more:
                        for u in range(MU):
                            if MAX_SLOTS[u] == t:
                                maximum(i + 1, u, 1 - parity)
                    if t == LAG and not first:
                        turn_rows(i - 1)
                    if more and t == TURN_SLOT:
                        turn_maxima(i + 1, 1 - parity, first)
                    if t >= LAG:
                        weigh_t(i, t - LAG, first)
                    elif not first:
                        weigh_t(i - 1, NT + t - LAG, False)

            over_tiles(pe, shared_tile, 1)
            for t in range(NT - LAG, NT):
                weigh_t(NT - 1, t, False)
            turn_rows(NT - 1)

            pe.wait_ge(om_read, 4 * NT)
            turn1(D_FILLS["omT"], om, None, 0)
            for g in range(4):
                o = d_fill(D_FILLS["mo"] + g)
                pe.wait_ge(d_drained, D_FILLS["omT"] + g + 1)
                for t in range(4 * g, 4 * g + 4):
                    ins = pe.matmul(o[:, P * (t % 4):P * (t % 4 + 1)], xnT[:, P * t:P * (t + 1)], wmo, start=True, stop=True)
                ins.then_inc(d_filled, 1)
            turn1(D_FILLS["nx2T"], om, nx_ready, NT)
            pe.wait_ge(d_drained, D_FILLS["nx2T"] + 4)
            o = d_fill(D_FILLS["lg1"])
            for t in range(NT):
                ins = pe.matmul(o[:, E1 * t:E1 * (t + 1)], xnT[:, P * t:P * (t + 1)], wr, start=True, stop=True)
            ins.then_inc(d_filled, 1)
            pe.wait_ge(d_drained, D_FILLS["lg1"] + 1)

            def hidden(j, e):
                n_ = j * ES + e
                if e >= 2 or not isinstance(j, int):
                    pe.wait_ge(h1T_ready, n_ - 1 + (e == 0))
                rhs = xnT[:, j * CH:(j + 1) * CH] if isinstance(j, int) else xnT[:, bass.ds(j * CH, CH)]
                pe.matmul(bank(2 * (e % 2)), e13[:, e, 0:D], rhs, start=True, stop=True)
                pe.matmul(bank(2 * (e % 2) + 1), e13[:, e, D:2 * D], rhs, start=True, stop=True).then_inc(h13_filled, 1)

            def project(j, e):
                n_ = j * ES + e
                pe.wait_ge(h1T_ready, n_ + 1)
                if e >= 2 or not isinstance(j, int):
                    pe.wait_ge(e_read, (n_ - 1 + (e == 0)) * (CH // P))
                for t in range(CH // P):
                    ins = pe.matmul(bank(4 + e % 2)[:, t * P:(t + 1) * P], h1T[:, e % 2, t * P:(t + 1) * P], e2[:, e, :],
                                    start=True, stop=True)
                ins.then_inc(e_filled, 1)

            def mixture(j):
                for e in range(ES + 1):
                    if e < ES:
                        hidden(j, e)
                    if e >= 1:
                        project(j, e - 1)

            mixture(0)
            with pe.Fori(1, NCH) as j:
                mixture(j)


def layouts(np, i):
    c = np.ascontiguousarray
    a = {k: np.asarray(v) for k, v in i.items()}
    D_ = a["L0_attn_Wq"].shape[0]
    return dict(
        x=c(a["L0_attn_x"].reshape(-1, D_)),
        w0=c(np.concatenate([a["L0_attn_Wq"].T, a["L0_attn_Wk"].T, a["L0_attn_Wv"].T, a["L0_ffn_Wqkv"][2 * D_:].T, a["L0_ffn_Wo"].T], axis=1)),
        cols0=c(np.stack([a["L0_ffn_bqkv"][2 * D_:], a["L0_attn_bk"], a["L0_attn_bq"]], axis=1)),
        rows0=c(np.concatenate([a["L0_attn_bv"], a["L0_ffn_bo"], a["L0_ffn_g1"], a["L0_ffn_be1"], a["L0_ffn_g2"], a["L0_ffn_be2"]])),
        wgT=c(a["L0_ffn_Wg"].T),
        w1=c(a["L0_ffn_W1"].transpose(1, 0, 2)),
        b1=c(a["L0_ffn_b1"].reshape(8, 4, 128).transpose(2, 0, 1)),
        w2=c(a["L0_ffn_W2"].reshape(8, 4, 128, D_).transpose(2, 0, 1, 3)),
        b2=c(a["L0_ffn_b2"].reshape(-1)),
        wl1=c(np.concatenate([a["L1_attn_W_qkv"], a["L1_attn_W_out"], a["L1_ffn_Wq"].T, a["L1_ffn_Wkc"].T, a["L1_ffn_Wvc"].T,
                              a["L1_ffn_Wo"].T, a["L1_ffn_Wr"].T], axis=1)),
        rows1=c(np.concatenate([a["L1_ffn_g1"], a["L1_ffn_g2"], a["L1_ffn_expert_bias"]])),
        e13=c(np.concatenate([np.concatenate([a["L1_ffn_eW1"], a["L1_ffn_sW1"][None]]),
                              np.concatenate([a["L1_ffn_eW3"], a["L1_ffn_sW3"][None]])], axis=1).transpose(2, 0, 1)),
        e2=c(np.concatenate([a["L1_ffn_eW2"], a["L1_ffn_sW2"][None]]).transpose(2, 0, 1)),
    )


def kernel(**inputs):
    import numpy as np
    import concourse.bacc as bacc
    from concourse.bass_utils import run_bass_kernel_spmd

    arrays = layouts(np, inputs)
    shape = tuple(inputs["L0_attn_x"].shape)
    nc = bacc.Bacc("TRN2", target_bir_lowering=False, num_devices=1)
    aps = {n: nc.dram_tensor(f"in_{n}", a.shape, mybir.dt.from_np(a.dtype), kind="ExternalInput").ap() for n, a in arrays.items()}
    out = nc.dram_tensor("out_0", [shape[0] * shape[1], shape[2]], F32, kind="ExternalOutput").ap()
    bass_recurrent_two_layers(nc, aps, out)
    r = run_bass_kernel_spmd(nc, [{f"in_{n}": a for n, a in arrays.items()}], core_ids=[0])
    return r.results[0]["out_0"].reshape(shape)
```

```python
from contextlib import ExitStack

import concourse.bass as bass
from concourse import mybir

P = 128
T = 2048
NT = T // P
D = 128
F32 = mybir.dt.float32
F32R = mybir.dt.float32r
I32 = mybir.dt.int32
U32 = mybir.dt.uint32
ALU = mybir.AluOpType
ACT = mybir.ActivationFunctionType
AX = mybir.AxisListType

E0 = 8
F0 = 512
FC0 = F0 // P
GROUP = 4
WINDOWS = -(-(NT + E0 - 1) // GROUP) * GROUP
GROUPS = WINDOWS // GROUP
NEG = -1.0e30

CS = 64
NC = T // CS
H1 = 16
D1 = D // H1
VP = 2 * D1 + 2
HG = 4
SC1 = float(D1) ** -0.5
MASKED = -65000.0
REGION = 23872
HM = 4
DM = D // HM
SCM = float(DM) ** -0.5
R_ROWS = 3 * DM
M_ROWS = R_ROWS + 2
VW = 3 * DM
KIND = "pdpwpdpdpdpwpdpw"
CUT = [t for t in range(NT) if KIND[t] != "w"]
CUT_D = [t for t in range(NT) if KIND[t] == "d"]
CUT_P = [t for t in range(NT) if KIND[t] == "p"]
RING = 4
LAG = 3
MU = HM * T // 512
MAX_START = 12
QUERY_SLOT = 9
TURN_SLOT = 13
E1 = 8
ES = E1 + 1
CH = 512
NCH = T // CH
FINISH = 3
TG = 4
NG = NT // TG


class Region:

    def __init__(self, tensor, size):
        self.tensor, self.size, self.at = tensor, size, 0

    def reset(self, at=0):
        self.at = at

    def take(self, *shape):
        words = 1
        for d in shape:
            words *= d
        assert self.at + words <= self.size, (self.at, words, self.size)
        a = self.tensor[:, self.at:self.at + words]
        self.at += words
        names = "abcd"[:len(shape)]
        if len(shape) == 1:
            return a
        return a.rearrange(f"p ({' '.join(names)}) -> p {' '.join(names)}", **dict(zip(names, shape)))


class Link:

    def __init__(self, engine, sem):
        self.engine, self.sem, self.n = engine, sem, 0

    def mark(self, ins):
        self.n += 1
        ins.then_inc(self.sem, 1)

    def wait(self):
        self.engine.wait_ge(self.sem, self.n)

    def __call__(self, ins):
        self.mark(ins)
        self.wait()


def at(a, i):
    if isinstance(i, int):
        return a[:, i]
    one = a[:, bass.ds(i, 1)]
    names = " ".join("abcd"[:len(one.shape) - 2])
    return one.rearrange(f"p o {names} -> p (o {names.split()[0]}) {' '.join(names.split()[1:])}")


def over_tiles(engine, tile, ahead):
    tile(0, 0, first=True, more=ahead < NT)
    tile(1, 1)
    with engine.Fori(1, NT // 2 - 1) as j:
        for parity in range(2):
            tile(j * 2 + parity, parity)
    tile(NT - 2, 0, more=ahead < 2)
    tile(NT - 1, 1, more=False)


def still(i, ahead):
    return not isinstance(i, int) or i + ahead < NT


def maximum_at(i, t):
    return (i + 2, t - MAX_START) if t >= MAX_START else (i + 1, t + NT - MAX_START)


def cuts(sizes):
    at, found = 0, []
    for n in sizes:
        found.append((at, at + n))
        at += n
    return found


def bass_recurrent_two_layers(nc, A, out):
    with ExitStack() as ctx:
        def sb(name, shape, dt=F32):
            return ctx.enter_context(nc.sbuf_tensor(name, shape, dt))

        def sem(name):
            return ctx.enter_context(nc.semaphore(name))

        ps = ctx.enter_context(nc.psum_tensor("ps", [P, 8, 512], F32))

        slots_in = nc.dram_tensor("slots_in", [WINDOWS * P, D], F32, kind="Internal").ap()
        slots_out = nc.dram_tensor("slots_out", [WINDOWS * P, D], F32, kind="Internal").ap()

        chunk_sums = nc.dram_tensor("chunk_sums", [NC, 2 * D], F32, kind="Internal").ap()

        region = Region(sb("region", [P, REGION]), REGION)
        x = sb("x", [P, NT, D])
        xn = sb("xn", [P, NT, D])
        xnT = sb("xnT", [P, T])
        qT = region.take(T)
        kT = region.take(T)
        v = region.take(NT, D)
        vfT = region.take(T)
        y = sb("y", [P, NT, D])
        s0 = sb("s0", [P, NT, D])
        w0 = sb("w0", [P, 5 * D])
        cols0 = sb("cols0", [P, 3])
        rows0 = sb("rows0", [P, 6 * D])
        bv_row, bo_row, g1_row, be1_row, g2_row, be2_row = (rows0[:, n * D:(n + 1) * D] for n in range(6))
        wgT = sb("wgT", [P, E0])
        b1_col = sb("b1_col", [P, E0, FC0])
        w1 = region.take(E0, F0)
        w2 = region.take(E0, FC0, D)
        b2_row = region.take(E0, D)
        ident = sb("ident", [P, P])
        ones = sb("ones", [P, P])
        before = sb("before", [P, P])
        causal = sb("causal", [P, P])
        zeros = sb("zeros", [P, D])
        amask = sb("amask", [P, CS])
        mask4 = sb("mask4", [P, HG])
        vmask = sb("vmask", [P, D])
        stats = sb("stats", [P, NT, 6])
        mv = sb("mv", [P, NT, 2])
        vare = sb("vare", [P, NT])
        mhalf = sb("mhalf", [P, NT])
        rstd = sb("rstd", [P, NT])
        lg = sb("lg", [P, NT, E0])
        top = sb("top", [P, NT, 8])
        topi = sb("topi", [P, NT, 8], U32)
        expert = sb("expert", [P, NT])
        iota_e = sb("iota_e", [P, E0, NT])
        onehot = sb("onehot", [P, E0, NT])
        rank = sb("rank", [P, E0, NT])
        upto = sb("upto", [P, E0, NT])
        scanmask = sb("scanmask", [P, E0, NT])
        cnt_i = sb("cnt_i", [P, E0], I32)
        pad = sb("pad", [P, E0])
        end = sb("end", [P, E0])
        base = sb("base", [P, E0])
        slot_f = sb("slot_f", [P, NT])
        slot = sb("slot", [P, NT], U32)
        wstart = sb("wstart", [P, WINDOWS, E0])
        wcmp = sb("wcmp", [P, WINDOWS, E0])
        wexp_f = sb("wexp_f", [P, WINDOWS])
        wexp = sb("wexp", [P, WINDOWS], I32)
        xg = region.take(GROUP, D)
        overlay = region.at
        prob = region.take(2, T)
        probT = region.take(2, 512)
        rmax = sb("rmax", [P, NT])
        nmax = sb("nmax", [P, NT])
        rsum = sb("rsum", [P, NT])
        rinv = sb("rinv", [P, NT])
        region.reset(overlay)
        xgT = region.take(GROUP, P)
        hb = region.take(GROUP, F0)
        hT = region.take(GROUP, F0)
        og = sb("og", [P, GROUP, D])
        moe = vfT[:, :].rearrange("p (t d) -> p t d", t=NT)
        yT = xn[:, :, :].rearrange("p t d -> p (t d)")

        wl1 = sb("wl1", [P, 3 * D + D + (D + 2 * DM) + D + E1])
        wq1, wk1, wv1, wout1, wmq, wmo, wr = (wl1[:, a:b] for a, b in cuts([D, D, D, D, D + 2 * DM, D, E1]))
        e13 = sb("e13", [P, ES, 2 * D])
        e2 = sb("e2", [P, ES, D])
        rg1_col = sb("rg1_col", [P, 1])
        rows1 = sb("rows1", [P, D + E1])
        rg2_row, eb_row = (rows1[:, a:b] for a, b in cuts([D, E1]))
        msq = sb("msq", [P, NT])
        rstdq = sb("rstdq", [P, NT])
        shift = sb("shift", [P, NT])
        each_group = [slice(TG * g, TG * (g + 1)) for g in range(NG)]
        region.reset()
        k4 = region.take(NC, HG, CS)
        vbd = region.take(NT, H1 // 2, 2, VP)
        vsum = region.take(NT, D)
        ksum = y
        q1T = region.take(T)
        sm_at = region.at
        sm = region.take(2, H1, CS)
        pe1 = region.take(2, H1, CS)
        p1T = region.take(H1 // 2, P)
        xsum = region.take(NC)
        xcum = region.take(NC)
        qtile = region.take(2, P)
        ktile = region.take(2, 2, HG, CS)
        sig = region.take(NT, H1)
        kvs = og[0:NC, 0:2, :].rearrange("p a d -> p (a d)")
        mx1 = region.take(H1)
        rs1 = region.take(H1)
        o1 = s0
        xtwice = region.tensor[:, sm_at:sm_at + 2 * T].rearrange("p (n r s) -> p n r s", r=2, s=CS)
        region.reset()
        om = region.take(NT, D)
        qkv = region.take(NT, D + 2 * DM)
        qa = region.take(NT, HM, R_ROWS)
        ka = region.take(NT, M_ROWS)
        qtile2 = region.take(2, HM, M_ROWS)
        v1 = region.take(NT, DM + 1)
        pm = region.take(RING, HM * P)
        mxp = region.take(HM, MU // HM)
        negm = region.take(HM)
        oT = region.take(HM * P)
        ol = region.take(HM, DM)
        rsm = region.take(HM)
        qm = sb("qm", [P, 2, HM * P], F32R)
        qr = sb("qr", [P, 2, HM * P], F32R)
        kr = sb("kr", [P, T], F32R)
        vr = sb("vr", [P, NT, VW], F32R)
        ph = sb("ph", [P, RING, HM * P], F32R)
        pl = sb("pl", [P, RING, HM * P], F32R)
        xh, xl = kr, ph
        pl_, qm_, vr_, qr_ = (a[:, :, :].rearrange("p a b -> p (a b)") for a in (pl, qm, vr, qr))
        eh = [pl_[:, 2 * D * e:2 * D * (e + 1)] for e in range(RING * HM * P // (2 * D))] + [qm_[:, 0:2 * D]]
        el = [vr_[:, 2 * D * e:2 * D * (e + 1)] for e in range(NT * VW // (2 * D))]
        el += [qr_[:, 2 * D * e:2 * D * (e + 1)] for e in range(ES - len(el))]
        region.reset(NT * D)
        lg1 = region.take(NT, E1)
        rw = region.take(NT, E1)
        top1 = region.take(NT, 8)
        topi1 = region.take(NT, 8).bitcast(U32)
        mrow = region.take(NT)
        w12 = region.take(2, NT)
        ix12 = region.take(2, NT)
        iota1 = region.take(NT, E1)
        comb = region.take(NT, ES)
        ctmp = region.take(NT, E1)
        sg = region.take(2, CH)
        h1T = region.take(2, CH)

        s_x = [sem(f"s_x{g}") for g in range(NG)]
        s_w0 = sem("s_w0"); s_rows0 = sem("s_rows0"); s_wexp = sem("s_wexp")
        s_const = sem("s_const"); s_zero = sem("s_zero"); s_zeroed = sem("s_zeroed")
        dve_step = sem("dve_step"); pool_step = sem("pool_step"); act_step = sem("act_step")
        var_ready = [sem(f"var{n}_ready") for n in range(5)]
        rstd_ready = [sem(f"rstd{n}_ready") for n in range(5)]
        xn_ready = sem("xn_ready")
        d_filled = sem("d_filled"); d_drained = sem("d_drained")
        a_filled = sem("a_filled"); a_drained = sem("a_drained")
        y_ready = sem("y_ready"); onehot_ready = sem("onehot_ready")
        slot_ready = sem("slot_ready"); scattered = sem("scattered"); wexp_ready = sem("wexp_ready")
        score_done = sem("score_done"); nmax_ready = sem("nmax_ready"); prob_ready = sem("prob_ready")
        xg_loaded = sem("xg_loaded"); xg_turned = sem("xg_turned"); xgT_ready = sem("xgT_ready")
        h_done = sem("h_done"); hb_ready = sem("hb_ready"); h_turned = sem("h_turned"); hT_ready = sem("hT_ready")
        o_done = sem("o_done"); og_ready = sem("og_ready"); og_stored = sem("og_stored")
        gathered = [sem(f"gathered{g}") for g in range(NG)]
        s_out = sem("s_out"); fin_ready = sem("fin_ready")

        s_w1 = sem("s_w1")
        zn_ready = sem("zn_ready"); z_ready = sem("z_ready"); g_ready = sem("g_ready"); x1_ready = sem("x1_ready")
        xsum_ready = sem("xsum_ready"); prep_ready = sem("prep_ready"); mask_ready = sem("mask_ready")
        qtile_ready = sem("qtile_ready"); s_done = sem("s_done"); s_read = sem("s_read")
        sm_ready = sem("sm_ready"); p_ready = sem("p_ready"); p_turned = sem("p_turned"); pT_ready = sem("pT_ready")
        sigexp_ready = sem("sigexp_ready"); crs_ready = sem("crs_ready"); pv_done = sem("pv_done"); pv_free = sem("pv_free")
        mx1_ready = sem("mx1_ready"); rs1_ready = sem("rs1_ready"); o1_ready = sem("o1_ready")
        cross_ready = sem("cross_ready"); twice_ready = sem("twice_ready"); half_done = sem("half_done"); sums_ready = sem("sums_ready")
        sums_stored = sem("sums_stored"); sums_loaded = sem("sums_loaded")
        nx_ready = sem("nx_ready"); parts_ready = sem("parts_ready"); kv_low_ready = sem("kv_low_ready")
        q_low_ready = sem("q_low_ready"); copies_ready = sem("copies_ready")
        chunks_done = sem("chunks_done"); wmq_ready = sem("wmq_ready"); rstdq_ready = sem("rstdq_ready"); qkv_ready = sem("qkv_ready")
        mx_filled = sem("mx_filled"); mx_read = sem("mx_read"); m_turned = sem("m_turned")
        tile_ready = sem("tile_ready"); q_turned = sem("q_turned"); qm_ready = sem("qm_ready")
        ph_ready = sem("ph_ready"); pl_ready = sem("pl_ready"); pl2_ready = sem("pl2_ready"); oT_ready = sem("oT_ready"); o_turned = sem("o_turned")
        mr_ready = sem("mr_ready"); st_filled = sem("st_filled"); p_whole = sem("p_whole"); pm_used = sem("pm_used")
        om_read = sem("om_read"); m_step = sem("m_step")
        eh_ready = sem("eh_ready"); el_ready = sem("el_ready"); xh_ready = sem("xh_ready"); xl_ready = sem("xl_ready")
        rx_ready = sem("rx_ready"); rexp_ready = sem("rexp_ready")
        h13_filled = sem("h13_filled"); sg_ready = sem("sg_ready"); h1T_ready = sem("h1T_ready"); e_filled = sem("e_filled")
        e_read = sem("e_read"); acc_ready = sem("acc_ready"); g1_ready = sem("g1_ready"); prod_ready = sem("prod_ready")

        def window_experts(engine, i):
            _, e = nc.values_load_multi_w_load_instructions(
                wexp[0:1, bass.ds(i * GROUP, GROUP)], engines=(engine,), min_val=0, max_val=E0 - 1,
                skip_runtime_bounds_check_because="wexp is a count of experts, and taken to at most E0 - 1")
            return e

        small = NT // 2
        scores_of = lambda i: ps[:, 4 + (2 * (i % 2) if i < small else 0):8, :].rearrange("p b c -> p (b c)")[:, 0:(i + 1) * P]
        prob_flat = prob.rearrange("p a b -> p (a b)")
        prob_of = lambda i: prob_flat[:, i % 4 * (T // 2):][:, 0:(i + 1) * P] if i < small else prob[:, i % 2, 0:(i + 1) * P]
        def bank(n):
            return ps[:, n, :]

        small = NT // 2
        between = {("values", n): [("mha", n), ("norm", n - 1)] for n in range(NG)}
        between["values", NG] = [("norm", NG - 1), ("turn_y", 0)]
        between.update({("values", NG + g): [("turn_y", g)] for g in range(1, NG)})
        between["values", 2 * NG] = [("logits", 0)]
        between["values", 2 * NG + 2] = [("ranks", 0)]
        attention_order = [("scores", 0), ("scores", 1)]
        for i in range(NT):
            if i + 2 < small:
                attention_order.append(("scores", i + 2))
            if small - 2 < i < NT - 1:
                attention_order.append(("scores", i + 1))
            attention_order.append(("values", i))
            attention_order += [b for b in between.get(("values", i), []) if b[1] >= 0]
        attention_fill = {stage: 2 * NG + n for n, stage in enumerate(
            b for b in attention_order if b[0] in ("values", "mha", "turn_y", "logits", "ranks"))}

        D_FILLS = dict(zip(
            ("xnT", "v", "attention", "xn1T", "vdup", "cross",
             "o1T", "kaT", "omT", "mo", "nx2T", "lg1"),
            (a for a, _ in cuts([4, 4, len(attention_fill), 4, 8, 4, 4, 4, 4, 4, 4, 1]))))
        A_FILLS = dict(zip(("proj", "turn", "k1", "q1", "sums", "qkv", "s1"),
                           (a for a, _ in cuts([12, sum(i // 4 + 1 for i in range(NT)), 4, 4, 1, 8, 4]))))

        rows = lambda r, n: r.unsqueeze(1).broadcast_to([P, n, D])

        block = ctx.enter_context(nc.Block())

        @block.sync
        def _(sp):
            for g, r in enumerate(each_group):
                sp.dma_start(x[:, r, :], A["x"].rearrange("(t p) d -> p t d", p=P)[:, r, :]).then_inc(s_x[g], 16)
            sp.dma_start(w0[:, :], A["w0"]).then_inc(s_w0, 16)
            sp.dma_start(cols0[:, :], A["cols0"]).then_inc(s_w0, 16)
            sp.dma_start(wgT[:, :], A["wgT"]).then_inc(s_w0, 16)
            sp.dma_start(rows0[:, :], A["rows0"].partition_broadcast(P)).then_inc(s_rows0, 16)
            sp.wait_ge(s_zero, 1)
            sp.dma_start(slots_in.rearrange("(w p) d -> p w d", p=P),
                         zeros[:, :].unsqueeze(1).broadcast_to([P, WINDOWS, D])).then_inc(s_zeroed, 16)
            sp.dma_start(w1[:, :, :], A["w1"]).then_inc(s_wexp, 16)
            sp.dma_start(b1_col[:, :, :], A["b1"]).then_inc(s_wexp, 16)
            sp.dma_start(w2[:, :, :, :], A["w2"]).then_inc(s_wexp, 16)
            sp.dma_start(b2_row[:, :, :], A["b2"].partition_broadcast(P)).then_inc(s_wexp, 16)
            sp.dma_start(wl1[:, :], A["wl1"]).then_inc(s_w1, 16)
            sp.dma_start(rows1[:, :], A["rows1"].partition_broadcast(P)).then_inc(s_w1, 16)
            sp.dma_start(rg1_col[:, :], A["g1c"]).then_inc(s_w1, 16)
            sp.dma_start(e13[:, :, :], A["e13"]).then_inc(s_w1, 16)
            sp.dma_start(e2[:, :, :], A["e2"]).then_inc(s_w1, 16)
            sp.wait_ge(scattered, 16 * NT)
            rin = slots_in.rearrange("(w p) d -> p w d", p=P)
            rout = slots_out.rearrange("(w p) d -> p w d", p=P)
            sp.dma_start(xg[:, :, :], rin[:, 0:GROUP, :]).then_inc(xg_loaded, 16)
            with sp.Fori(1, GROUPS) as i:
                sp.wait_ge(xg_turned, i)
                sp.dma_start(xg[:, :, :], rin[:, bass.ds(i * GROUP, GROUP), :]).then_inc(xg_loaded, 16)
                sp.wait_ge(og_ready, i * GROUP)
                sp.dma_start(rout[:, bass.ds((i - 1) * GROUP, GROUP), :], og[:, :, :]).then_inc(og_stored, 16)
            sp.wait_ge(og_ready, GROUPS * GROUP)
            sp.dma_start(rout[:, (GROUPS - 1) * GROUP:GROUPS * GROUP, :], og[:, :, :]).then_inc(og_stored, 16)
            sp.wait_ge(og_stored, 16 * GROUPS)
            sp.wait_ge(sums_ready, 1)
            sp.dma_start(chunk_sums, kvs).then_inc(sums_stored, 16)
            sp.wait_ge(sums_stored, 16)
            sp.wait_ge(x1_ready, NG)
            for c in range(2):
                for dst, r in ((ksum, slice(0, D)), (vsum, slice(D, 2 * D))):
                    sp.dma_start(dst[CS * c:CS * (c + 1), :, :],
                                 chunk_sums.rearrange("(t c) d -> c t d", c=2)[c, :, r].partition_broadcast(CS)).then_inc(sums_loaded, 16)
            q_ = CH // P
            rows_out = out.rearrange("(t p) d -> p t d", p=P)
            for j in range(NCH):
                sp.wait_ge(fin_ready, j + 1)
                sp.dma_start(rows_out[:, j * q_:(j + 1) * q_, :], y[:, j * q_:(j + 1) * q_, :]).then_inc(s_out, 16)
            sp.wait_ge(s_out, 16 * NCH)

        @block.gpsimd
        def _(pool):
            link = Link(pool, pool_step)
            pool.memset(zeros[:, :], 0.0).then_inc(s_zero, 1)
            link.mark(pool.memset(ident[:, :], 0.0))
            link.mark(pool.memset(before[:, :], 1.0))
            link.mark(pool.memset(causal[:, :], 0.0))
            link.mark(pool.memset(scanmask[:, :, :], 1.0))
            link(pool.memset(mhalf[:, :], -0.5))
            link.mark(pool.affine_select(out=ident[:, :], in_=ident[:, :], compare_op=ALU.not_equal, fill=1.0,
                                         base=0, pattern=[[-1, P]], channel_multiplier=1))
            link.mark(pool.affine_select(out=before[:, :], in_=before[:, :], compare_op=ALU.is_gt, fill=0.0,
                                         base=0, pattern=[[1, P]], channel_multiplier=-1))
            link.mark(pool.affine_select(out=causal[:, :], in_=causal[:, :], compare_op=ALU.is_ge, fill=NEG,
                                         base=0, pattern=[[-1, P]], channel_multiplier=1))
            link.mark(pool.memset(scanmask[:, :, 0:1], 0.0))
            link.mark(pool.iota(iota_e[:, :, :], pattern=[[1, E0], [0, NT]], base=0, channel_multiplier=0,
                                allow_small_or_imprecise_dtypes=True))
            link.mark(pool.iota(wstart[:, :, :], pattern=[[P, WINDOWS], [0, E0]], base=0, channel_multiplier=0,
                                allow_small_or_imprecise_dtypes=True))
            link(pool.memset(ones[:, :], 1.0))
            pool.sem_inc(s_const, 1)

            def inverse_deviation(n, g, eps):
                r = each_group[g]
                pool.wait_ge(var_ready[n], TG * (g + 1))
                link(pool.tensor_scalar(vare[:, r], mv[:, r, 1], eps, None, ALU.add))
                if n < 2:
                    pool.tensor_tensor(rstd[:, r], vare[:, r], mhalf[:, r], ALU.pow).then_inc(rstd_ready[n], 1)
                else:
                    link(pool.tensor_tensor(rstd[:, r], vare[:, r], mhalf[:, r], ALU.pow))
                    link(pool.tensor_tensor(shift[:, r], mv[:, r, 0], rstd[:, r], ALU.mult))
                    pool.tensor_scalar(shift[:, r], shift[:, r], -1.0, None, ALU.mult).then_inc(rstd_ready[n], 1)

            def inverse_root(n, g, eps):
                r = each_group[g]
                pool.wait_ge(var_ready[n], TG * (g + 1))
                link(pool.tensor_tensor(msq[:, r], mv[:, r, 0], mv[:, r, 0], ALU.mult))
                link(pool.tensor_tensor(msq[:, r], msq[:, r], mv[:, r, 1], ALU.add))
                link(pool.tensor_scalar(vare[:, r], msq[:, r], eps, None, ALU.add))
                pool.tensor_tensor(rstd[:, r], vare[:, r], mhalf[:, r], ALU.pow).then_inc(rstd_ready[n], 1)

            for g in range(NG):
                inverse_deviation(0, g, 1e-5)
            link.mark(pool.memset(amask[:, :], 0.0))
            link.mark(pool.memset(mask4[:, :], 1.0))
            link(pool.memset(vmask[:, :], 1.0))
            for c in range(2):
                v_ = amask[CS * c:CS * (c + 1), :]
                link(pool.affine_select(out=v_, in_=v_, compare_op=ALU.is_ge, fill=MASKED / SC1,
                                             base=0, pattern=[[-1, CS]], channel_multiplier=1))
            for g in range(D // 32):
                m_ = mask4[32 * g:32 * (g + 1), :]
                link(pool.affine_select(out=m_, in_=m_, compare_op=ALU.is_ge, fill=0.0,
                                        base=0, pattern=[[-D1, HG]], channel_multiplier=1))
                link(pool.affine_select(out=m_, in_=m_, compare_op=ALU.is_ge, fill=0.0,
                                             base=D1 - 1, pattern=[[D1, HG]], channel_multiplier=-1))
            for h in range(2):
                hv = vmask[CS * h:CS * (h + 1), :].rearrange("p (n two d) -> p n two d", two=2, d=D1)
                link(pool.memset(hv[:, :, 1 - h, :], 0.0))
            link.wait()
            pool.sem_inc(mask_ready, 1)
            for g in range(NG):
                inverse_deviation(1, g, 1e-5)
            pool.wait_ge(slot_ready, 1)
            pool.wait_ge(y_ready, NT)
            pool.wait_ge(s_zeroed, 16)
            for t in range(NT):
                pool.indirect_dma_start(out=slots_in[:, :], out_offset=bass.IndirectOffsetOnAxis(ap=slot[:, t:t + 1], axis=0),
                                        in_=y[:, t, :], in_offset=None).then_inc(scattered, 16)
            pool.wait_ge(og_stored, 16 * GROUPS)
            def gather(g):
                for t in range(TG * g, TG * (g + 1)):
                    pool.indirect_dma_start(out=moe[:, t, :], out_offset=None, in_=slots_out[:, :],
                                            in_offset=bass.IndirectOffsetOnAxis(ap=slot[:, t:t + 1], axis=0)).then_inc(gathered[g], 16)

            gather(0)
            for step in range(1, NG + 3):
                if step < NG:
                    gather(step)
                if step - 1 < NG:
                    inverse_deviation(2, step - 1, 1e-5)
                if 0 <= step - 3 < NG:
                    inverse_deviation(3, step - 3, 1e-5)

            pool.wait_ge(rstd_ready[3], NG)
            link(pool.tensor_tensor(msq[:, :], mv[:, :, 1], rstd[:, :], ALU.mult))
            link(pool.tensor_tensor(msq[:, :], msq[:, :], rstd[:, :], ALU.mult))
            link(pool.tensor_scalar(msq[:, :], msq[:, :], 1e-6, None, ALU.add))
            pool.tensor_tensor(rstdq[:, :], msq[:, :], mhalf[:, :], ALU.pow).then_inc(rstdq_ready, 1)
            pool.wait_ge(s_w1, 80)
            pool.tensor_scalar(wmq, wmq, rg1_col[:, 0:1], None, ALU.mult).then_inc(wmq_ready, 1)

            pool.wait_ge(x1_ready, NG)
            link(pool.memset(vbd[:, :, :, :, 2 * D1:VP], 0.0))
            for h in range(2):
                link(pool.memset(vbd[CS * h:CS * (h + 1), :, :, :, 2 * D1 + h], 1.0))
            pool.sem_inc(mask_ready, 1)

            pool.wait_ge(prep_ready, 2)

            def chunk_tiles(i, parity, first=False, more=True):
                if not first:
                    if not isinstance(i, int) or i >= 2:
                        pool.wait_ge(s_done, i - 1)
                pool.tensor_copy(at(qtile, parity), q1T[:, bass.ds(i * P, P)]).then_inc(qtile_ready, 1)
                pool.tensor_copy(ktile[:, parity, :, :, :], k4[:, bass.ds(i * 2, 2), :, :]).then_inc(qtile_ready, 1)

            over_tiles(pool, chunk_tiles, 1)
            pool.wait_ge(cross_ready, 1)
            pool.wait_ge(sums_loaded, 64)
            pool.tensor_tensor(vsum[:, :, :].rearrange("p t (h d) -> p (t h) d", d=D1),
                               vsum[:, :, :].rearrange("p t (h d) -> p (t h) d", d=D1),
                               sig[:, :, :].rearrange("p t h -> p (t h)").unsqueeze(2).broadcast_to([P, NT * H1, D1]),
                               ALU.mult).then_inc(cross_ready, 1)

            pool.wait_ge(chunks_done, 1)
            link(pool.memset(ka[:, :, R_ROWS:M_ROWS], 1.0))
            link(pool.memset(vr[:, :, DM:DM + 1].bitcast(F32), 1.0))
            link(pool.memset(vr[:, :, 2 * DM + 1:VW].bitcast(F32), 0.0))
            link(pool.memset(v1[:, :, DM:DM + 1], 1.0))
            pool.sem_inc(copies_ready, 1)

            def query_tile(i, parity, first=False):
                if not first:
                    pool.wait_ge(m_turned, i - 1)
                pool.tensor_copy(qtile2[:, parity, :, 0:R_ROWS], at(qa, i)).then_inc(tile_ready, 1)

            pool.wait_ge(copies_ready, 2)
            pool.wait_ge(q_low_ready, 1)
            query_tile(0, 0, first=True)
            query_tile(1, 1, first=True)

            def shared_tile(i, parity, first=False, more=True):
                for t in range(NT):
                    if t == 1 and more:
                        query_tile(i + 2, parity)
                    if t in CUT_P:
                        pool.wait_ge(p_whole, i * NT + t + 1)
                        pool.wait_ge(ph_ready, i * len(CUT) + CUT.index(t) + 1)
                        pool.tensor_tensor(pl[:, t % RING, :], pm[:, t % RING, :], ph[:, t % RING, :].bitcast(F32),
                                           ALU.subtract).then_inc(pl2_ready, 1)

            over_tiles(pool, shared_tile, 2)
            for e in range(ES):
                pool.wait_ge(eh_ready, e + 1)
                pool.tensor_tensor(el[e], e13[:, e, :], eh[e].bitcast(F32), ALU.subtract).then_inc(el_ready, 1)
            for g in range(NG):
                inverse_root(4, g, 1e-6)
            for j in range(NCH):
                pool.wait_ge(xh_ready, j + 1)
                pool.tensor_tensor(xl[:, j, :], xnT[:, CH * j:CH * (j + 1)], xh[:, CH * j:CH * (j + 1)].bitcast(F32),
                                   ALU.subtract).then_inc(xl_ready, 1)

        @block.vector
        def _(dve):
            link = Link(dve, dve_step)

            def variances(n, g, src):
                for t in range(TG * g, TG * (g + 1)):
                    link.mark(dve.bn_stats(stats[:, t, :], src[:, t, :]))
                link.wait()
                for t in range(TG * g, TG * (g + 1)):
                    dve.bn_aggr(mv[:, t, :], stats[:, t, :]).then_inc(var_ready[n], 1)

            def normalise(n, g, src, dst, ready=None):
                dve.wait_ge(var_ready[n], TG * (g + 1))
                dve.wait_ge(rstd_ready[n], g + 1)
                for t in range(TG * g, TG * (g + 1)):
                    ins = dve.tensor_scalar(dst[:, t, :], src[:, t, :], mv[:, t, 0:1], rstd[:, t:t + 1],
                                            ALU.subtract, ALU.mult)
                    if ready is None:
                        link.mark(ins)
                    else:
                        ins.then_inc(ready, 1)
                if ready is None:
                    link.wait()

            def drain(k, dst):
                dve.wait_ge(d_filled, k + 1)
                dve.tensor_copy(dst, bank(k % 2)[:, 0:dst.free_size()] if len(dst.shape) == 2 else bank(k % 2)).then_inc(d_drained, 1)

            for g in range(NG + 2):
                if g < NG:
                    dve.wait_ge(s_x[g], 16)
                    variances(0, g, x)
                if 0 <= g - 1 < NG:
                    normalise(0, g - 1, x, xn, xn_ready)
                if g - 2 >= 0:
                    drain(D_FILLS["xnT"] + g - 2, xnT[:, 512 * (g - 2):512 * (g - 1)])
            dve.wait_ge(xn_ready, NT)
            dve.wait_ge(s_rows0, 16)
            for g in range(4):
                k = D_FILLS["v"] + g
                dve.wait_ge(d_filled, k + 1)
                dve.tensor_tensor(v[:, 4 * g:4 * g + 4, :], bank(k % 2).rearrange("p (t d) -> p t d", t=4),
                                  rows(bv_row, 4), ALU.add).then_inc(d_drained, 1)
            link(dve.tensor_tensor(y[:, :, :], xn[:, :, :], rows(bo_row, NT), ALU.add))

            def residual(g):
                k = attention_fill["mha", g]
                dve.wait_ge(d_filled, k + 1)
                dve.tensor_tensor(y[:, each_group[g], :], bank(k % 2).rearrange("p (t d) -> p t d", t=TG),
                                  y[:, each_group[g], :], ALU.add).then_inc(d_drained, 1)
                dve.wait_ge(d_drained, k + 1)
                variances(1, g, y)

            def norm(g):
                r = each_group[g]
                normalise(1, g, y, y)
                link(dve.tensor_tensor(y[:, r, :], y[:, r, :], rows(g1_row, TG), ALU.mult))
                dve.tensor_tensor(y[:, r, :], y[:, r, :], rows(be1_row, TG), ALU.add).then_inc(y_ready, TG)

            def router(_):
                k = attention_fill["logits", 0]
                dve.wait_ge(d_filled, k + 1)
                dve.tensor_copy(lg[:, :, :], bank(k % 2)[:, 0:NT * E0].rearrange("p (t e) -> p t e", t=NT)).then_inc(d_drained, 1)
                dve.wait_ge(d_drained, k + 1)
                for t in range(NT):
                    link.mark(dve.max(top[:, t, :], lg[:, t, :]))
                link.wait()
                for t in range(NT):
                    link.mark(dve.max_index(topi[:, t, :], top[:, t, :], lg[:, t, :]))
                link.wait()
                link(dve.tensor_copy(expert[:, :], topi[:, :, 0]))
                dve.wait_ge(s_const, 1)
                dve.tensor_tensor(onehot[:, :, :], iota_e[:, :, :], expert[:, :].unsqueeze(1).broadcast_to([P, E0, NT]),
                                  ALU.is_equal).then_inc(onehot_ready, 1)

            def places(_):
                k = attention_fill["ranks", 0]
                dve.wait_ge(d_filled, k + 1)
                in_tile = bank(k % 2)[:, 0:NT * E0].rearrange("p (e t) -> p e t", e=E0)
                of_tile = bank(k % 2)[:, NT * E0:2 * NT * E0].rearrange("p (e t) -> p e t", e=E0)
                fl = lambda a: a[:, :, :].rearrange("p e t -> p (e t)")
                link(dve.tensor_tensor_scan(fl(upto), fl(scanmask), bank(k % 2)[:, NT * E0:2 * NT * E0], 0.0, ALU.mult, ALU.add))
                link(dve.tensor_tensor(rank[:, :, :], upto[:, :, :], of_tile, ALU.subtract))
                link(dve.tensor_tensor(rank[:, :, :], rank[:, :, :], in_tile, ALU.add))
                dve.sem_inc(d_drained, 1)
                link(dve.tensor_scalar(cnt_i[:, :], upto[:, :, NT - 1], float(P - 1), None, ALU.add))
                sh = P.bit_length() - 1
                link(dve.tensor_scalar(cnt_i[:, :], cnt_i[:, :], sh, sh, ALU.logical_shift_right, ALU.logical_shift_left))
                link(dve.tensor_copy(pad[:, :], cnt_i[:, :]))
                link(dve.tensor_tensor_scan(end[:, :], ones[:, 0:E0], pad[:, :], 0.0, ALU.mult, ALU.add))
                link(dve.tensor_tensor(base[:, :], end[:, :], pad[:, :], ALU.subtract))
                link(dve.tensor_tensor(rank[:, :, :], rank[:, :, :], base[:, :].unsqueeze(2).broadcast_to([P, E0, NT]), ALU.add))
                link(dve.tensor_tensor(rank[:, :, :], rank[:, :, :], onehot[:, :, :], ALU.mult))
                link(dve.tensor_reduce(slot_f[:, :], rank[:, :, :].rearrange("p e t -> p t e"), AX.X, ALU.add))
                dve.tensor_copy(slot[:, :], slot_f[:, :]).then_inc(slot_ready, 1)
                link(dve.tensor_tensor(wcmp[:, :, :], end[:, :].unsqueeze(1).broadcast_to([P, WINDOWS, E0]), wstart[:, :, :], ALU.is_le))
                link(dve.tensor_reduce(wexp_f[:, :], wcmp[:, :, :], AX.X, ALU.add))
                dve.tensor_scalar(wexp[:, :], wexp_f[:, :], float(E0 - 1), None, ALU.min).then_inc(wexp_ready, 1)


            def row_max(i):
                dve.wait_ge(score_done, i + 1)
                s = scores_of(i)
                diag = s[:, P * i:P * (i + 1)]
                link(dve.tensor_tensor(diag, diag, causal[:, :], ALU.add))
                link(dve.tensor_reduce(rmax[:, i:i + 1], s, AX.X, ALU.max))
                dve.tensor_scalar(nmax[:, i:i + 1], rmax[:, i:i + 1], -float(D) ** -0.5, None, ALU.mult).then_inc(nmax_ready, 1)

            def attention_out(i):
                k = attention_fill["values", i]
                dve.wait_ge(prob_ready, i + 1)
                link(dve.reciprocal(rinv[:, i:i + 1], rsum[:, i:i + 1]))
                dve.wait_ge(d_filled, k + 1)
                dve.tensor_scalar(s0[:, i, :], bank(k % 2)[:, 0:D], rinv[:, i:i + 1], None, ALU.mult).then_inc(d_drained, 1)

            turned_y = lambda g: drain(attention_fill["turn_y", g], yT[:, 512 * g:512 * (g + 1)])
            steps = dict(scores=row_max, values=attention_out, mha=residual, norm=norm, turn_y=turned_y, logits=router, ranks=places)
            for stage, i in attention_order:
                steps[stage](i)

            dve.wait_ge(s_wexp, 64)
            dve.wait_ge(wexp_ready, 1)

            def rows_turned(i):
                dve.wait_ge(xg_turned, i + 1)
                if not isinstance(i, int) or i > 0:
                    dve.wait_ge(h_done, i * GROUP)
                dve.tensor_copy(xgT[:, :, :], bank(0).rearrange("p (b d) -> p b d", b=GROUP)).then_inc(xgT_ready, 1)

            def mix(i, first=False, more=True):
                e = window_experts(mybir.EngineType.DVE, i)
                for b in range(GROUP):
                    dve.wait_ge(h_turned, i * GROUP + b + 1)
                    for c in range(FC0):
                        ins = dve.tensor_scalar(hT[:, b, c * P:(c + 1) * P], bank(6 + b % 2)[:, c * P:(c + 1) * P],
                                                b1_col[:, e[b], c:c + 1], 0.0, ALU.add, ALU.max)
                    ins.then_inc(hT_ready, 1)
                    if b == 1 and more:
                        rows_turned(i + 1)
                if not first:
                    dve.wait_ge(og_stored, i * 16)
                dve.wait_ge(o_done, i + 1)
                for b in range(GROUP):
                    dve.tensor_tensor(og[:, b, :], bank(1)[:, b * D:(b + 1) * D], b2_row[:, e[b], :], ALU.add).then_inc(og_ready, 1)

            rows_turned(0)
            mix(0, first=True)
            with dve.Fori(1, GROUPS - 1) as i:
                mix(i)
            mix(GROUPS - 1, more=False)

            def experts_added(g):
                r = each_group[g]
                dve.wait_ge(gathered[g], 16 * TG)
                link(dve.tensor_tensor(moe[:, r, :], y[:, r, :], moe[:, r, :], ALU.add))
                variances(2, g, moe)

            def gate_inputs(g):
                r = each_group[g]
                dve.wait_ge(zn_ready, TG * (g + 1))
                link(dve.tensor_tensor(moe[:, r, :], moe[:, r, :], rows(g2_row, TG), ALU.mult))
                dve.tensor_tensor(moe[:, r, :], moe[:, r, :], rows(be2_row, TG), ALU.add).then_inc(z_ready, 1)

            def gated(g):
                r = each_group[g]
                dve.wait_ge(g_ready, g + 1)
                link(dve.tensor_tensor(moe[:, r, :], moe[:, r, :], s0[:, r, :], ALU.mult))
                dve.tensor_tensor(x[:, r, :], x[:, r, :], moe[:, r, :], ALU.add).then_inc(x1_ready, 1)
                dve.wait_ge(x1_ready, g + 1)
                variances(3, g, x)

            for step in range(NG + 2):
                if step < NG:
                    experts_added(step)
                if 0 <= step - 1 < NG:
                    gate_inputs(step - 1)
                if 0 <= step - 2:
                    gated(step - 2)
            dve.wait_ge(xn_ready, 2 * NT)
            for g in range(4):
                drain(D_FILLS["xn1T"] + g, xnT[:, 512 * g:512 * (g + 1)])
            dve.wait_ge(d_drained, D_FILLS["xn1T"] + 4)
            link(dve.tensor_reduce(xsum[:, :], xnT[:, :].rearrange("p (c s) -> p c s", s=CS), AX.X, ALU.add))
            link(dve.tensor_scalar(xsum[:, :], xsum[:, :], 1.0 / CS, None, ALU.mult))
            link(dve.tensor_tensor_scan(xcum[:, :], ones[:, 0:NC], xsum[:, :], 0.0, ALU.mult, ALU.add))
            dve.tensor_tensor(xcum[:, :], xcum[:, :], xsum[:, :], ALU.subtract).then_inc(xsum_ready, 1)
            dve.wait_ge(mask_ready, 2)
            for g in range(8):
                k = D_FILLS["vdup"] + g
                dve.wait_ge(d_filled, k + 1)
                for t in range(2):
                    ins = dve.tensor_tensor(vbd[:, 2 * g + t, :, :, 0:2 * D1].rearrange("p n c d -> p c n d"),
                                            bank(k % 2)[:, 2 * t * D:2 * (t + 1) * D].rearrange("p (c n d) -> p c n d", c=2, d=2 * D1),
                                            vmask[:, :].rearrange("p (n d) -> p n d", d=2 * D1).unsqueeze(1).broadcast_to([P, 2, H1 // 2, 2 * D1]),
                                            ALU.mult)
                ins.then_inc(d_drained, 1)
            dve.wait_ge(d_drained, D_FILLS["vdup"] + 8)
            dve.sem_inc(prep_ready, 1)
            def chunk_scores(i, parity):
                s_ = ps[:, 4 + 2 * parity:6 + 2 * parity, :].rearrange("p b (k c) -> p k b c", k=2)
                dve.wait_ge(s_done, i + 1)
                if not isinstance(i, int) or i >= 2:
                    dve.wait_ge(p_ready, i - 1)
                for k in range(2):
                    ins = dve.tensor_tensor(sm[:, parity, 2 * HG * k:2 * HG * (k + 1), :].rearrange("p (b h) s -> p b h s", b=2),
                                            s_[:, k, :, :].rearrange("p b (h s) -> p b h s", s=CS),
                                            amask[:, :].unsqueeze(1).unsqueeze(1).broadcast_to([P, 2, HG, CS]), ALU.add)
                ins.then_inc(s_read, 1)
                dve.wait_ge(s_read, i + 1)
                dve.tensor_reduce(mx1[:, :], sm[:, parity, :, :], AX.X, ALU.max).then_inc(mx1_ready, 1)
                dve.wait_ge(mx1_ready, i + 1)
                dve.tensor_tensor(sm[:, parity, :, :], sm[:, parity, :, :], mx1[:, :].unsqueeze(2).broadcast_to([P, H1, CS]),
                                  ALU.subtract).then_inc(sm_ready, 1)

            def chunk_out(i, parity):
                dve.wait_ge(pv_done, i + 1)
                dve.wait_ge(pv_free, 2 * i + 4)
                halves = [(slice(CS * c, CS * (c + 1)),
                           bank(parity)[CS * c:CS * (c + 1), 0:H1 * VP].rearrange("p (n c e) -> p n c e", c=2, e=VP)[:, :, c, :])
                          for c in range(2)]
                for r, pv in halves:
                    dve.reciprocal(rs1[r, :].rearrange("p (n c) -> p n c", c=2), pv[:, :, 2 * D1:VP]).then_inc(rs1_ready, 1)
                dve.wait_ge(rs1_ready, 2 * i + 2)
                for r, pv in halves:
                    ot = o1[r, i, :] if isinstance(i, int) else o1[r, bass.ds(i, 1), :].rearrange("p o d -> p (o d)")
                    dve.tensor_tensor(ot.rearrange("p (n c d) -> p n c d", c=2, d=D1), pv[:, :, 0:2 * D1].rearrange("p n (c d) -> p n c d", c=2),
                                      rs1[r, :].rearrange("p (n c) -> p n c", c=2).unsqueeze(3).broadcast_to([CS, H1 // 2, 2, D1]),
                                      ALU.mult).then_inc(pv_free, 1)

            dve.sem_inc(pv_free, 4)

            def cross_scores():
                dve.wait_ge(sums_loaded, 64)
                for g in range(4):
                    k = D_FILLS["cross"] + g
                    dve.wait_ge(d_filled, k + 1)
                    dve.tensor_tensor(ksum[:, 4 * g:4 * g + 4, :], bank(k % 2).rearrange("p (t d) -> p t d", t=4),
                                      ksum[:, 4 * g:4 * g + 4, :], ALU.mult).then_inc(d_drained, 1)
                dve.wait_ge(d_drained, D_FILLS["cross"] + 4)
                dve.tensor_reduce(sig[:, :, :].rearrange("p t h -> p (t h)"), ksum[:, :, :].rearrange("p t (h d) -> p (t h) d", d=D1),
                                  AX.X, ALU.add).then_inc(crs_ready, 1)

            def cross_weights():
                dve.wait_ge(sigexp_ready, 1)
                link(dve.tensor_scalar(sig[:, :, :], sig[:, :, :], 2.0, 2.0, ALU.mult, ALU.add))
                dve.reciprocal(sig[:, :, :], sig[:, :, :]).then_inc(cross_ready, 1)

            def chunk_step(i, parity, first=False, more=True):
                chunk_scores(i, parity)
                if isinstance(i, int) and i == 1:
                    cross_scores()
                if isinstance(i, int) and i == NT - 2:
                    cross_weights()
                if not isinstance(i, int) or i >= 2:
                    chunk_out(i - 2, parity)

            over_tiles(dve, chunk_step, 1)
            for i in (NT - 2, NT - 1):
                chunk_out(i, i % 2)
            dve.wait_ge(pv_free, 2 * NT + 4)
            dve.wait_ge(cross_ready, 2)
            for g in range(4):
                dve.tensor_tensor(o1[:, 4 * g:4 * g + 4, :], o1[:, 4 * g:4 * g + 4, :], vsum[:, 4 * g:4 * g + 4, :],
                                  ALU.add).then_inc(o1_ready, 4)
            for g in range(4):
                drain(D_FILLS["o1T"] + g, q1T[:, 512 * g:512 * (g + 1)])
            dve.wait_ge(o1_ready, NT)
            dve.sem_inc(chunks_done, 1)

            dve.wait_ge(qkv_ready, NT)
            W3 = D + 2 * DM
            qv = qkv[:, :, 0:D].rearrange("p t (h d) -> p t h d", h=HM)
            kv = qkv[:, :, D:D + DM]
            vv = qkv[:, :, D + DM:W3]
            link.mark(dve.tensor_copy(ka[:, :, 0:DM].bitcast(F32R), kv))
            link.mark(dve.tensor_copy(vr[:, :, 0:DM], vv))
            link.mark(dve.tensor_copy(v1[:, :, 0:DM], vv))
            link(dve.tensor_copy(qa[:, :, :, 0:DM].bitcast(F32R), qv))
            dve.sem_inc(parts_ready, 1)
            link.mark(dve.tensor_tensor(ka[:, :, DM:2 * DM].bitcast(F32R), kv, ka[:, :, 0:DM], ALU.subtract))
            link(dve.tensor_tensor(vr[:, :, DM + 1:2 * DM + 1], vv, vr[:, :, 0:DM].bitcast(F32), ALU.subtract))
            dve.sem_inc(kv_low_ready, 1)
            dve.tensor_tensor(qa[:, :, :, 2 * DM:3 * DM].bitcast(F32R), qv, qa[:, :, :, 0:DM], ALU.subtract).then_inc(q_low_ready, 1)
            for g in range(4):
                k = D_FILLS["kaT"] + g
                dve.wait_ge(d_filled, k + 1)
                dve.tensor_copy(kr[0:M_ROWS, 512 * g:512 * (g + 1)], bank(k % 2)[0:M_ROWS, :]).then_inc(d_drained, 1)

            MSTEPS = 3

            def maximum(i, u):
                dve.wait_ge(mx_filled, i * MU + u + 1)
                dve.tensor_reduce(mxp[:, u // HM, u % HM:u % HM + 1], bank(u % 2), AX.X, ALU.max).then_inc(mx_read, 1)

            def cut_maximum(i, parity):
                high, low = (qtile2[:, parity, :, R_ROWS + n] for n in range(2))
                dve.wait_ge(mx_read, i * MU + MU)
                dve.wait_ge(tile_ready, i + 1)
                dve.tensor_reduce(negm[:, :], mxp[:, :, :], AX.X, ALU.max, negate=True).then_inc(m_step, 1)
                dve.wait_ge(m_step, i * MSTEPS + 1)
                dve.tensor_copy(high.bitcast(F32R), negm[:, :]).then_inc(m_step, 1)
                dve.wait_ge(m_step, i * MSTEPS + 2)
                dve.tensor_tensor(low.bitcast(F32R), negm[:, :], high, ALU.subtract).then_inc(m_step, 1)

            def low_parts(i, t):
                dve.wait_ge(p_whole, i * NT + t + 1)
                dve.wait_ge(ph_ready, i * len(CUT) + CUT.index(t) + 1)
                dve.tensor_tensor(pl[:, t % RING, :], pm[:, t % RING, :], ph[:, t % RING, :].bitcast(F32),
                                  ALU.subtract).then_inc(pl_ready, 1)

            OSTEPS = 4

            def shared_out(i):
                dve.wait_ge(o_turned, i + 1)
                o4 = bank(7)[:, 0:HM * VW].rearrange("p (h c) -> p h c", h=HM)
                dve.reciprocal(rsm[:, :], o4[:, :, DM]).then_inc(om_read, 1)
                dve.tensor_copy(ol[:, :, :], o4[:, :, DM + 1:2 * DM + 1]).then_inc(om_read, 1)
                dve.wait_ge(om_read, OSTEPS * i + 2)
                dve.tensor_tensor(ol[:, :, :], ol[:, :, :], o4[:, :, 0:DM], ALU.add).then_inc(om_read, 1)
                dve.wait_ge(om_read, OSTEPS * i + 3)
                dst = at(om, i).rearrange("p (h d) -> p h d", h=HM)
                dve.tensor_tensor(dst, ol[:, :, :], rsm[:, :].unsqueeze(2).broadcast_to([P, HM, DM]), ALU.mult).then_inc(om_read, 1)

            dve.wait_ge(copies_ready, 2)
            for u in range(MU):
                maximum(0, u)
            cut_maximum(0, 0)
            for u in range(NT - MAX_START):
                maximum(1, u)

            def shared_tile(i, parity, first=False, more=True):
                for t in range(NT):
                    n, u = maximum_at(i, t)
                    if still(n, 0):
                        maximum(n, u)
                        if u == MU - 1:
                            cut_maximum(n, 1 - parity)
                    if t == LAG + 1 and not first:
                        shared_out(i - 1)
                    if t in CUT_D:
                        low_parts(i, t)

            over_tiles(dve, shared_tile, 1)
            shared_out(NT - 1)
            dve.wait_ge(om_read, OSTEPS * NT)

            for g in range(4):
                drain(D_FILLS["omT"] + g, xnT[:, 512 * g:512 * (g + 1)])
            nx2 = om
            for g in range(NG + 1):
                if g < NG:
                    r = each_group[g]
                    k = D_FILLS["mo"] + g
                    dve.wait_ge(d_filled, k + 1)
                    dve.tensor_tensor(xn[:, r, :], bank(k % 2).rearrange("p (t d) -> p t d", t=TG), xn[:, r, :],
                                      ALU.add).then_inc(d_drained, 1)
                    dve.wait_ge(d_drained, k + 1)
                    variances(4, g, xn)
                if g >= 1:
                    dve.wait_ge(rstd_ready[4], g)
                    for t in range(TG * (g - 1), TG * g):
                        dve.scalar_tensor_tensor(out=nx2[:, t, :], in0=xn[:, t, :], scalar=rstd[:, t:t + 1], in1=rg2_row,
                                                 op0=ALU.mult, op1=ALU.mult).then_inc(nx_ready, 1)
            for g in range(4):
                drain(D_FILLS["nx2T"] + g, xnT[:, 512 * g:512 * (g + 1)])
            k = D_FILLS["lg1"]
            dve.wait_ge(d_filled, k + 1)
            dve.tensor_tensor(lg1[:, :, :], bank(k % 2)[:, 0:NT * E1].rearrange("p (t e) -> p t e", t=NT),
                              eb_row.unsqueeze(1).broadcast_to([P, NT, E1]), ALU.add).then_inc(d_drained, 1)
            dve.wait_ge(d_drained, k + 1)
            wide = lambda a: a.unsqueeze(2).broadcast_to([P, NT, E1])
            link(dve.tensor_reduce(mrow[:, :], lg1[:, :, :], AX.X, ALU.max))
            dve.tensor_tensor(lg1[:, :, :], lg1[:, :, :], wide(mrow[:, :]), ALU.subtract).then_inc(rx_ready, 1)
            dve.wait_ge(rexp_ready, 1)
            link(dve.tensor_reduce(mrow[:, :], rw[:, :, :], AX.X, ALU.add))
            link(dve.reciprocal(mrow[:, :], mrow[:, :]))
            link(dve.tensor_tensor(rw[:, :, :], rw[:, :, :], wide(mrow[:, :]), ALU.mult))
            for t in range(NT):
                link.mark(dve.max(top1[:, t, :], rw[:, t, :]))
            link.wait()
            for t in range(NT):
                link.mark(dve.max_index(topi1[:, t, :], top1[:, t, :], rw[:, t, :]))
            link.wait()
            dve.tensor_tensor(w12[:, 1, :], top1[:, :, 1], top1[:, :, 0], ALU.subtract).then_inc(rx_ready, 1)
            link.mark(dve.tensor_copy(ix12[:, 0, :], topi1[:, :, 0]))
            link(dve.tensor_copy(ix12[:, 1, :], topi1[:, :, 1]))
            for e in range(E1):
                link.mark(dve.memset(iota1[:, :, e], float(e)))
            link.mark(dve.memset(comb[:, :, E1:ES], 1.0))
            dve.wait_ge(rexp_ready, 2)
            link(dve.tensor_scalar(w12[:, 0, :], w12[:, 1, :], 1.0, None, ALU.add))
            link(dve.reciprocal(w12[:, 0, :], w12[:, 0, :]))
            link(dve.tensor_tensor(w12[:, 1, :], w12[:, 1, :], w12[:, 0, :], ALU.mult))
            link.mark(dve.tensor_tensor(comb[:, :, 0:E1], iota1[:, :, :], wide(ix12[:, 0, :]), ALU.is_equal))
            link(dve.tensor_tensor(ctmp[:, :, :], iota1[:, :, :], wide(ix12[:, 1, :]), ALU.is_equal))
            link.mark(dve.tensor_tensor(comb[:, :, 0:E1], comb[:, :, 0:E1], wide(w12[:, 0, :]), ALU.mult))
            link(dve.tensor_tensor(ctmp[:, :, :], ctmp[:, :, :], wide(w12[:, 1, :]), ALU.mult))
            link(dve.tensor_tensor(comb[:, :, 0:E1], comb[:, :, 0:E1], ctmp[:, :, :], ALU.add))

            def expert_rows(j, e):
                n_ = j * ES + e
                dve.wait_ge(sg_ready, n_ + 1)
                if e >= 2 or not isinstance(j, int):
                    dve.wait_ge(e_filled, n_ - 1 + (e == 0))
                dve.tensor_tensor(h1T[:, e % 2, :], sg[:, e % 2, :], bank(2 * (e % 2) + 1), ALU.mult).then_inc(h1T_ready, 1)

            def add_expert(j, e):
                n_ = j * ES + e
                dve.wait_ge(e_filled, n_ + 1)
                q_ = CH // P
                for t in range(q_):
                    a_ = (xn[:, j * q_ + t, :] if isinstance(j, int) else xn[:, bass.ds(j * q_ + t, 1), :].rearrange("p o d -> p (o d)"))
                    c_ = (comb[:, j * q_ + t, e:e + 1] if isinstance(j, int) else comb[:, bass.ds(j * q_ + t, 1), e])
                    if e > 0:
                        dve.wait_ge(e_read, (n_ - 1) * q_ + t + 1)
                    dve.scalar_tensor_tensor(out=a_, in0=bank(4 + e % 2)[:, t * P:(t + 1) * P], scalar=c_, in1=a_,
                                             op0=ALU.mult, op1=ALU.add).then_inc(e_read, 1)

            def finish(j):
                some = slice(j * (CH // P), (j + 1) * (CH // P)) if isinstance(j, int) else bass.ds(j * (CH // P), CH // P)
                dve.wait_ge(g1_ready, j + 1)
                dve.tensor_tensor(y[:, some, :], y[:, some, :], s0[:, some, :], ALU.mult).then_inc(prod_ready, 1)
                dve.wait_ge(prod_ready, j + 1)
                dve.tensor_tensor(y[:, some, :], y[:, some, :], x[:, some, :], ALU.add).then_inc(fin_ready, 1)

            def mixture(j):
                for e in range(ES + 1):
                    if e < ES:
                        expert_rows(j, e)
                    if e >= 1:
                        add_expert(j, e - 1)
                    if e == FINISH + 1 and not isinstance(j, int):
                        finish(j - 1)
                dve.wait_ge(e_read, (j + 1) * ES * (CH // P))
                dve.sem_inc(acc_ready, 1)

            mixture(0)
            with dve.Fori(1, NCH) as j:
                mixture(j)
            finish(NCH - 1)

        @block.scalar
        def _(act):
            act.wait_ge(s_w0, 48)
            dst = [vfT, kT, qT]
            for n in range(3):
                for g in range(4):
                    k = A_FILLS["proj"] + 4 * n + g
                    act.wait_ge(a_filled, k + 1)
                    act.activation(dst[n][:, 512 * g:512 * (g + 1)], bank(2 + k % 2), ACT.Identity,
                                   bias=cols0[:, n:n + 1], scale=1.0).then_inc(a_drained, 1)

            def exponents(i):
                act.wait_ge(nmax_ready, i + 1)
                if i >= small:
                    act.wait_ge(d_filled, attention_fill["values", i - 2] + 1)
                elif i >= 4:
                    act.wait_ge(d_filled, attention_fill["values", i - 4] + 1)
                act.activation(prob_of(i), scores_of(i), ACT.Exp, bias=nmax[:, i:i + 1], scale=float(D) ** -0.5,
                               accum_out=rsum[:, i:i + 1]).then_inc(prob_ready, 1)

            turn = [A_FILLS["turn"]]

            def turned(i, blocks):
                for b in blocks:
                    k = turn[0]
                    n = min(4, i + 1 - b) * P
                    act.wait_ge(a_filled, k + 1)
                    act.activation(probT[:, k % 2, 0:n], bank(2 + k % 2)[:, 0:n], ACT.Copy).then_inc(a_drained, 1)
                    turn[0] += 1

            waiting = []
            for stage, i in attention_order:
                if stage == "scores":
                    waiting.append(i)
                    if i < 2:
                        exponents(waiting.pop())
                elif stage == "values":
                    blocks = range(0, i + 1, 4)
                    turned(i, blocks[:2])
                    for n in waiting:
                        exponents(n)
                    waiting = []
                    turned(i, blocks[2:])

            with act.Fori(0, GROUPS) as i:
                for b in range(GROUP):
                    act.wait_ge(h_done, i * GROUP + b + 1)
                    act.activation(hb[:, b, :], bank(2 + b), ACT.Copy).then_inc(hb_ready, 1)

            def normalise(n, g, src, dst, ready):
                act.wait_ge(rstd_ready[n], g + 1)
                for t in range(TG * g, TG * (g + 1)):
                    act.activation(dst[:, t, :], src[:, t, :], ACT.Identity, bias=shift[:, t:t + 1],
                                   scale=rstd[:, t:t + 1]).then_inc(ready, 1)

            def gate(g):
                r = each_group[g]
                act.wait_ge(z_ready, g + 1)
                act.activation(moe[:, r, :], moe[:, r, :], ACT.Silu).then_inc(g_ready, 1)

            for step in range(NG + 2):
                if step < NG:
                    normalise(2, step, moe, moe, zn_ready)
                if 0 <= step - 1 < NG:
                    gate(step - 1)
                if 0 <= step - 2:
                    normalise(3, step - 2, x, xn, xn_ready)

            n = 512 // CS
            act.wait_ge(mask_ready, 2)
            for g in range(4):
                act.wait_ge(d_drained, D_FILLS["xn1T"] + g + 1)
                act.activation(xtwice[:, n * g:n * (g + 1), :, :],
                               xnT[:, 512 * g:512 * (g + 1)].rearrange("p (n s) -> p n s", s=CS).unsqueeze(2).broadcast_to([P, n, 2, CS]),
                               ACT.Copy).then_inc(twice_ready, 1)
                k = A_FILLS["k1"] + g
                act.wait_ge(a_filled, k + 1)
                for h in range(HG):
                    ins = act.activation(k4[:, n * g:n * (g + 1), h, :], bank(2 + k % 2).rearrange("p (c s) -> p c s", s=CS),
                                         ACT.Copy, scale=mask4[:, h:h + 1])
                ins.then_inc(a_drained, 1)
            for g in range(4):
                k = A_FILLS["q1"] + g
                act.wait_ge(a_filled, k + 1)
                act.activation(q1T[:, 512 * g:512 * (g + 1)], bank(2 + k % 2), ACT.Copy).then_inc(a_drained, 1)
            act.wait_ge(a_drained, A_FILLS["q1"] + 4)
            act.sem_inc(prep_ready, 1)
            k = A_FILLS["sums"]
            act.wait_ge(a_filled, k + 1)
            act.activation(kvs, bank(2 + k % 2)[0:NC, 0:2 * D], ACT.Copy).then_inc(sums_ready, 1)
            act.wait_ge(sums_ready, 1)
            act.sem_inc(a_drained, 1)

            def chunk_exponents(i, parity):
                act.wait_ge(sm_ready, i + 1)
                if not isinstance(i, int) or i >= 2:
                    act.wait_ge(p_turned, i - 1)
                act.activation(pe1[:, parity, :, :], sm[:, parity, :, :], ACT.Exp, scale=SC1).then_inc(p_ready, 1)

            def chunk_turned(i):
                act.wait_ge(p_turned, i + 1)
                act.activation(p1T[:, :, :], ps[:, 2:4, :].rearrange("p b (n c) -> p (b n) c", c=P), ACT.Copy).then_inc(pT_ready, 1)

            def chunk_step(i, parity, first=False, more=True):
                if isinstance(i, int) and i == NT - 2:
                    act.wait_ge(crs_ready, 1)
                    act.activation(sig[:, :, :], sig[:, :, :], ACT.Exp, scale=-SC1).then_inc(sigexp_ready, 1)
                chunk_exponents(i, parity)
                if not first:
                    chunk_turned(i - 1)

            over_tiles(act, chunk_step, 1)
            chunk_turned(NT - 1)

            act.wait_ge(rstdq_ready, 1)
            for g in range(8):
                k = A_FILLS["qkv"] + g
                act.wait_ge(a_filled, k + 1)
                for t in (2 * g, 2 * g + 1):
                    ins = act.activation(qkv[:, t, :], bank(2 + k % 2)[:, (D + 2 * DM) * (t % 2):(D + 2 * DM) * (t % 2 + 1)],
                                         ACT.Copy, scale=rstdq[:, t:t + 1])
                    ins.then_inc(qkv_ready, 1)
                act.wait_ge(qkv_ready, 2 * g + 2)
                act.sem_inc(a_drained, 1)
            act.wait_ge(parts_ready, 1)
            act.activation(ka[:, :, 2 * DM:3 * DM], ka[:, :, 0:DM], ACT.Copy).then_inc(act_step, 1)
            act.activation(qa[:, :, :, DM:2 * DM], qa[:, :, :, 0:DM], ACT.Copy).then_inc(act_step, 1)
            act.wait_ge(act_step, 2)
            act.sem_inc(copies_ready, 1)
            for g in range(4):
                k = A_FILLS["s1"] + g
                act.wait_ge(a_filled, k + 1)
                act.wait_ge(d_drained, D_FILLS["o1T"] + 4)
                act.activation(s0[:, 4 * g:4 * g + 4, :].rearrange("p t d -> p (t d)"), bank(2 + k % 2), ACT.Copy).then_inc(a_drained, 1)

            def queries(i, parity, first=False):
                act.wait_ge(q_turned, i + 1)
                if not first:
                    act.wait_ge(mx_filled, (i - 1) * MU)
                act.activation(qm[0:R_ROWS, parity, :], bank(7)[0:R_ROWS, :], ACT.Copy).then_inc(qm_ready, 1)

            def maxima(i, parity):
                act.wait_ge(m_turned, i + 1)
                act.activation(qr[0:M_ROWS, parity, :], bank(7)[0:M_ROWS, :], ACT.Copy).then_inc(mr_ready, 1)

            def probabilities(i, t, first):
                act.wait_ge(st_filled, i * NT + t + 1)
                if not (first and t < RING):
                    act.wait_ge(pm_used, i * NT + t - RING + 1)
                act.activation(pm[:, t % RING, :], bank(2 + t % RING), ACT.Exp, scale=SCM).then_inc(p_whole, 1)
                if t in CUT:
                    act.activation(ph[:, t % RING, :], bank(2 + t % RING), ACT.Exp, scale=SCM).then_inc(ph_ready, 1)

            def sums(i):
                act.wait_ge(pm_used, i * NT + NT)
                if not isinstance(i, int) or i > 0:
                    act.wait_ge(o_turned, i)
                act.activation(oT[0:VW, :], bank(6)[0:VW, :], ACT.Copy).then_inc(oT_ready, 1)

            queries(0, 0, first=True)
            queries(1, 1, first=True)
            maxima(0, 0)

            def shared_tile(i, parity, first=False, more=True):
                for t in range(NT):
                    probabilities(i, t, first)
                    if t == QUERY_SLOT and still(i, 2):
                        queries(i + 2, parity)
                    if t == LAG - 1 and not first:
                        sums(i - 1)
                    if t == TURN_SLOT and more:
                        maxima(i + 1, 1 - parity)

            over_tiles(act, shared_tile, 1)
            sums(NT - 1)

            for e in range(ES):
                act.activation(eh[e], e13[:, e, :], ACT.Copy).then_inc(eh_ready, 1)
            for j in range(NCH):
                act.wait_ge(d_drained, D_FILLS["nx2T"] + j + 1)
                act.activation(xh[:, CH * j:CH * (j + 1)], xnT[:, CH * j:CH * (j + 1)], ACT.Copy).then_inc(xh_ready, 1)
            act.wait_ge(rx_ready, 1)
            act.activation(rw[:, :, :], lg1[:, :, :], ACT.Exp).then_inc(rexp_ready, 1)
            act.wait_ge(rx_ready, 2)
            act.activation(w12[:, 1, :], w12[:, 1, :], ACT.Exp).then_inc(rexp_ready, 1)

            def finish(j):
                some = slice(j * (CH // P), (j + 1) * (CH // P)) if isinstance(j, int) else bass.ds(j * (CH // P), CH // P)
                act.wait_ge(acc_ready, j + 1)
                act.activation(y[:, some, :], xn[:, some, :], ACT.Silu).then_inc(g1_ready, 1)

            def gates(j):
                for e in range(ES):
                    n_ = j * ES + e
                    act.wait_ge(h13_filled, n_ + 1)
                    if e >= 2 or not isinstance(j, int):
                        act.wait_ge(h1T_ready, n_ - 1 + (e == 0))
                    act.activation(sg[:, e % 2, :], bank(2 * (e % 2)), ACT.Silu).then_inc(sg_ready, 1)
                    if e == FINISH and not isinstance(j, int):
                        finish(j - 1)

            gates(0)
            with act.Fori(1, NCH) as j:
                gates(j)
            finish(NCH - 1)

        @block.tensor
        def _(pe):
            def d_fill(k):
                if k >= 2:
                    pe.wait_ge(d_drained, k - 1)
                return bank(k % 2)

            def a_fill(k):
                if k >= 2:
                    pe.wait_ge(a_drained, k - 1)
                return bank(2 + k % 2)

            pe.wait_ge(s_const, 1)

            def turn(k0, src, ready):
                for g in range(4):
                    o = d_fill(k0 + g)
                    for t in range(4 * g, 4 * g + 4):
                        if ready is not None:
                            pe.wait_ge(ready, t + 1)
                        ins = pe.transpose(o[:, P * (t % 4):P * (t % 4 + 1)], src[:, t, :], ident[:, :])
                    ins.then_inc(d_filled, 1)

            turn(D_FILLS["xnT"], xn, xn_ready)
            pe.wait_ge(s_w0, 48)
            W = dict(q=w0[:, 0:D], k=w0[:, D:2 * D], v=w0[:, 2 * D:3 * D], vf=w0[:, 3 * D:4 * D], o=w0[:, 4 * D:5 * D])
            for g in range(4):
                pe.wait_ge(d_drained, D_FILLS["xnT"] + g + 1)
                pe.matmul(a_fill(g), W["vf"], xnT[:, 512 * g:512 * (g + 1)], start=True, stop=True).then_inc(a_filled, 1)
            for g in range(4):
                o = d_fill(D_FILLS["v"] + g)
                for t in range(4 * g, 4 * g + 4):
                    ins = pe.matmul(o[:, P * (t % 4):P * (t % 4 + 1)], xnT[:, P * t:P * (t + 1)], W["v"], start=True, stop=True)
                ins.then_inc(d_filled, 1)
            for n, w in ((4, W["k"]), (8, W["q"])):
                for g in range(4):
                    pe.matmul(a_fill(n + g), w, xnT[:, 512 * g:512 * (g + 1)], start=True, stop=True).then_inc(a_filled, 1)

            def mha(g):
                o = d_fill(attention_fill["mha", g])
                for t in range(4 * g, 4 * g + 4):
                    ins = pe.matmul(o[:, P * (t % 4):P * (t % 4 + 1)], vfT[:, P * t:P * (t + 1)], W["o"], start=True, stop=True)
                ins.then_inc(d_filled, 1)

            def turn_y(g):
                o = d_fill(attention_fill["turn_y", g])
                pe.wait_ge(y_ready, NT)
                for t in range(4 * g, 4 * g + 4):
                    ins = pe.transpose(o[:, P * (t % 4):P * (t % 4 + 1)], y[:, t, :], ident[:, :])
                ins.then_inc(d_filled, 1)

            def logits(_):
                o = d_fill(attention_fill["logits", 0])
                pe.wait_ge(d_drained, attention_fill["turn_y", NG - 1] + 1)
                for t in range(NT):
                    ins = pe.matmul(o[:, E0 * t:E0 * (t + 1)], yT[:, P * t:P * (t + 1)], wgT[:, :], start=True, stop=True)
                ins.then_inc(d_filled, 1)

            def ranks(_):
                pe.wait_ge(onehot_ready, 1)
                o = d_fill(attention_fill["ranks", 0])
                oh = onehot[:, :, :].rearrange("p e t -> p (e t)")
                pe.matmul(o[:, 0:NT * E0], before[:, :], oh, start=True, stop=True)
                pe.matmul(o[:, NT * E0:2 * NT * E0], ones[:, :], oh, start=True, stop=True).then_inc(d_filled, 1)

            pe.wait_ge(a_drained, A_FILLS["turn"])
            turns = [A_FILLS["turn"]]

            def scores(i):
                n = (i + 1) * P
                if i >= small:
                    pe.wait_ge(prob_ready, i)
                elif i >= 2:
                    pe.wait_ge(prob_ready, i - 1)
                for c in range(0, n, 512):
                    m = min(512, n - c)
                    ins = pe.matmul(scores_of(i)[:, c:c + m], qT[:, P * i:P * (i + 1)], kT[:, c:c + m], start=True, stop=True)
                ins.then_inc(score_done, 1)

            def turn_probs(i, b):
                k = turns[0]
                o = a_fill(k)
                if b == 0:
                    pe.wait_ge(prob_ready, i + 1)
                for j in range(b, min(b + 4, i + 1)):
                    ins = pe.transpose(o[:, P * (j - b):P * (j - b + 1)], prob_of(i)[:, P * j:P * (j + 1)], ident[:, :])
                ins.then_inc(a_filled, 1)
                turns[0] += 1
                return k

            def weigh(i, b, k, o):
                pe.wait_ge(a_drained, k + 1)
                for j in range(b, min(b + 4, i + 1)):
                    ins = pe.matmul(o[:, 0:D], probT[:, k % 2, P * (j - b):P * (j - b + 1)], v[:, j, :],
                                    start=(j == 0), stop=(j == i))
                if b + 4 > i:
                    ins.then_inc(d_filled, 1)

            def values(i):
                o = d_fill(attention_fill["values", i])
                last = None
                for b in range(0, i + 1, 4):
                    k = turn_probs(i, b)
                    if last is not None:
                        weigh(i, *last, o)
                    last = (b, k)
                weigh(i, *last, o)

            steps = dict(scores=scores, values=values, mha=mha, norm=lambda g: None, turn_y=turn_y, logits=logits, ranks=ranks)
            for stage, i in attention_order:
                steps[stage](i)

            pe.wait_ge(wexp_ready, 1)
            pe.wait_ge(s_wexp, 64)
            pe.wait_ge(d_drained, D_FILLS["attention"] + len(attention_fill))
            pe.wait_ge(prob_ready, NT)

            def turn_window_rows(i):
                pe.wait_ge(xg_loaded, i * 16 + 16)
                if not isinstance(i, int) or i > 0:
                    pe.wait_ge(xgT_ready, i)
                for b in range(GROUP):
                    ins = pe.transpose(bank(0)[:, b * D:(b + 1) * D], xg[:, b, :], ident[:, :])
                ins.then_inc(xg_turned, 1)

            def turn_hidden(i, b):
                pe.wait_ge(hb_ready, i * GROUP + b + 1)
                if b >= 2:
                    pe.wait_ge(hT_ready, i * GROUP + b - 1)
                for c in range(FC0):
                    ins = pe.transpose(bank(6 + b % 2)[:, c * P:(c + 1) * P], hb[:, b, c * P:(c + 1) * P], ident[:, :])
                ins.then_inc(h_turned, 1)

            def second_products(i, b, e):
                pe.wait_ge(hT_ready, i * GROUP + b + 1)
                for c in range(FC0):
                    ins = pe.matmul(bank(1)[:, b * D:(b + 1) * D], hT[:, b, c * P:(c + 1) * P], w2[:, e[b], c, :],
                                    start=(c == 0), stop=(c == FC0 - 1))
                return ins

            def mix(i, first=False, more=True):
                e = window_experts(mybir.EngineType.PE, i)
                pe.wait_ge(xgT_ready, i + 1)
                if not first:
                    pe.wait_ge(og_ready, i * GROUP)
                for b in range(GROUP):
                    pe.matmul(bank(2 + b), xgT[:, b, :], w1[:, e[b], :], start=True, stop=True).then_inc(h_done, 1)
                turn_hidden(i, 0)
                turn_hidden(i, 1)
                if more:
                    turn_window_rows(i + 1)
                for b in range(GROUP):
                    ins = second_products(i, b, e)
                    if b + 2 < GROUP:
                        turn_hidden(i, b + 2)
                ins.then_inc(o_done, 1)

            turn_window_rows(0)
            mix(0, first=True)
            with pe.Fori(1, GROUPS - 1) as i:
                mix(i)
            mix(GROUPS - 1, more=False)

            pe.wait_ge(s_w1, 80)

            def turn1(k0, src, ready, first):
                for g in range(4):
                    o = d_fill(k0 + g)
                    for t in range(4 * g, 4 * g + 4):
                        if ready is not None:
                            pe.wait_ge(ready, first + t + 1)
                        ins = pe.transpose(o[:, P * (t % 4):P * (t % 4 + 1)], src[:, t, :], ident[:, :])
                    ins.then_inc(d_filled, 1)

            turn1(D_FILLS["xn1T"], xn, xn_ready, NT)
            pe.wait_ge(d_drained, D_FILLS["xn1T"] + 4)
            for g in range(4):
                pe.matmul(a_fill(A_FILLS["k1"] + g), wk1, xnT[:, 512 * g:512 * (g + 1)], start=True, stop=True).then_inc(a_filled, 1)
                pe.wait_ge(twice_ready, g + 1)
                for u in (2 * g, 2 * g + 1):
                    o = d_fill(D_FILLS["vdup"] + u)
                    for c in range(4):
                        twice = xtwice[:, 4 * u + c, :, :].rearrange("p r s -> p (r s)")
                        ins = pe.matmul(o[:, c * D:(c + 1) * D], twice, wv1, start=True, stop=True)
                    ins.then_inc(d_filled, 1)
            for g in range(4):
                pe.matmul(a_fill(A_FILLS["q1"] + g), wq1, xnT[:, 512 * g:512 * (g + 1)], start=True, stop=True).then_inc(a_filled, 1)
            pe.wait_ge(xsum_ready, 1)
            pe.matmul(a_fill(A_FILLS["sums"])[0:NC, 0:2 * D], xcum[:, :], wl1[:, D:3 * D], start=True, stop=True).then_inc(a_filled, 1)
            pe.wait_ge(a_drained, A_FILLS["sums"] + 1)

            def cross_products():
                for g in range(4):
                    o = d_fill(D_FILLS["cross"] + g)
                    for t in range(4):
                        ins = pe.matmul(o[:, D * t:D * (t + 1)], xnT[:, (4 * g + t) * P:(4 * g + t + 1) * P], wq1, start=True, stop=True)
                    ins.then_inc(d_filled, 1)

            def chunk_products(i, parity):
                pe.wait_ge(qtile_ready, i * 2 + 2)
                if not isinstance(i, int) or i >= 2:
                    pe.wait_ge(s_read, i - 1)
                n = HG * CS
                for g in range(D // 32):
                    for c in range(2):
                        r = slice(32 * g, 32 * (g + 1))
                        kk = ktile[r, parity, c, :, :].rearrange("p h s -> p (h s)")
                        ins = pe.matmul(ps[CS * c:CS * (c + 1), 4 + 2 * parity + g % 2, n * (g // 2):n * (g // 2 + 1)],
                                        qtile[r, parity, CS * c:CS * (c + 1)], kk, start=True, stop=True)
                    if g == 1:
                        ins.then_inc(half_done, 1)
                        pe.wait_ge(half_done, i + 1)
                ins.then_inc(s_done, 1)

            def chunk_turn(i, parity):
                pe.wait_ge(p_ready, i + 1)
                if not isinstance(i, int) or i >= 1:
                    pe.wait_ge(pT_ready, i)
                flat = pe1[:, parity, :, :].rearrange("p h s -> p (h s)")
                for n in range(H1 // 2):
                    ins = pe.transpose(ps[:, 2 + n // 4, P * (n % 4):P * (n % 4 + 1)], flat[:, P * n:P * (n + 1)], ident[:, :])
                ins.then_inc(p_turned, 1)

            def chunk_weigh(i, parity):
                pe.wait_ge(pT_ready, i + 1)
                pe.wait_ge(pv_free, 2 * i + 2)
                for n in range(H1 // 2):
                    ins = pe.matmul(bank(parity)[:, 2 * VP * n:2 * VP * (n + 1)], p1T[:, n, :],
                                    at(vbd, i)[:, n, :, :].rearrange("p c e -> p (c e)"), start=True, stop=True)
                ins.then_inc(pv_done, 1)

            def chunk_step(i, parity, first=False, more=True):
                chunk_products(i, parity)
                if not isinstance(i, int) or i >= 2:
                    chunk_weigh(i - 2, parity)
                if not first:
                    chunk_turn(i - 1, 1 - parity)
                if isinstance(i, int) and i == 1:
                    cross_products()
                    pe.wait_ge(d_drained, D_FILLS["cross"] + 4)

            over_tiles(pe, chunk_step, 1)
            chunk_weigh(NT - 2, 0)
            chunk_turn(NT - 1, 1)
            chunk_weigh(NT - 1, 1)
            W3 = D + 2 * DM
            pe.wait_ge(wmq_ready, 1)
            for g in range(8):
                o = a_fill(A_FILLS["qkv"] + g)
                for t in range(2 * g, 2 * g + 2):
                    ins = pe.matmul(o[:, W3 * (t % 2):W3 * (t % 2 + 1)], xnT[:, P * t:P * (t + 1)], wmq, start=True, stop=True)
                ins.then_inc(a_filled, 1)
                if g == 1:
                    turn1(D_FILLS["o1T"], o1, o1_ready, 0)
            for g in range(4):
                o = a_fill(A_FILLS["s1"] + g)
                pe.wait_ge(d_drained, D_FILLS["o1T"] + g + 1)
                for t in range(4 * g, 4 * g + 4):
                    ins = pe.matmul(o[:, P * (t % 4):P * (t % 4 + 1)], q1T[:, P * t:P * (t + 1)], wout1, start=True, stop=True)
                ins.then_inc(a_filled, 1)
            pe.wait_ge(copies_ready, 2)
            pe.wait_ge(kv_low_ready, 1)
            for g in range(4):
                o = d_fill(D_FILLS["kaT"] + g)
                for t in range(4):
                    ins = pe.transpose(o[0:M_ROWS, P * t:P * (t + 1)], ka[:, 4 * g + t, :], ident[:, :])
                ins.then_inc(d_filled, 1)
            pe.wait_ge(d_drained, D_FILLS["kaT"] + 4)
            pe.wait_ge(a_drained, A_FILLS["s1"] + 4)

            def turn_queries(i, parity, first=False):
                pe.wait_ge(tile_ready, i + 1)
                if not first:
                    pe.wait_ge(om_read, 4 * (i - 2))
                for h in range(HM):
                    ins = pe.transpose(bank(7)[0:R_ROWS, P * h:P * (h + 1)], qtile2[:, parity, h, 0:R_ROWS], ident[:, :])
                ins.then_inc(q_turned, 1)

            def turn_maxima(i, parity):
                pe.wait_ge(m_step, 3 * i + 3)
                pe.wait_ge(qm_ready, min(i + 2, NT) if isinstance(i, int) else i + 2)
                for h in range(HM):
                    ins = pe.transpose(bank(7)[0:M_ROWS, P * h:P * (h + 1)], qtile2[:, parity, h, :], ident[:, :])
                ins.then_inc(m_turned, 1)

            def maximum(i, u, parity, first=False):
                h, c = u // HM, u % HM * 512
                if u == 0:
                    pe.wait_ge(qm_ready, i + 1)
                if not (first and u < 2):
                    pe.wait_ge(mx_read, i * MU + u - 1)
                pe.matmul(bank(u % 2), qm[0:R_ROWS, parity, h * P:(h + 1) * P], kr[0:R_ROWS, c:c + 512],
                          start=True, stop=True).then_inc(mx_filled, 1)

            def scores_t(i, t, parity, first):
                if t == 0:
                    pe.wait_ge(mr_ready, i + 1)
                if not (first and t < RING):
                    pe.wait_ge(p_whole, i * NT + t - RING + 1)
                    pe.wait_ge(ph_ready, i * len(CUT) + len([c for c in CUT if c <= t - RING])
                               if t >= RING else i * len(CUT) - len([c for c in CUT if c > NT + t - RING]))
                pe.matmul(bank(2 + t % RING), kr[0:M_ROWS, t * P:(t + 1) * P], qr[0:M_ROWS, parity, :],
                          start=True, stop=True).then_inc(st_filled, 1)

            def weigh_t(i, t, first):
                if t == 0 and not first:
                    pe.wait_ge(oT_ready, i)
                if KIND[t] == "w":
                    pe.wait_ge(p_whole, i * NT + t + 1)
                    ins = pe.matmul(bank(6)[0:DM + 1, :], v1[:, t, :], pm[:, t % RING, :], start=False, stop=(t == NT - 1),
                                    skip_group_check=True)
                else:
                    pe.wait_ge(ph_ready, i * len(CUT) + CUT.index(t) + 1)
                    pe.matmul(bank(6)[0:VW, :], vr[:, t, :], ph[:, t % RING, :], start=(t == 0), stop=False, skip_group_check=True)
                    if KIND[t] == "p":
                        pe.wait_ge(pl2_ready, i * len(CUT_P) + CUT_P.index(t) + 1)
                    else:
                        pe.wait_ge(pl_ready, i * len(CUT_D) + CUT_D.index(t) + 1)
                    ins = pe.matmul(bank(6)[0:VW, :], vr[:, t, :], pl[:, t % RING, :], start=False, stop=(t == NT - 1),
                                    skip_group_check=True)
                ins.then_inc(pm_used, 1)

            def turn_rows(i):
                pe.wait_ge(oT_ready, i + 1)
                pe.wait_ge(mr_ready, min(i + 2, NT) if isinstance(i, int) else i + 2)
                for h in range(HM):
                    ins = pe.transpose(bank(7)[:, h * VW:(h + 1) * VW], oT[0:VW, h * P:(h + 1) * P], ident[0:VW, 0:VW])
                ins.then_inc(o_turned, 1)

            turn_queries(0, 0, first=True)
            pe.wait_ge(qm_ready, 1)
            turn_queries(1, 1, first=True)
            for u in range(MU):
                maximum(0, u, 0, first=True)
            turn_maxima(0, 0)
            for u in range(NT - MAX_START):
                maximum(1, u, 1)

            def shared_tile(i, parity, first=False, more=True):
                for t in range(NT):
                    scores_t(i, t, parity, first)
                    n, u = maximum_at(i, t)
                    if still(n, 0):
                        maximum(n, u, parity if t >= MAX_START else 1 - parity)
                    if t == LAG and not first:
                        turn_rows(i - 1)
                    if t == QUERY_SLOT and still(i, 2):
                        turn_queries(i + 2, parity, first)
                    if t == TURN_SLOT and more:
                        turn_maxima(i + 1, 1 - parity)
                    if t >= LAG:
                        weigh_t(i, t - LAG, first)
                    elif not first:
                        weigh_t(i - 1, NT + t - LAG, False)

            over_tiles(pe, shared_tile, 1)
            for t in range(NT - LAG, NT):
                weigh_t(NT - 1, t, False)
            turn_rows(NT - 1)

            pe.wait_ge(om_read, 4 * NT)
            turn1(D_FILLS["omT"], om, None, 0)
            for g in range(4):
                o = d_fill(D_FILLS["mo"] + g)
                pe.wait_ge(d_drained, D_FILLS["omT"] + g + 1)
                for t in range(4 * g, 4 * g + 4):
                    ins = pe.matmul(o[:, P * (t % 4):P * (t % 4 + 1)], xnT[:, P * t:P * (t + 1)], wmo, start=True, stop=True)
                ins.then_inc(d_filled, 1)
            turn1(D_FILLS["nx2T"], om, nx_ready, 0)
            pe.wait_ge(d_drained, D_FILLS["nx2T"] + 4)
            o = d_fill(D_FILLS["lg1"])
            for t in range(NT):
                ins = pe.matmul(o[:, E1 * t:E1 * (t + 1)], xnT[:, P * t:P * (t + 1)], wr, start=True, stop=True)
            ins.then_inc(d_filled, 1)
            pe.wait_ge(d_drained, D_FILLS["lg1"] + 1)

            def hidden(j, e):
                n_ = j * ES + e
                if e >= 2 or not isinstance(j, int):
                    pe.wait_ge(h1T_ready, n_ - 1 + (e == 0))
                if e == 0:
                    pe.wait_ge(xl_ready, j + 1)
                high = xh[:, j * CH:(j + 1) * CH] if isinstance(j, int) else xh[:, bass.ds(j * CH, CH)]
                for w in range(2):
                    c = slice(w * D, (w + 1) * D)
                    o = bank(2 * (e % 2) + w)
                    pe.matmul(o, eh[e][:, c], high, start=True, stop=False)
                    pe.matmul(o, el[e][:, c], high, start=False, stop=False)
                    ins = pe.matmul(o, eh[e][:, c], at(xl, j), start=False, stop=True)
                ins.then_inc(h13_filled, 1)

            def project(j, e):
                n_ = j * ES + e
                pe.wait_ge(h1T_ready, n_ + 1)
                if e >= 2 or not isinstance(j, int):
                    pe.wait_ge(e_read, (n_ - 1 + (e == 0)) * (CH // P))
                for t in range(CH // P):
                    ins = pe.matmul(bank(4 + e % 2)[:, t * P:(t + 1) * P], h1T[:, e % 2, t * P:(t + 1) * P], e2[:, e, :],
                                    start=True, stop=True)
                ins.then_inc(e_filled, 1)

            def mixture(j):
                for e in range(ES + 1):
                    if e < ES:
                        hidden(j, e)
                    if e >= 1:
                        project(j, e - 1)

            pe.wait_ge(el_ready, ES)
            mixture(0)
            with pe.Fori(1, NCH) as j:
                mixture(j)


def layouts(np, i):
    c = np.ascontiguousarray
    a = {k: np.asarray(v) for k, v in i.items()}
    D_ = a["L0_attn_Wq"].shape[0]
    return dict(
        x=c(a["L0_attn_x"].reshape(-1, D_)),
        w0=c(np.concatenate([a["L0_attn_Wq"].T, a["L0_attn_Wk"].T, a["L0_attn_Wv"].T, a["L0_ffn_Wqkv"][2 * D_:].T, a["L0_ffn_Wo"].T], axis=1)),
        cols0=c(np.stack([a["L0_ffn_bqkv"][2 * D_:], a["L0_attn_bk"], a["L0_attn_bq"]], axis=1)),
        rows0=c(np.concatenate([a["L0_attn_bv"], a["L0_ffn_bo"], a["L0_ffn_g1"], a["L0_ffn_be1"], a["L0_ffn_g2"], a["L0_ffn_be2"]])),
        wgT=c(a["L0_ffn_Wg"].T),
        w1=c(a["L0_ffn_W1"].transpose(1, 0, 2)),
        b1=c(a["L0_ffn_b1"].reshape(8, 4, 128).transpose(2, 0, 1)),
        w2=c(a["L0_ffn_W2"].reshape(8, 4, 128, D_).transpose(2, 0, 1, 3)),
        b2=c(a["L0_ffn_b2"].reshape(-1)),
        wl1=c(np.concatenate([a["L1_attn_W_qkv"], a["L1_attn_W_out"], a["L1_ffn_Wq"].T, a["L1_ffn_Wkc"].T, a["L1_ffn_Wvc"].T,
                              a["L1_ffn_Wo"].T, a["L1_ffn_Wr"].T], axis=1)),
        g1c=c(a["L1_ffn_g1"].reshape(-1, 1)),
        rows1=c(np.concatenate([a["L1_ffn_g2"], a["L1_ffn_expert_bias"]])),
        e13=c(np.concatenate([np.concatenate([a["L1_ffn_eW1"], a["L1_ffn_sW1"][None]]),
                              np.concatenate([a["L1_ffn_eW3"], a["L1_ffn_sW3"][None]])], axis=1).transpose(2, 0, 1)),
        e2=c(np.concatenate([a["L1_ffn_eW2"], a["L1_ffn_sW2"][None]]).transpose(2, 0, 1)),
    )


def kernel(**inputs):
    import numpy as np
    import concourse.bacc as bacc
    from concourse.bass_utils import run_bass_kernel_spmd

    arrays = layouts(np, inputs)
    shape = tuple(inputs["L0_attn_x"].shape)
    nc = bacc.Bacc("TRN2", target_bir_lowering=False, num_devices=1)
    aps = {n: nc.dram_tensor(f"in_{n}", a.shape, mybir.dt.from_np(a.dtype), kind="ExternalInput").ap() for n, a in arrays.items()}
    out = nc.dram_tensor("out_0", [shape[0] * shape[1], shape[2]], F32, kind="ExternalOutput").ap()
    bass_recurrent_two_layers(nc, aps, out)
    r = run_bass_kernel_spmd(nc, [{f"in_{n}": a for n, a in arrays.items()}], core_ids=[0])
    return r.results[0]["out_0"].reshape(shape)
```
